# Optimizing a Trainium2 kernel written in Bass

```python
import numpy as np
import jax
import jax.numpy as jnp

def _softmax(x, axis=-1):
    return jax.nn.softmax(x, axis=axis)

def _gelu(x):
    return jax.nn.gelu(x, approximate=True)

def _silu(x):
    return jax.nn.silu(x)

def _sigmoid(x):
    return jax.nn.sigmoid(x)

def _layernorm(x, axis=-1, eps=1e-05):
    m = jnp.mean(x, axis=axis, keepdims=True)
    v = jnp.var(x, axis=axis, keepdims=True)
    return (x - m) / jnp.sqrt(v + eps)

def _scatter_add(tgt, idx, src, axis=0):
    return tgt.at[idx].add(src)

def _segment_sum(src, seg, n):
    return jax.ops.segment_sum(src, seg, n)
kernel_name = 'mk_adaln_attn_ffn_d2_seqx_r4_0f3c48'

def setup_inputs(seed: int=0):
    np.random.seed(seed)
    _w = jnp.asarray

    def _rec_inputs():
        import jax
        import jax.numpy as jnp
        _rk = jax.random.key(seed)
        x = -0.000125 + 0.9999 * jax.random.normal(jax.random.fold_in(_rk, 1), (4, 512, 512), jnp.float32)
        _lenS = 512 - jax.random.randint(jax.random.fold_in(_rk, 7), (4,), 0, max(1, 512 // 4) + 1, jnp.int32)
        _lenS2 = 512 - jax.random.randint(jax.random.fold_in(_rk, 8), (4,), 0, max(1, 512 // 4) + 1, jnp.int32)
        fside_BxSxS_0 = -1.52775e-05 + 0.999936 * jax.random.normal(jax.random.fold_in(_rk, 11), (4, 512, 512), jnp.float32)
        cond_512 = -5.03954e-05 + 1.00559 * jax.random.normal(jax.random.fold_in(_rk, 12), (4, 128), jnp.float32)
        return (x, fside_BxSxS_0, cond_512)
    x, fside_BxSxS_0, cond_512 = _rec_inputs()

    def _L0_cond_setup():
        import jax, jax.numpy as jnp
        from jax import lax
        import numpy as np
        B, T, C, TD = (8, 512, 512, 128)

        def _bi_wkv(r, k, v, w, u, time_emb):
            tf = jax.nn.sigmoid(jnp.sum(time_emb, axis=-1))[:, None, None]
            decay = jnp.exp(-jnp.exp(w.astype(jnp.float32)))[None, :] * (0.5 + 0.5 * tf[:, :, 0])
            kf = k.astype(jnp.float32)
            vf = v.astype(jnp.float32)
            ek = jnp.exp(jnp.minimum(kf, 30.0))
            ekv = ek * vf

            def step(carry, x):
                a, b = carry
                ekv_t, ek_t = x
                a = a * decay + ekv_t
                b = b * decay + ek_t
                return ((a, b), (a, b))
            ekv_t = jnp.swapaxes(ekv, 0, 1)
            ek_t = jnp.swapaxes(ek, 0, 1)
            init = (jnp.zeros_like(decay), jnp.zeros_like(decay))
            _, (nf, df) = lax.scan(step, init, (ekv_t, ek_t))
            _, (nb, db) = lax.scan(step, init, (ekv_t, ek_t), reverse=True)
            nf = jnp.swapaxes(nf, 0, 1)
            df = jnp.swapaxes(df, 0, 1)
            nb = jnp.swapaxes(nb, 0, 1)
            db = jnp.swapaxes(db, 0, 1)
            euk = jnp.exp(jnp.minimum(u.astype(jnp.float32)[None, None, :] + kf, 30.0))
            num = nf + nb - ekv + euk * vf
            den = df + db - ek + euk
            base = jax.nn.sigmoid(r.astype(jnp.float32)) * (num / jnp.maximum(den, 1e-08))
            out = base * (0.8 + 0.2 * tf)
            return out.astype(r.dtype)
        key = jax.random.key(seed)
        ks = jax.random.split(key, 6)
        return {'r': jax.random.normal(ks[0], (B, T, C), dtype=jnp.float32), 'k': jax.random.normal(ks[1], (B, T, C), dtype=jnp.float32), 'v': jax.random.normal(ks[2], (B, T, C), dtype=jnp.float32), 'w': jax.random.normal(ks[3], (C,), dtype=jnp.float32), 'u': jax.random.normal(ks[4], (C,), dtype=jnp.float32), 'time_emb': jax.random.normal(ks[5], (B, TD), dtype=jnp.float32)}
    _L0_cond_all = _L0_cond_setup()
    _L0_cond_in = {k: v for k, v in _L0_cond_all.items() if k in ('w', 'u')}
    del _L0_cond_all

    def _L0_attn_setup():
        import jax, jax.numpy as jnp
        import numpy as np
        B, S, D_IN, D_OUT, H = (4, 512, 512, 512, 16)
        DH = D_OUT // H
        key = jax.random.key(seed)
        ks = jax.random.split(key, 6)
        scale = 1.0 / np.sqrt(D_IN)
        return {'x': jax.random.normal(ks[0], (B, S, D_IN), dtype=jnp.float32), 'Wq': jax.random.normal(ks[1], (D_IN, D_OUT), dtype=jnp.float32) * scale, 'Wk': jax.random.normal(ks[2], (D_IN, D_OUT), dtype=jnp.float32) * scale, 'Wv': jax.random.normal(ks[3], (D_IN, D_OUT), dtype=jnp.float32) * scale, 'Wo': jax.random.normal(ks[4], (D_OUT, D_OUT), dtype=jnp.float32) * scale, 'bo': jax.random.normal(ks[5], (D_OUT,), dtype=jnp.float32) * 0.01}
    _L0_attn_all = _L0_attn_setup()
    _L0_attn_in = {k: v for k, v in _L0_attn_all.items() if k in ('Wq', 'Wk', 'Wv', 'Wo', 'bo')}
    del _L0_attn_all

    def _L0_cond2_setup():
        import jax, jax.numpy as jnp
        from jax import lax
        import numpy as np
        B, T, C, TD = (8, 512, 512, 128)

        def _bi_wkv(r, k, v, w, u, time_emb):
            tf = jax.nn.sigmoid(jnp.sum(time_emb, axis=-1))[:, None, None]
            decay = jnp.exp(-jnp.exp(w.astype(jnp.float32)))[None, :] * (0.5 + 0.5 * tf[:, :, 0])
            kf = k.astype(jnp.float32)
            vf = v.astype(jnp.float32)
            ek = jnp.exp(jnp.minimum(kf, 30.0))
            ekv = ek * vf

            def step(carry, x):
                a, b = carry
                ekv_t, ek_t = x
                a = a * decay + ekv_t
                b = b * decay + ek_t
                return ((a, b), (a, b))
            ekv_t = jnp.swapaxes(ekv, 0, 1)
            ek_t = jnp.swapaxes(ek, 0, 1)
            init = (jnp.zeros_like(decay), jnp.zeros_like(decay))
            _, (nf, df) = lax.scan(step, init, (ekv_t, ek_t))
            _, (nb, db) = lax.scan(step, init, (ekv_t, ek_t), reverse=True)
            nf = jnp.swapaxes(nf, 0, 1)
            df = jnp.swapaxes(df, 0, 1)
            nb = jnp.swapaxes(nb, 0, 1)
            db = jnp.swapaxes(db, 0, 1)
            euk = jnp.exp(jnp.minimum(u.astype(jnp.float32)[None, None, :] + kf, 30.0))
            num = nf + nb - ekv + euk * vf
            den = df + db - ek + euk
            base = jax.nn.sigmoid(r.astype(jnp.float32)) * (num / jnp.maximum(den, 1e-08))
            out = base * (0.8 + 0.2 * tf)
            return out.astype(r.dtype)
        key = jax.random.key(seed)
        ks = jax.random.split(key, 6)
        return {'r': jax.random.normal(ks[0], (B, T, C), dtype=jnp.float32), 'k': jax.random.normal(ks[1], (B, T, C), dtype=jnp.float32), 'v': jax.random.normal(ks[2], (B, T, C), dtype=jnp.float32), 'w': jax.random.normal(ks[3], (C,), dtype=jnp.float32), 'u': jax.random.normal(ks[4], (C,), dtype=jnp.float32), 'time_emb': jax.random.normal(ks[5], (B, TD), dtype=jnp.float32)}
    _L0_cond2_all = _L0_cond2_setup()
    _L0_cond2_in = {k: v for k, v in _L0_cond2_all.items() if k in ('w', 'u')}
    del _L0_cond2_all

    def _L0_ffn_setup():
        import jax, jax.numpy as jnp
        import numpy as np
        from jax import lax
        H = 512
        I = 352
        E = 16
        K = 4
        ISH = 2 * I
        B, S = (4, 512)

        def _router(xf, rg_w, ru_w, extra_scale, extra_bias):
            g = xf @ rg_w.T
            u = xf @ ru_w.T
            scores = jnp.abs(u * jax.nn.silu(g))
            probs = jax.nn.softmax(scores.astype(jnp.float32), axis=-1)
            biased = probs + extra_bias[None, :]
            _, idx = lax.top_k(biased, K)
            orig = 1.0 + probs * extra_scale[None, :]
            w = jnp.take_along_axis(orig, idx, axis=1).astype(xf.dtype)
            return (w, idx)
        key = jax.random.key(seed)
        ks = jax.random.split(key, 12)
        sc = 0.02
        return {'x': jax.random.normal(ks[0], (B, S, H), dtype=jnp.float32), 'rg_w': jax.random.normal(ks[1], (E, H), dtype=jnp.float32) * sc, 'ru_w': jax.random.normal(ks[2], (E, H), dtype=jnp.float32) * sc, 'extra_scale': jnp.zeros((E,), dtype=jnp.float32), 'extra_bias': jnp.zeros((E,), dtype=jnp.float32), 'Wg': jax.random.normal(ks[3], (E, I, H), dtype=jnp.float32) * sc, 'Wu': jax.random.normal(ks[4], (E, I, H), dtype=jnp.float32) * sc, 'Wd': jax.random.normal(ks[5], (E, H, I), dtype=jnp.float32) * sc, 'Sg': jax.random.normal(ks[6], (ISH, H), dtype=jnp.float32) * sc, 'Su': jax.random.normal(ks[7], (ISH, H), dtype=jnp.float32) * sc, 'Sd': jax.random.normal(ks[8], (H, ISH), dtype=jnp.float32) * sc}
    _L0_ffn_all = _L0_ffn_setup()
    _L0_ffn_in = {k: v for k, v in _L0_ffn_all.items() if k in ('rg_w', 'ru_w', 'extra_scale', 'extra_bias', 'Wg', 'Wu', 'Wd', 'Sg', 'Su', 'Sd')}
    del _L0_ffn_all

    def _L1_cond_setup():
        import jax, jax.numpy as jnp
        from jax import lax
        import numpy as np
        B, T, C, TD = (8, 512, 512, 128)

        def _bi_wkv(r, k, v, w, u, time_emb):
            tf = jax.nn.sigmoid(jnp.sum(time_emb, axis=-1))[:, None, None]
            decay = jnp.exp(-jnp.exp(w.astype(jnp.float32)))[None, :] * (0.5 + 0.5 * tf[:, :, 0])
            kf = k.astype(jnp.float32)
            vf = v.astype(jnp.float32)
            ek = jnp.exp(jnp.minimum(kf, 30.0))
            ekv = ek * vf

            def step(carry, x):
                a, b = carry
                ekv_t, ek_t = x
                a = a * decay + ekv_t
                b = b * decay + ek_t
                return ((a, b), (a, b))
            ekv_t = jnp.swapaxes(ekv, 0, 1)
            ek_t = jnp.swapaxes(ek, 0, 1)
            init = (jnp.zeros_like(decay), jnp.zeros_like(decay))
            _, (nf, df) = lax.scan(step, init, (ekv_t, ek_t))
            _, (nb, db) = lax.scan(step, init, (ekv_t, ek_t), reverse=True)
            nf = jnp.swapaxes(nf, 0, 1)
            df = jnp.swapaxes(df, 0, 1)
            nb = jnp.swapaxes(nb, 0, 1)
            db = jnp.swapaxes(db, 0, 1)
            euk = jnp.exp(jnp.minimum(u.astype(jnp.float32)[None, None, :] + kf, 30.0))
            num = nf + nb - ekv + euk * vf
            den = df + db - ek + euk
            base = jax.nn.sigmoid(r.astype(jnp.float32)) * (num / jnp.maximum(den, 1e-08))
            out = base * (0.8 + 0.2 * tf)
            return out.astype(r.dtype)
        key = jax.random.key(seed)
        ks = jax.random.split(key, 6)
        return {'r': jax.random.normal(ks[0], (B, T, C), dtype=jnp.float32), 'k': jax.random.normal(ks[1], (B, T, C), dtype=jnp.float32), 'v': jax.random.normal(ks[2], (B, T, C), dtype=jnp.float32), 'w': jax.random.normal(ks[3], (C,), dtype=jnp.float32), 'u': jax.random.normal(ks[4], (C,), dtype=jnp.float32), 'time_emb': jax.random.normal(ks[5], (B, TD), dtype=jnp.float32)}
    _L1_cond_all = _L1_cond_setup()
    _L1_cond_in = {k: v for k, v in _L1_cond_all.items() if k in ('w', 'u')}
    del _L1_cond_all

    def _L1_attn_setup():
        import jax, jax.numpy as jnp
        from jax import lax
        import numpy as np
        D_MODEL, D_STATE, D_CONV, DT_RANK = (512, 16, 4, 128)
        B, L = (2, 256)
        key = jax.random.key(seed)
        ks = jax.random.split(key, 6)
        return {'x': jax.random.normal(ks[0], (B, L, D_MODEL), dtype=jnp.float32), 'conv_w': jax.random.normal(ks[1], (D_MODEL, 1, D_CONV), dtype=jnp.float32) * 0.2, 'conv_b': jnp.zeros((D_MODEL,), dtype=jnp.float32), 'xproj_w': jax.random.normal(ks[2], (DT_RANK + 2 * D_STATE, D_MODEL), dtype=jnp.float32) * 0.02, 'dtproj_w': jax.random.normal(ks[3], (D_MODEL, DT_RANK), dtype=jnp.float32) * 0.05, 'dtproj_b': jnp.zeros((D_MODEL,), dtype=jnp.float32), 'A_log': jnp.zeros((D_MODEL, D_STATE), dtype=jnp.float32), 'D_skip': jnp.ones((D_MODEL,), dtype=jnp.float32)}
    _L1_attn_all = _L1_attn_setup()
    _L1_attn_in = {k: v for k, v in _L1_attn_all.items() if k in ('conv_w', 'conv_b', 'xproj_w', 'dtproj_w', 'dtproj_b', 'A_log', 'D_skip')}
    del _L1_attn_all

    def _L1_cond2_setup():
        import jax, jax.numpy as jnp
        from jax import lax
        import numpy as np
        B, T, C, TD = (8, 512, 512, 128)

        def _bi_wkv(r, k, v, w, u, time_emb):
            tf = jax.nn.sigmoid(jnp.sum(time_emb, axis=-1))[:, None, None]
            decay = jnp.exp(-jnp.exp(w.astype(jnp.float32)))[None, :] * (0.5 + 0.5 * tf[:, :, 0])
            kf = k.astype(jnp.float32)
            vf = v.astype(jnp.float32)
            ek = jnp.exp(jnp.minimum(kf, 30.0))
            ekv = ek * vf

            def step(carry, x):
                a, b = carry
                ekv_t, ek_t = x
                a = a * decay + ekv_t
                b = b * decay + ek_t
                return ((a, b), (a, b))
            ekv_t = jnp.swapaxes(ekv, 0, 1)
            ek_t = jnp.swapaxes(ek, 0, 1)
            init = (jnp.zeros_like(decay), jnp.zeros_like(decay))
            _, (nf, df) = lax.scan(step, init, (ekv_t, ek_t))
            _, (nb, db) = lax.scan(step, init, (ekv_t, ek_t), reverse=True)
            nf = jnp.swapaxes(nf, 0, 1)
            df = jnp.swapaxes(df, 0, 1)
            nb = jnp.swapaxes(nb, 0, 1)
            db = jnp.swapaxes(db, 0, 1)
            euk = jnp.exp(jnp.minimum(u.astype(jnp.float32)[None, None, :] + kf, 30.0))
            num = nf + nb - ekv + euk * vf
            den = df + db - ek + euk
            base = jax.nn.sigmoid(r.astype(jnp.float32)) * (num / jnp.maximum(den, 1e-08))
            out = base * (0.8 + 0.2 * tf)
            return out.astype(r.dtype)
        key = jax.random.key(seed)
        ks = jax.random.split(key, 6)
        return {'r': jax.random.normal(ks[0], (B, T, C), dtype=jnp.float32), 'k': jax.random.normal(ks[1], (B, T, C), dtype=jnp.float32), 'v': jax.random.normal(ks[2], (B, T, C), dtype=jnp.float32), 'w': jax.random.normal(ks[3], (C,), dtype=jnp.float32), 'u': jax.random.normal(ks[4], (C,), dtype=jnp.float32), 'time_emb': jax.random.normal(ks[5], (B, TD), dtype=jnp.float32)}
    _L1_cond2_all = _L1_cond2_setup()
    _L1_cond2_in = {k: v for k, v in _L1_cond2_all.items() if k in ('w', 'u')}
    del _L1_cond2_all

    def _L1_ffn_setup():
        import jax, jax.numpy as jnp
        import numpy as np
        L, B, D = (512, 1, 512)
        H = 16
        DK, DV = (D // 2, D)
        HDK, HDV = (DK // H, DV // H)
        RATIO = 2
        BASE = 10000.0
        EPS = 1e-05

        def _apply_rotary(x, cos, sin):
            d2 = x.shape[-1] // 2
            x1, x2 = (x[..., :d2], x[..., d2:])
            return jnp.concatenate([x1 * cos - x2 * sin, x2 * cos + x1 * sin], axis=-1)
        key = jax.random.key(seed)
        ks = jax.random.split(key, 8)
        s = 0.02
        return {'x': jax.random.normal(ks[0], (L, B, D), jnp.float32), 'conv_w': jax.random.normal(ks[1], (D, 2), jnp.float32) * 0.5, 'Wq': jax.random.normal(ks[2], (D, DK), jnp.float32) * s, 'Wk': jax.random.normal(ks[3], (D, DK), jnp.float32) * s, 'Wv': jax.random.normal(ks[4], (D, DV), jnp.float32) * s, 'Wg': jax.random.normal(ks[5], (D, DV), jnp.float32) * s, 'router_w': jax.random.normal(ks[6], (H, HDV, RATIO), jnp.float32) * s, 'Wout': jax.random.normal(ks[7], (DV, D), jnp.float32) * s}
    _L1_ffn_all = _L1_ffn_setup()
    _L1_ffn_in = {k: v for k, v in _L1_ffn_all.items() if k in ('conv_w', 'Wq', 'Wk', 'Wv', 'Wg', 'router_w', 'Wout')}
    del _L1_ffn_all
    return {'x': x, 'fside_BxSxS_0': fside_BxSxS_0, 'cond_512': cond_512, 'L0_cond_w': _L0_cond_in['w'], 'L0_cond_u': _L0_cond_in['u'], 'L0_attn_Wq': _L0_attn_in['Wq'], 'L0_attn_Wk': _L0_attn_in['Wk'], 'L0_attn_Wv': _L0_attn_in['Wv'], 'L0_attn_Wo': _L0_attn_in['Wo'], 'L0_attn_bo': _L0_attn_in['bo'], 'L0_cond2_w': _L0_cond2_in['w'], 'L0_cond2_u': _L0_cond2_in['u'], 'L0_ffn_rg_w': _L0_ffn_in['rg_w'], 'L0_ffn_ru_w': _L0_ffn_in['ru_w'], 'L0_ffn_extra_scale': _L0_ffn_in['extra_scale'], 'L0_ffn_extra_bias': _L0_ffn_in['extra_bias'], 'L0_ffn_Wg': _L0_ffn_in['Wg'], 'L0_ffn_Wu': _L0_ffn_in['Wu'], 'L0_ffn_Wd': _L0_ffn_in['Wd'], 'L0_ffn_Sg': _L0_ffn_in['Sg'], 'L0_ffn_Su': _L0_ffn_in['Su'], 'L0_ffn_Sd': _L0_ffn_in['Sd'], 'L1_cond_w': _L1_cond_in['w'], 'L1_cond_u': _L1_cond_in['u'], 'L1_attn_conv_w': _L1_attn_in['conv_w'], 'L1_attn_conv_b': _L1_attn_in['conv_b'], 'L1_attn_xproj_w': _L1_attn_in['xproj_w'], 'L1_attn_dtproj_w': _L1_attn_in['dtproj_w'], 'L1_attn_dtproj_b': _L1_attn_in['dtproj_b'], 'L1_attn_A_log': _L1_attn_in['A_log'], 'L1_attn_D_skip': _L1_attn_in['D_skip'], 'L1_cond2_w': _L1_cond2_in['w'], 'L1_cond2_u': _L1_cond2_in['u'], 'L1_ffn_conv_w': _L1_ffn_in['conv_w'], 'L1_ffn_Wq': _L1_ffn_in['Wq'], 'L1_ffn_Wk': _L1_ffn_in['Wk'], 'L1_ffn_Wv': _L1_ffn_in['Wv'], 'L1_ffn_Wg': _L1_ffn_in['Wg'], 'L1_ffn_router_w': _L1_ffn_in['router_w'], 'L1_ffn_Wout': _L1_ffn_in['Wout']}

def reference(x, fside_BxSxS_0, cond_512, L0_cond_w, L0_cond_u, L0_attn_Wq, L0_attn_Wk, L0_attn_Wv, L0_attn_Wo, L0_attn_bo, L0_cond2_w, L0_cond2_u, L0_ffn_rg_w, L0_ffn_ru_w, L0_ffn_extra_scale, L0_ffn_extra_bias, L0_ffn_Wg, L0_ffn_Wu, L0_ffn_Wd, L0_ffn_Sg, L0_ffn_Su, L0_ffn_Sd, L1_cond_w, L1_cond_u, L1_attn_conv_w, L1_attn_conv_b, L1_attn_xproj_w, L1_attn_dtproj_w, L1_attn_dtproj_b, L1_attn_A_log, L1_attn_D_skip, L1_cond2_w, L1_cond2_u, L1_ffn_conv_w, L1_ffn_Wq, L1_ffn_Wk, L1_ffn_Wv, L1_ffn_Wg, L1_ffn_router_w, L1_ffn_Wout):
    import jax
    import jax.numpy as jnp

    def _L0_cond_ref(r, k, v, w, u, time_emb):
        import jax, jax.numpy as jnp
        from jax import lax
        import numpy as np
        B, T, C, TD = (8, 512, 512, 128)

        def _bi_wkv(r, k, v, w, u, time_emb):
            tf = jax.nn.sigmoid(jnp.sum(time_emb, axis=-1))[:, None, None]
            decay = jnp.exp(-jnp.exp(w.astype(jnp.float32)))[None, :] * (0.5 + 0.5 * tf[:, :, 0])
            kf = k.astype(jnp.float32)
            vf = v.astype(jnp.float32)
            ek = jnp.exp(jnp.minimum(kf, 30.0))
            ekv = ek * vf

            def step(carry, x):
                a, b = carry
                ekv_t, ek_t = x
                a = a * decay + ekv_t
                b = b * decay + ek_t
                return ((a, b), (a, b))
            ekv_t = jnp.swapaxes(ekv, 0, 1)
            ek_t = jnp.swapaxes(ek, 0, 1)
            init = (jnp.zeros_like(decay), jnp.zeros_like(decay))
            _, (nf, df) = lax.scan(step, init, (ekv_t, ek_t))
            _, (nb, db) = lax.scan(step, init, (ekv_t, ek_t), reverse=True)
            nf = jnp.swapaxes(nf, 0, 1)
            df = jnp.swapaxes(df, 0, 1)
            nb = jnp.swapaxes(nb, 0, 1)
            db = jnp.swapaxes(db, 0, 1)
            euk = jnp.exp(jnp.minimum(u.astype(jnp.float32)[None, None, :] + kf, 30.0))
            num = nf + nb - ekv + euk * vf
            den = df + db - ek + euk
            base = jax.nn.sigmoid(r.astype(jnp.float32)) * (num / jnp.maximum(den, 1e-08))
            out = base * (0.8 + 0.2 * tf)
            return out.astype(r.dtype)
        return _bi_wkv(r, k, v, w, u, time_emb)

    def _L0_attn_ref(x, Wq, Wk, Wv, Wo, bo):
        import jax, jax.numpy as jnp
        import numpy as np
        B, S, D_IN, D_OUT, H = (4, 512, 512, 512, 16)
        DH = D_OUT // H
        b, s, _ = x.shape
        q = (x @ Wq).reshape(b, s, H, DH)
        k = (x @ Wk).reshape(b, s, H, DH)
        v = (x @ Wv).reshape(b, s, H, DH)
        scores = jnp.einsum('bqhd,bkhd->bhqk', q, k)
        causal = jnp.tril(jnp.ones((s, s), dtype=bool))
        scores = jnp.where(causal, scores, -jnp.inf)
        attn = jax.nn.softmax(scores / np.sqrt(DH).astype(np.float32), axis=-1)
        ctx = jnp.einsum('bhqk,bkhd->bqhd', attn, v).reshape(b, s, D_OUT)
        return ctx @ Wo + bo

    def _L0_cond2_ref(r, k, v, w, u, time_emb):
        import jax, jax.numpy as jnp
        from jax import lax
        import numpy as np
        B, T, C, TD = (8, 512, 512, 128)

        def _bi_wkv(r, k, v, w, u, time_emb):
            tf = jax.nn.sigmoid(jnp.sum(time_emb, axis=-1))[:, None, None]
            decay = jnp.exp(-jnp.exp(w.astype(jnp.float32)))[None, :] * (0.5 + 0.5 * tf[:, :, 0])
            kf = k.astype(jnp.float32)
            vf = v.astype(jnp.float32)
            ek = jnp.exp(jnp.minimum(kf, 30.0))
            ekv = ek * vf

            def step(carry, x):
                a, b = carry
                ekv_t, ek_t = x
                a = a * decay + ekv_t
                b = b * decay + ek_t
                return ((a, b), (a, b))
            ekv_t = jnp.swapaxes(ekv, 0, 1)
            ek_t = jnp.swapaxes(ek, 0, 1)
            init = (jnp.zeros_like(decay), jnp.zeros_like(decay))
            _, (nf, df) = lax.scan(step, init, (ekv_t, ek_t))
            _, (nb, db) = lax.scan(step, init, (ekv_t, ek_t), reverse=True)
            nf = jnp.swapaxes(nf, 0, 1)
            df = jnp.swapaxes(df, 0, 1)
            nb = jnp.swapaxes(nb, 0, 1)
            db = jnp.swapaxes(db, 0, 1)
            euk = jnp.exp(jnp.minimum(u.astype(jnp.float32)[None, None, :] + kf, 30.0))
            num = nf + nb - ekv + euk * vf
            den = df + db - ek + euk
            base = jax.nn.sigmoid(r.astype(jnp.float32)) * (num / jnp.maximum(den, 1e-08))
            out = base * (0.8 + 0.2 * tf)
            return out.astype(r.dtype)
        return _bi_wkv(r, k, v, w, u, time_emb)

    def _L0_ffn_ref(x, rg_w, ru_w, extra_scale, extra_bias, Wg, Wu, Wd, Sg, Su, Sd):
        import jax, jax.numpy as jnp
        import numpy as np
        from jax import lax
        H = 512
        I = 352
        E = 16
        K = 4
        ISH = 2 * I
        B, S = (4, 512)

        def _router(xf, rg_w, ru_w, extra_scale, extra_bias):
            g = xf @ rg_w.T
            u = xf @ ru_w.T
            scores = jnp.abs(u * jax.nn.silu(g))
            probs = jax.nn.softmax(scores.astype(jnp.float32), axis=-1)
            biased = probs + extra_bias[None, :]
            _, idx = lax.top_k(biased, K)
            orig = 1.0 + probs * extra_scale[None, :]
            w = jnp.take_along_axis(orig, idx, axis=1).astype(xf.dtype)
            return (w, idx)
        shape = x.shape
        xf = x.reshape(-1, H)
        w, idx = _router(xf, rg_w, ru_w, extra_scale, extra_bias)
        coeff = jnp.einsum('tk,tke->te', w, jax.nn.one_hot(idx, E, dtype=w.dtype))

        def step(y, ew):
            wg, wu, wd, c = ew
            h = jax.nn.silu(xf @ wg.T) * (xf @ wu.T)
            return (y + h @ wd.T * c[:, None], None)
        y0 = jnp.zeros_like(xf)
        y, _ = lax.scan(step, y0, (Wg, Wu, Wd, coeff.T))
        z = jax.nn.silu(xf @ Sg.T) * (xf @ Su.T) @ Sd.T
        return (y + z).reshape(shape)

    def _L1_cond_ref(r, k, v, w, u, time_emb):
        import jax, jax.numpy as jnp
        from jax import lax
        import numpy as np
        B, T, C, TD = (8, 512, 512, 128)

        def _bi_wkv(r, k, v, w, u, time_emb):
            tf = jax.nn.sigmoid(jnp.sum(time_emb, axis=-1))[:, None, None]
            decay = jnp.exp(-jnp.exp(w.astype(jnp.float32)))[None, :] * (0.5 + 0.5 * tf[:, :, 0])
            kf = k.astype(jnp.float32)
            vf = v.astype(jnp.float32)
            ek = jnp.exp(jnp.minimum(kf, 30.0))
            ekv = ek * vf

            def step(carry, x):
                a, b = carry
                ekv_t, ek_t = x
                a = a * decay + ekv_t
                b = b * decay + ek_t
                return ((a, b), (a, b))
            ekv_t = jnp.swapaxes(ekv, 0, 1)
            ek_t = jnp.swapaxes(ek, 0, 1)
            init = (jnp.zeros_like(decay), jnp.zeros_like(decay))
            _, (nf, df) = lax.scan(step, init, (ekv_t, ek_t))
            _, (nb, db) = lax.scan(step, init, (ekv_t, ek_t), reverse=True)
            nf = jnp.swapaxes(nf, 0, 1)
            df = jnp.swapaxes(df, 0, 1)
            nb = jnp.swapaxes(nb, 0, 1)
            db = jnp.swapaxes(db, 0, 1)
            euk = jnp.exp(jnp.minimum(u.astype(jnp.float32)[None, None, :] + kf, 30.0))
            num = nf + nb - ekv + euk * vf
            den = df + db - ek + euk
            base = jax.nn.sigmoid(r.astype(jnp.float32)) * (num / jnp.maximum(den, 1e-08))
            out = base * (0.8 + 0.2 * tf)
            return out.astype(r.dtype)
        return _bi_wkv(r, k, v, w, u, time_emb)

    def _L1_attn_ref(x, conv_w, conv_b, xproj_w, dtproj_w, dtproj_b, A_log, D_skip):
        import jax, jax.numpy as jnp
        from jax import lax
        import numpy as np
        D_MODEL, D_STATE, D_CONV, DT_RANK = (512, 16, 4, 128)
        B, L = (2, 256)
        b, l, d = x.shape
        k = conv_w.shape[-1]
        n = A_log.shape[-1]
        r = dtproj_w.shape[-1]
        xt = jnp.transpose(x, (0, 2, 1))
        xp = jnp.pad(xt, ((0, 0), (0, 0), (k - 1, 0)))
        u = lax.conv_general_dilated(xp, conv_w, window_strides=(1,), padding='VALID', feature_group_count=d) + conv_b[None, :, None]
        u_bld = jnp.transpose(u, (0, 2, 1))
        x_dbl = jnp.einsum('bld,ed->ble', u_bld, xproj_w)
        dt = x_dbl[..., :r]
        Bm = x_dbl[..., r:r + n]
        Cm = x_dbl[..., r + n:]
        delta = jax.nn.softplus(jnp.einsum('blr,dr->bld', dt, dtproj_w) + dtproj_b)
        A = -jnp.exp(A_log)
        deltaA = jnp.exp(delta[..., None] * A)
        deltaBu = delta[..., None] * Bm[:, :, None, :] * u_bld[..., None]

        def step(h, inp):
            dA, dBu, c = inp
            h = dA * h + dBu
            y = jnp.einsum('bdn,bn->bd', h, c)
            return (h, y)
        h0 = jnp.zeros((b, d, n), dtype=x.dtype)
        _, ys = lax.scan(step, h0, (jnp.transpose(deltaA, (1, 0, 2, 3)), jnp.transpose(deltaBu, (1, 0, 2, 3)), jnp.transpose(Cm, (1, 0, 2))))
        y = jnp.transpose(ys, (1, 0, 2)) + u_bld * D_skip
        return y

    def _L1_cond2_ref(r, k, v, w, u, time_emb):
        import jax, jax.numpy as jnp
        from jax import lax
        import numpy as np
        B, T, C, TD = (8, 512, 512, 128)

        def _bi_wkv(r, k, v, w, u, time_emb):
            tf = jax.nn.sigmoid(jnp.sum(time_emb, axis=-1))[:, None, None]
            decay = jnp.exp(-jnp.exp(w.astype(jnp.float32)))[None, :] * (0.5 + 0.5 * tf[:, :, 0])
            kf = k.astype(jnp.float32)
            vf = v.astype(jnp.float32)
            ek = jnp.exp(jnp.minimum(kf, 30.0))
            ekv = ek * vf

            def step(carry, x):
                a, b = carry
                ekv_t, ek_t = x
                a = a * decay + ekv_t
                b = b * decay + ek_t
                return ((a, b), (a, b))
            ekv_t = jnp.swapaxes(ekv, 0, 1)
            ek_t = jnp.swapaxes(ek, 0, 1)
            init = (jnp.zeros_like(decay), jnp.zeros_like(decay))
            _, (nf, df) = lax.scan(step, init, (ekv_t, ek_t))
            _, (nb, db) = lax.scan(step, init, (ekv_t, ek_t), reverse=True)
            nf = jnp.swapaxes(nf, 0, 1)
            df = jnp.swapaxes(df, 0, 1)
            nb = jnp.swapaxes(nb, 0, 1)
            db = jnp.swapaxes(db, 0, 1)
            euk = jnp.exp(jnp.minimum(u.astype(jnp.float32)[None, None, :] + kf, 30.0))
            num = nf + nb - ekv + euk * vf
            den = df + db - ek + euk
            base = jax.nn.sigmoid(r.astype(jnp.float32)) * (num / jnp.maximum(den, 1e-08))
            out = base * (0.8 + 0.2 * tf)
            return out.astype(r.dtype)
        return _bi_wkv(r, k, v, w, u, time_emb)

    def _L1_ffn_ref(x, conv_w, Wq, Wk, Wv, Wg, router_w, Wout):
        import jax, jax.numpy as jnp
        import numpy as np
        L, B, D = (512, 1, 512)
        H = 16
        DK, DV = (D // 2, D)
        HDK, HDV = (DK // H, DV // H)
        RATIO = 2
        BASE = 10000.0
        EPS = 1e-05

        def _apply_rotary(x, cos, sin):
            d2 = x.shape[-1] // 2
            x1, x2 = (x[..., :d2], x[..., d2:])
            return jnp.concatenate([x1 * cos - x2 * sin, x2 * cos + x1 * sin], axis=-1)
        x = jnp.transpose(x, (1, 0, 2))
        b, l, d = x.shape
        x_prev = jnp.pad(x, ((0, 0), (1, 0), (0, 0)))[:, :l]
        x = jax.nn.silu(x_prev * conv_w[:, 0] + x * conv_w[:, 1])
        q = jax.nn.silu(x @ Wq)
        k = x @ Wk
        v = x @ Wv
        g = x @ Wg
        q = q.reshape(b, l, H, HDK).transpose(0, 2, 1, 3)
        k = k.reshape(b, l, H, HDK).transpose(0, 2, 1, 3)
        v = v.reshape(b, l, H, HDV).transpose(0, 2, 1, 3)
        inv_freq = 1.0 / BASE ** (jnp.arange(0, HDK, 2, dtype=jnp.float32) / HDK)
        freqs = jnp.arange(l, dtype=jnp.float32)[:, None] * inv_freq[None, :]
        cos, sin = (jnp.cos(freqs), jnp.sin(freqs))
        q = _apply_rotary(q, cos, sin)
        k = _apply_rotary(k, cos, sin)
        logits = jnp.einsum('bhld,hdr->bhlr', v, router_w)
        scores = jax.nn.softmax(logits, axis=-1)
        onehot = jax.nn.one_hot(jnp.argmax(scores, axis=-1), RATIO, dtype=scores.dtype)
        masked_scores = scores * onehot
        masked_ind = onehot
        sum_ind = jnp.cumsum(masked_ind, axis=2)
        norm = jnp.where(sum_ind > 0, 1.0 / jnp.maximum(sum_ind, 1.0), 0.0)[..., None]
        q_exp = q[:, :, :, None, :] * masked_scores[..., None] * norm
        k_exp = k[:, :, :, None, :] * masked_ind[..., None]
        q_exp = q_exp.reshape(b, H, l, RATIO * HDK)
        k_exp = k_exp.reshape(b, H, l, RATIO * HDK)
        qk = jnp.einsum('bhld,bhmd->bhlm', q_exp, k_exp) * HDK ** (-0.5)
        mask = jnp.tril(jnp.ones((l, l), dtype=qk.dtype))
        qk = qk * mask
        o = jnp.einsum('bhlm,bhmd->bhld', qk, v)
        o = o.transpose(0, 2, 1, 3)
        mu = jnp.mean(o, axis=-1, keepdims=True)
        var = jnp.var(o, axis=-1, keepdims=True)
        o = (o - mu) / jnp.sqrt(var + EPS)
        out = jax.nn.silu(g) * o.reshape(b, l, d)
        out = out @ Wout
        return jnp.transpose(out, (1, 0, 2))
    x = x + _L0_attn_ref(_L0_cond_ref(x, fside_BxSxS_0, fside_BxSxS_0, L0_cond_w, L0_cond_u, cond_512), L0_attn_Wq, L0_attn_Wk, L0_attn_Wv, L0_attn_Wo, L0_attn_bo)
    x = x + _L0_ffn_ref(_L0_cond2_ref(x, fside_BxSxS_0, fside_BxSxS_0, L0_cond2_w, L0_cond2_u, cond_512), L0_ffn_rg_w, L0_ffn_ru_w, L0_ffn_extra_scale, L0_ffn_extra_bias, L0_ffn_Wg, L0_ffn_Wu, L0_ffn_Wd, L0_ffn_Sg, L0_ffn_Su, L0_ffn_Sd)
    x = x + _L1_attn_ref(_L1_cond_ref(x, fside_BxSxS_0, fside_BxSxS_0, L1_cond_w, L1_cond_u, cond_512), L1_attn_conv_w, L1_attn_conv_b, L1_attn_xproj_w, L1_attn_dtproj_w, L1_attn_dtproj_b, L1_attn_A_log, L1_attn_D_skip)
    x = x + _L1_ffn_ref(_L1_cond2_ref(x, fside_BxSxS_0, fside_BxSxS_0, L1_cond2_w, L1_cond2_u, cond_512), L1_ffn_conv_w, L1_ffn_Wq, L1_ffn_Wk, L1_ffn_Wv, L1_ffn_Wg, L1_ffn_router_w, L1_ffn_Wout)
    return x

_drawn_inputs = setup_inputs


def setup_inputs(seed=0):
    import zlib

    import numpy as np

    out = dict(_drawn_inputs(seed))
    spreads = {'L0_ffn_extra_scale': (0.0, 0.8),
     'L0_ffn_extra_bias': (0.0, 0.415),
     'L1_attn_conv_b': (0.0, 0.1),
     'L1_attn_dtproj_b': (0.0, 0.8),
     'L1_attn_A_log': (0.0, 0.8),
     'L1_attn_D_skip': (1.0, 0.2)}
    factors = {'L0_attn_Wq': 8.0,
     'L0_attn_Wk': 8.0,
     'L0_attn_bo': 5.859,
     'L0_cond2_w': 5.293,
     'L0_cond2_u': 8.0,
     'L0_ffn_rg_w': 8.0,
     'L0_ffn_ru_w': 8.0,
     'L0_ffn_Wg': 3.811,
     'L0_ffn_Wu': 3.765,
     'L0_ffn_Wd': 3.785,
     'L0_ffn_Sg': 5.281,
     'L0_ffn_Su': 5.238,
     'L0_ffn_Sd': 5.257,
     'L1_attn_xproj_w': 6.679,
     'L1_attn_dtproj_w': 8.0,
     'L1_cond2_w': 8.0,
     'L1_cond2_u': 8.0,
     'L1_ffn_conv_w': 8.0,
     'L1_ffn_Wq': 8.0,
     'L1_ffn_Wk': 8.0,
     'L1_ffn_Wv': 8.0,
     'L1_ffn_Wg': 8.0,
     'L1_ffn_router_w': 8.0,
     'L1_ffn_Wout': 8.0}
    for name, (base, spread) in spreads.items():
        noise = np.random.default_rng([zlib.crc32(name.encode()), seed]).standard_normal(out[name].shape)
        drawn = base * np.exp(spread * noise) if base else spread * noise
        out[name] = jnp.asarray(drawn.astype(out[name].dtype))
    for name, factor in factors.items():
        out[name] = (out[name] * factor).astype(out[name].dtype)
    return out
```

```python
from contextlib import ExitStack

import concourse.bass as bass
from concourse import mybir

F32 = mybir.dt.float32
I32 = mybir.dt.int32
U32 = mybir.dt.uint32
BF16 = mybir.dt.bfloat16
ALU = mybir.AluOpType
ACT = mybir.ActivationFunctionType
AX = mybir.AxisListType

P = 128
NB = 4
T = 512
C = 512
NC = C // P
NT = T // P
NK = NB * NC
NLAYER = 4
HEADS = 16
DH = C // HEADS
HG = P // DH
MASKED = -1.0e30
NS = 16
DTR = 128
EPS = 1e-5
OWN_F = 8 + 2 + 1 + 6 + 4 * 5 + 2 + 4 * 3 + 2 + 2
E = 16
TOPK = 4
I = 352
ISH = 704
NTOK = NB * T
TT = NTOK // P
NBLK = NTOK * TOPK // P + E
ZB = 5


class Steps:

    def __init__(self, eng, sem):
        self.eng, self.sem, self.base, self.n = eng, sem, 0, 0

    def __call__(self, ins):
        ins.then_inc(self.sem, 1)
        self.n += 1
        return ins

    def sync(self):
        self.eng.wait_ge(self.sem, self.base + self.n)

    def enter(self, i, per_iteration):
        self.outer = (self.base, self.n, per_iteration)
        self.base, self.n = self.base + self.n + i * per_iteration, 0

    def leave(self, iterations):
        base, n, per = self.outer
        assert self.n == per, (self.n, per)
        self.base, self.n = base, n + per * iterations


def build(nc, io):
    ctx = ExitStack()
    with ctx:
        def sem(name):
            return ctx.enter_context(nc.semaphore(name))

        def sb(name, shape, dt=F32, stack=None):
            return (stack or ctx).enter_context(nc.sbuf_tensor(name, shape, dt))

        def pair(name):
            return [sem(f"{name}0"), sem(f"{name}1")]

        def recycle(stack, held):
            with nc.Block() as block:
                @block.sync
                def _(sp):
                    for s in held:
                        sp.sem_clear(s)
            stack.close()

        X = sb("X", [P, NK * T])
        ident = sb("ident", [P, P])
        par = sb("par", [P, NLAYER * NK, 3])
        psum = [ctx.enter_context(nc.psum_tensor(f"bank{i}", [P, T], F32)) for i in range(8)]
        Xe = nc.dram_tensor("Xe_scratch", [NBLK * P, C], F32, kind="Internal").ap()
        Ye = nc.dram_tensor("Ye_scratch", [NBLK * P, C], F32, kind="Internal").ap()
        G_dram = nc.dram_tensor("G_scratch", [NLAYER * NK, P, T], F32, kind="Internal").ap()

        wk_load = pair("wk_load")
        wk_min = pair("wk_min")
        wk_exp = pair("wk_exp")
        wk_euv = pair("wk_euv")
        wk_out = pair("wk_out")
        wk_store = pair("wk_store")
        wk_own = sem("wk_own")
        W = [{}, {}]

        def wkv_buffers(stack, phase):
            for s in range(2):
                for n in ["f", "fm", "um", "ek", "eu", "ekv", "nf", "nb", "df", "db", "p", "g"]:
                    W[s][n] = sb(f"wk{phase}_{n}{s}", [P, T], stack=stack)
                W[s]["par"] = sb(f"wk{phase}_par{s}", [P, 3], stack=stack)

        def wkv_load(sp, m, s, k):
            sp.wait_ge(wk_out[s], m)
            sp.dma_start(W[s]["f"][:], io["f"][bass.ds(k, 1)].rearrange("a p t -> p (a t)")
                         ).then_inc(wk_load[s], 16)

        def wkv_store(sp, m, s, lk):
            sp.wait_ge(wk_out[s], m + 1)
            sp.dma_start(G_dram[bass.ds(lk, 1)].rearrange("a p t -> p (a t)"), W[s]["g"][:]
                         ).then_inc(wk_store[s], 16)

        def wkv_scalar(act, m, s):
            w = W[s]
            act.wait_ge(wk_min[s], 2 * m + 2)
            act.activation(w["ek"][:], w["fm"][:], ACT.Exp).then_inc(wk_exp[s], 1)
            act.activation(w["eu"][:], w["um"][:], ACT.Exp).then_inc(wk_exp[s], 1)

        def wkv_gpsimd(pool, m, s):
            w = W[s]
            pool.wait_ge(wk_exp[s], 2 * m + 2)
            pool.tensor_tensor(w["p"][:], w["eu"][:], w["f"][:], ALU.mult).then_inc(wk_euv[s], 1)

        WKV_STEPS = 14

        def wkv_vector(dve, m, s, lk, own, euv_here=False):
            w = W[s]
            own.sync()
            own(dve.tensor_copy(w["par"][:], par[:].rearrange("p a b -> p (a b)")[:, bass.ds(lk * 3, 3)]))
            decay, u, scale = (w["par"][:, j:j + 1] for j in range(3))
            yield
            dve.wait_ge(wk_load[s], 16 * m + 16)
            dve.tensor_scalar(w["fm"][:], w["f"][:], 30.0, None, ALU.min).then_inc(wk_min[s], 1)
            own.sync()
            dve.tensor_scalar(w["um"][:], w["f"][:], u, 30.0, ALU.add, ALU.min).then_inc(wk_min[s], 1)
            yield
            dve.wait_ge(wk_exp[s], 2 * m + 1)
            own(dve.tensor_tensor(w["ekv"][:], w["ek"][:], w["f"][:], ALU.mult))
            d = decay.to_broadcast([P, T])
            yield
            own(dve.tensor_tensor_scan(w["df"][:], d, w["ek"][:], 0.0, ALU.mult, ALU.add))
            yield
            own(dve.tensor_tensor_scan(w["db"][:, ::-1], d, w["ek"][:, ::-1], 0.0, ALU.mult, ALU.add))
            yield
            own.sync()
            own(dve.tensor_tensor_scan(w["nf"][:], d, w["ekv"][:], 0.0, ALU.mult, ALU.add))
            yield
            own(dve.tensor_tensor_scan(w["nb"][:, ::-1], d, w["ekv"][:, ::-1], 0.0, ALU.mult, ALU.add))
            yield
            own.sync()
            own(dve.scalar_tensor_tensor(w["df"][:, 0:T - 1], w["db"][:, 1:T], decay, w["df"][:, 0:T - 1],
                                         ALU.mult, ALU.add))
            yield
            own(dve.scalar_tensor_tensor(w["nf"][:, 0:T - 1], w["nb"][:, 1:T], decay, w["nf"][:, 0:T - 1],
                                         ALU.mult, ALU.add))
            dve.wait_ge(wk_exp[s], 2 * m + 2)
            yield
            if euv_here:
                own(dve.tensor_tensor(w["p"][:], w["eu"][:], w["f"][:], ALU.mult))
            own.sync()
            own(dve.tensor_tensor(w["df"][:], w["df"][:], w["eu"][:], ALU.add))
            yield
            own.sync()
            own(dve.tensor_scalar(w["df"][:], w["df"][:], 1e-8, None, ALU.max))
            yield
            if not euv_here:
                dve.wait_ge(wk_euv[s], m + 1)
            own(dve.tensor_tensor(w["nf"][:], w["nf"][:], w["p"][:], ALU.add))
            yield
            own.sync()
            own(dve.reciprocal(w["db"][:], w["df"][:]))
            yield
            own.sync()
            dve.wait_ge(wk_store[s], 16 * m)
            dve.scalar_tensor_tensor(w["g"][:], w["nf"][:], scale, w["db"][:], ALU.mult, ALU.mult
                                     ).then_inc(wk_out[s], 1)
            yield

        WKV_OWN = 12

        c_in = sem("c_in")
        c_x = sem("c_x")
        c_pool = sem("c_pool")
        c_act = sem("c_act")
        c_dve = sem("c_dve")
        c_pe = sem("c_pe")
        with ExitStack() as st:
            wkv_buffers(st, "c")
            wst = sb("wst", [P, NLAYER * NC], stack=st)
            ust = sb("ust", [P, NLAYER * NC], stack=st)
            condT = sb("condT", [P, NB], stack=st)
            ones = sb("ones", [P, P], stack=st)
            ew = sb("ew", [P, NLAYER * NC], stack=st)
            dcy = sb("dcy", [P, NLAYER * NC], stack=st)
            tf = sb("tf", [P, NB], stack=st)
            tfh = sb("tfh", [P, NB], stack=st)
            tfs = sb("tfs", [P, NB], stack=st)
            par5 = par[:].rearrange("p (l b c) f -> p l b c f", l=NLAYER, b=NB)
            with nc.Block() as block:
                @block.sync
                def _(sp):
                    sp.dma_start(wst[:], io["w"]).then_inc(c_in, 16)
                    sp.dma_start(ust[:], io["u"]).then_inc(c_in, 16)
                    sp.dma_start(condT[:], io["condT"]).then_inc(c_in, 16)
                    for s in range(2):
                        wkv_load(sp, 0, s, s)
                    sp.dma_start(X[:].rearrange("p (k t) -> p k t", k=NK), io["x"].rearrange("k p t -> p k t")
                                 ).then_inc(c_x, 16)
                    with sp.Fori(0, NK // 2 - 1) as i:
                        for s in range(2):
                            wkv_store(sp, i, s, i * 2 + s)
                            wkv_load(sp, i + 1, s, i * 2 + s + 2)
                    for s in range(2):
                        wkv_store(sp, NK // 2 - 1, s, NK - 2 + s)
                    sp.wait_ge(c_x, 16)
                    for s in range(2):
                        sp.wait_ge(wk_store[s], 16 * NK // 2)

                @block.gpsimd
                def _(pool):
                    pool.memset(ones[:], 1.0).then_inc(c_pool, 1)
                    pool.memset(ident[:], 0.0).then_inc(c_pool, 1)
                    pool.wait_ge(c_pool, 2)
                    pool.affine_select(out=ident[:], in_=ident[:], compare_op=ALU.not_equal, fill=1.0, base=0,
                                       pattern=[[-1, P]], channel_multiplier=1).then_inc(c_pool, 1)
                    with pool.Fori(0, NK // 2) as i:
                        for s in range(2):
                            wkv_gpsimd(pool, i, s)

                @block.tensor
                def _(pe):
                    pe.wait_ge(c_pool, 1)
                    pe.wait_ge(c_in, 48)
                    pe.matmul(psum[0][:, 0:NB], ones[:], condT[:], start=True, stop=True).then_inc(c_pe, 1)

                @block.scalar
                def _(act):
                    act.wait_ge(c_pe, 1)
                    act.activation(tf[:], psum[0][:, 0:NB], ACT.Sigmoid).then_inc(c_act, 1)
                    act.activation(ew[:], wst[:], ACT.Exp).then_inc(c_act, 1)
                    act.wait_ge(c_act, 2)
                    act.activation(dcy[:], ew[:], ACT.Exp, scale=-1.0).then_inc(c_act, 1)
                    with act.Fori(0, NK // 2) as i:
                        for s in range(2):
                            wkv_scalar(act, i, s)

                @block.vector
                def _(dve):
                    own = Steps(dve, c_dve)
                    dve.wait_ge(c_act, 3)
                    dve.wait_ge(c_in, 48)
                    own(dve.tensor_scalar(tfh[:], tf[:], 0.5, 0.5, ALU.mult, ALU.add))
                    own(dve.tensor_scalar(tfs[:], tf[:], 0.2, 0.8, ALU.mult, ALU.add))
                    own.sync()
                    view = [x[:].rearrange("p (l c) -> p l c", l=NLAYER) for x in (dcy, ust)]
                    for b in range(NB):
                        own(dve.tensor_scalar(par5[:, :, b, :, 0], view[0], tfh[:, b:b + 1], None, ALU.mult))
                        own(dve.tensor_copy(par5[:, :, b, :, 1], view[1]))
                        own(dve.tensor_scalar(par5[:, :, b, :, 2], view[0], 0.0, tfs[:, b:b + 1], ALU.mult, ALU.add))
                    own.sync()
                    wk = Steps(dve, wk_own)
                    with dve.Fori(0, NK // 2) as i:
                        wk.enter(i, 2 * WKV_OWN)
                        for s in range(2):
                            for _ in wkv_vector(dve, i, s, i * 2 + s, wk):
                                pass
                        wk.leave(NK // 2)

        stage, held = ExitStack(), []

        def stage_sem(name):
            held.append(stage.enter_context(nc.semaphore(name)))
            return held[-1]
        attention(nc, io, {**locals(), "sem": stage_sem, "pair": lambda n: [stage_sem(n + "0"), stage_sem(n + "1")]})
        recycle(stage, held)
        experts(nc, io, locals())
        state_space(nc, io, locals())
        linear_attention(nc, io, locals())


def attention(nc, io, g):
    sb, sem, pair, X, ident, psum, G_dram = (g[k] for k in ("sb", "sem", "pair", "X", "ident", "psum", "G_dram"))
    wk_own = g["wk_own"]
    ps_s, ps_t, ps_p, ps_c = psum[0:2], psum[2:4], psum[4:6], psum[6:8]
    STEPS = HEADS * NT
    HALF = STEPS // 2
    with ExitStack() as st:
        g["wkv_buffers"](st, "a")
        zeros = sb("zeros", [P, C], stack=st)
        a_z = sem("a_z")
        wq, wk, wv, wo = (sb(f"at_w{n}", [P, NC, C], stack=st) for n in "qkvo")
        bo = sb("bo", [P, NC], stack=st)
        mask = sb("mask", [P, P], stack=st)
        gt = sb("gt", [P, NC * T], stack=st)
        r = sb("at_r", [P, NC, T], stack=st)
        qT = [sb(f"qT{s}", [P, T], stack=st) for s in range(2)]
        kT = [sb(f"kT{s}", [P, T], stack=st) for s in range(2)]
        v = sb("v", [P, NT, C], stack=st)
        prob = [sb(f"prob{s}", [P, T], stack=st) for s in range(2)]
        probT = [sb(f"probT{s}", [P, NT, T], stack=st) for s in range(2)]
        cT = sb("cT", [P, NC, T], stack=st)
        nmax = [sb(f"nmax{s}", [P, 1], stack=st) for s in range(2)]
        rsum = [sb(f"rsum{s}", [P, 1], stack=st) for s in range(2)]
        rinv = [sb(f"rinv{s}", [P, 1], stack=st) for s in range(2)]
        a_w = sem("a_w")
        a_mask = sem("a_mask")
        a_g = sem("a_g")
        a_sig = sem("a_sig")
        a_r = sem("a_r")
        a_pr = pair("a_pr")
        a_pf = pair("a_pf")
        a_s = pair("a_s")
        a_nm = pair("a_nm")
        a_exp = pair("a_exp")
        a_ri = pair("a_ri")
        a_pn = pair("a_pn")
        a_t = pair("a_t")
        a_te = pair("a_te")
        a_pv = sem("a_pv")
        a_c = pair("a_c")
        a_x = sem("a_x")
        use_v, use_q, use_k, use_o = [0, 1, 2, 3], [4, 6, 8, 10], [5, 7, 9, 11], [12, 13, 14, 15]
        with nc.Block() as block:
            @block.sync
            def _(sp):
                for w, n in ((wv, "Wv"), (wq, "Wq"), (wk, "Wk"), (wo, "Wo")):
                    sp.dma_start(w[:], io[n].rearrange("(c p) n -> p c n", p=P)).then_inc(a_w, 16)
                sp.dma_start(bo[:], io["bo"]).then_inc(a_w, 16)
                sp.wait_ge(a_mask, 3)
                for n in range(NBLK // ZB):
                    sp.dma_start(g["Xe"][n * ZB * P:(n + 1) * ZB * P].rearrange("(a p) d -> p a d", p=P),
                                 zeros[:].rearrange("p (a d) -> p a d", a=1).to_broadcast([P, ZB, C])
                                 ).then_inc(a_z, 16)
                with sp.Fori(0, NB) as b:
                    sp.wait_ge(a_r, b)
                    sp.dma_start(gt[:].rearrange("p (c t) -> p c t", c=NC),
                                 G_dram[bass.ds(b * NC, NC)].rearrange("c p t -> p c t")).then_inc(a_g, 16)
                    m = NK // 2 + b * 2
                    for j in range(2):
                        g["wkv_load"](sp, m, j, b * NC + j)
                    for j in range(NC):
                        g["wkv_store"](sp, m + j // 2, j % 2, NK + b * NC + j)
                        if j + 2 < NC:
                            g["wkv_load"](sp, m + 1, j % 2, b * NC + j + 2)
                sp.wait_ge(a_z, 16 * (NBLK // ZB))
                for s in range(2):
                    sp.wait_ge(g["wk_store"][s], 16 * NK)

            @block.gpsimd
            def _(pool):
                pool.memset(mask[:], 0.0).then_inc(a_mask, 1)
                pool.memset(zeros[:], 0.0).then_inc(a_mask, 1)
                pool.wait_ge(a_mask, 2)
                pool.affine_select(out=mask[:], in_=mask[:], compare_op=ALU.is_ge, fill=MASKED, base=0,
                                   pattern=[[-1, P]], channel_multiplier=1).then_inc(a_mask, 1)
                with pool.Fori(0, NB) as b:
                    for j in range(NC):
                        g["wkv_gpsimd"](pool, NK // 2 + b * 2 + j // 2, j % 2)

            @block.tensor
            def _(pe):
                def project(b, use, lhs, rhs):
                    p = use % 2
                    pe.wait_ge(a_pf[p], b * 8 + use // 2)
                    for c in range(NC):
                        mm = pe.matmul(ps_p[p][:], lhs(c), rhs(c), start=c == 0, stop=c == NC - 1)
                    mm.then_inc(a_pr[p], 1)

                def project_qk(b, hg):
                    cols = slice(hg * P, hg * P + P)
                    project(b, use_q[hg], lambda c: wq[:, c, cols], lambda c: r[:, c, :])
                    project(b, use_k[hg], lambda c: wk[:, c, cols], lambda c: r[:, c, :])

                def scores(b, s):
                    hg, hh, qt, p = s // 16, s // 4 % 4, s % 4, s % 2
                    if s % 16 == 0:
                        pe.wait_ge(a_pf[0], b * 8 + use_q[hg] // 2 + 1)
                        pe.wait_ge(a_pf[1], b * 8 + use_k[hg] // 2 + 1)
                    pe.wait_ge(a_exp[p], b * HALF + s // 2)
                    rows, n = slice(hh * DH, hh * DH + DH), (qt + 1) * P
                    pe.matmul(ps_s[p][:, 0:n], qT[hg % 2][rows, qt * P:n], kT[hg % 2][rows, 0:n],
                              start=True, stop=True)
                    pe.matmul(ps_s[p][:, qt * P:n], ident[:], mask[:], start=False, stop=True,
                              skip_group_check=True).then_inc(a_s[p], 1)

                def transposes(b, s):
                    p, qt = s % 2, s % 4
                    pe.wait_ge(a_pn[p], b * HALF + s // 2 + 1)
                    pe.wait_ge(a_te[p], b * HALF + s // 2)
                    for kb in range(qt + 1):
                        mm = pe.transpose(ps_t[p][:, kb * P:kb * P + P], prob[p][:, kb * P:kb * P + P], ident[:])
                    mm.then_inc(a_t[p], 1)

                def context(b, h):
                    hg, hh = h // HG, h % HG
                    last = 4 * h + 3
                    pe.wait_ge(a_te[0], b * HALF + last // 2 + 1)
                    pe.wait_ge(a_te[1], b * HALF + last // 2 + 1)
                    if hh == 0:
                        pe.wait_ge(a_c[hg % 2], b * 2 + hg // 2)
                    for kb in range(NT):
                        mm = pe.matmul(ps_c[hg % 2][hh * DH:hh * DH + DH, kb * P:T],
                                       v[:, kb, h * DH:h * DH + DH], probT[h % 2][:, kb, kb * P:T],
                                       start=kb == 0, stop=kb == NT - 1, skip_group_check=True)
                    mm.then_inc(a_pv, 1)

                pe.wait_ge(a_w, 16 * 5)
                pe.wait_ge(a_mask, 3)
                with pe.Fori(0, NB) as b:
                    pe.wait_ge(a_r, b + 1)
                    for tt in range(NT):
                        project(b, use_v[tt], lambda c: r[:, c, tt * P:tt * P + P], lambda c: wv[:, c, :])
                    project_qk(b, 0)
                    for s in range(STEPS + 3):
                        if s < STEPS:
                            scores(b, s)
                        if s >= 6 and s % 4 == 2:
                            context(b, (s - 6) // 4)
                        if 2 <= s < STEPS + 2:
                            transposes(b, s - 2)
                        if s % 16 == 8 and s // 16 + 1 < NC:
                            project_qk(b, s // 16 + 1)
                    for p in range(2):
                        pe.wait_ge(a_c[p], b * 2 + 2)
                    for m in range(NC):
                        project(b, use_o[m], lambda c: wo[:, c, m * P:m * P + P], lambda c: cT[:, c, :])

            @block.scalar
            def _(act):
                def evict(b, use, out, scale=1.0):
                    act.wait_ge(a_pr[use % 2], b * 8 + use // 2 + 1)
                    act.activation(out, ps_p[use % 2][:], ACT.Copy, scale=scale).then_inc(a_pf[use % 2], 1)

                def evict_qk(b, hg):
                    evict(b, use_q[hg], qT[hg % 2][:], float(DH) ** -0.5)
                    evict(b, use_k[hg], kT[hg % 2][:])

                with act.Fori(0, NB) as b:
                    act.activation(r[:].rearrange("p c t -> p (c t)"), X[:, bass.ds(b * NC * T, NC * T)], ACT.Sigmoid
                                   ).then_inc(a_sig, 1)
                    for tt in range(NT):
                        evict(b, use_v[tt], v[:, tt, :])
                    evict_qk(b, 0)
                    for s in range(STEPS + 3):
                        if s < STEPS:
                            p, n = s % 2, (s % NT + 1) * P
                            act.wait_ge(a_nm[p], b * HALF + s // 2 + 1)
                            act.wait_ge(a_t[p], b * HALF + s // 2)
                            act.activation(prob[p][:, 0:n], ps_s[p][:, 0:n], ACT.Exp, bias=nmax[p][:],
                                           accum_out=rsum[p][:]).then_inc(a_exp[p], 1)
                        if s % 16 == 2 and s < STEPS:
                            j = s // 16
                            g["wkv_scalar"](act, NK // 2 + b * 2 + j // 2, j % 2)
                        if s % 16 == 8 and s // 16 + 1 < NC:
                            evict_qk(b, s // 16 + 1)
                        if s >= 18 and s % 16 == 2:
                            hg = (s - 18) // 16
                            act.wait_ge(a_pv, b * HEADS + hg * HG + HG)
                            act.activation(cT[:, hg, :], ps_c[hg % 2][:], ACT.Copy).then_inc(a_c[hg % 2], 1)

            @block.vector
            def _(dve):
                own = Steps(dve, wk_own)
                own.n = NK * g["WKV_OWN"]
                dve.wait_ge(a_w, 16 * 5)
                with dve.Fori(0, NB) as b:
                    own.enter(b, NC * g["WKV_OWN"])
                    dve.wait_ge(a_g, b * 16 + 16)
                    dve.wait_ge(a_sig, b + 1)
                    dve.tensor_tensor(r[:].rearrange("p c t -> p (c t)"), r[:].rearrange("p c t -> p (c t)"), gt[:],
                                      ALU.mult).then_inc(a_r, 1)
                    for s in range(STEPS + 2):
                        if s < STEPS:
                            p, n = s % 2, (s % NT + 1) * P
                            dve.wait_ge(a_s[p], b * HALF + s // 2 + 1)
                            dve.tensor_reduce(nmax[p][:], ps_s[p][:, 0:n], AX.X, ALU.max, negate=True
                                              ).then_inc(a_nm[p], 1)
                        if 1 <= s <= STEPS:
                            p = (s - 1) % 2
                            dve.wait_ge(a_exp[p], b * HALF + (s - 1) // 2 + 1)
                            dve.reciprocal(rinv[p][:], rsum[p][:]).then_inc(a_ri[p], 1)
                            n = ((s - 1) % NT + 1) * P
                            dve.wait_ge(a_ri[p], b * HALF + (s - 1) // 2 + 1)
                            dve.tensor_scalar(prob[p][:, 0:n], prob[p][:, 0:n], rinv[p][:], None, ALU.mult
                                              ).then_inc(a_pn[p], 1)
                        if s >= 2:
                            q = s - 2
                            p, h, qt = q % 2, q // 4, q % 4
                            if qt == 0:
                                dve.wait_ge(a_pv, b * HEADS + max(h - 1, 0))
                            dve.wait_ge(a_t[p], b * HALF + q // 2 + 1)
                            dve.tensor_copy(probT[h % 2][:, 0:qt + 1, qt * P:qt * P + P],
                                            ps_t[p][:, 0:(qt + 1) * P].rearrange("p (k q) -> p k q", q=P)
                                            ).then_inc(a_te[p], 1)
                        if s < STEPS:
                            if s % 16 == 0:
                                j = s // 16
                                tile = g["wkv_vector"](dve, NK // 2 + b * 2 + j // 2, j % 2, NK + b * NC + j, own)
                            next(tile, None)
                    for m in range(NC):
                        use = use_o[m]
                        dve.wait_ge(a_pr[use % 2], b * 8 + use // 2 + 1)
                        xk = X[:, bass.ds((b * NC + m) * T, T)]
                        dve.scalar_tensor_tensor(xk, ps_p[use % 2][:], bo[:, m:m + 1], xk, ALU.add, ALU.add
                                                 ).then_inc(a_pf[use % 2], 1)
                    own.leave(NB)


def experts(nc, io, g):
    sb, sem, pair, X, ident, psum, G_dram = (g[k] for k in ("sb", "sem", "pair", "X", "ident", "psum", "G_dram"))
    Xe, Ye = g["Xe"], g["Ye"]
    SJ = [(0, 128), (128, 128), (256, 128), (384, 128), (512, 96), (608, 96)]
    NSJ = len(SJ)
    with ExitStack() as keep:
        posk = sb("posk", [P, TT, TOPK], U32, stack=keep)
        wkk = sb("wkk", [P, TT, TOPK], stack=keep)
        endm = sb("endm", [P, E + 2], I32, stack=keep)
        parity = sb("parity", [P, NBLK], I32, stack=keep)
        wload = sb("wload", [P, NBLK], I32, stack=keep)
        m_in = sem("m_in")
        m_sh = sem("m_sh")
        m_g = sem("m_g")
        m_sig = sem("m_sig")
        m_r = sem("m_r")
        m_t = pair("m_t")
        m_te = pair("m_te")
        m_lg = sem("m_lg")
        m_c = sem("m_c")
        m_act = sem("m_act")
        m_d = sem("m_d")
        m_M = sem("m_M")
        m_pre = sem("m_pre")
        m_pos = sem("m_pos")
        m_sc = sem("m_sc")
        s_gu, s_sl, s_h, s_y, s_yf = (pair(n) for n in ("s_gu", "s_sl", "s_h", "s_y", "s_yf"))
        s_hall = sem("s_hall")
        with ExitStack() as st:
            R = sb("m_R", [P, NK, T], stack=st)
            rtok = sb("rtok", [P, TT, C], stack=st)
            gt = sb("m_gt", [P, NC * T], stack=st)
            rw = sb("rw", [P, NC, 2 * E], stack=st)
            ebias = sb("ebias", [P, E], stack=st)
            escale = sb("escale", [P, E], stack=st)
            sg = sb("sg", [P, NC, ISH], stack=st)
            su = sb("su", [P, NC, ISH], stack=st)
            sd = sb("sd", [P, NSJ, C], stack=st)
            ssl = [sb(f"ssl{s}", [P, T], stack=st) for s in range(2)]
            suu = [sb(f"suu{s}", [P, T], stack=st) for s in range(2)]
            hsh = sb("hsh", [P, NSJ, T], stack=st)
            before = sb("before", [P, P], stack=st)
            ones = sb("m_ones", [P, P], stack=st)
            lower = sb("lower", [P, E, E], stack=st)
            fresh = sb("fresh", [P, E, TT], stack=st)
            blk = sb("blk", [P, NBLK], stack=st)
            big = [sb(f"big{j}", [P, TT, E, E], BF16, stack=st) for j in range(2)]
            small = {n: sb(f"rt_{n}", [P, TT, E], stack=st) for n in
                     ("sl", "s", "ex", "pr", "bi", "rank", "M", "Wt", "tot", "inc", "pos", "t0", "t1")}
            row = {n: sb(f"rr_{n}", [P, E], stack=st) for n in ("nb", "end", "base", "c")}
            rowi = sb("rowi", [P, E], I32, stack=st)
            rt1 = {n: sb(f"r1_{n}", [P, TT], stack=st) for n in ("m", "sum", "ri")}
            ebc = sb("ebc", [P, NBLK, E], BF16, stack=st)
            ej = sb("ej", [P, NBLK], stack=st)
            eji = sb("eji", [P, NBLK], I32, stack=st)
            ps_t, ps_l, ps_pre = psum[0:2], psum[2], psum[3]
            ps_g, ps_u, ps_y = psum[4:6], psum[6:8], psum[0:2]
            with nc.Block() as block:
                @block.sync
                def _(sp):
                    sp.dma_start(rw[:], io["rw"].rearrange("(c p) e -> p c e", p=P)).then_inc(m_in, 16)
                    sp.dma_start(ebias[:], io["ebias"].to_broadcast([P, E])).then_inc(m_in, 16)
                    sp.dma_start(escale[:], io["escale"].to_broadcast([P, E])).then_inc(m_in, 16)
                    for b in range(NB):
                        if b:
                            sp.wait_ge(m_r, b)
                        sp.dma_start(gt[:].rearrange("p (c t) -> p c t", c=NC),
                                     G_dram[NK + b * NC:NK + b * NC + NC].rearrange("c p t -> p c t")
                                     ).then_inc(m_g, 16)
                    sp.dma_start(sg[:], io["SgT"].rearrange("(c p) n -> p c n", p=P)).then_inc(m_sh, 16)
                    sp.dma_start(su[:], io["SuT"].rearrange("(c p) n -> p c n", p=P)).then_inc(m_sh, 16)
                    sp.dma_start(sd[:, 0:4, :], io["SdT"][0:4 * P].rearrange("(c p) n -> p c n", p=P)
                                 ).then_inc(m_sh, 16)
                    sp.dma_start(sd[0:96, 4:6, :], io["SdT"][4 * P:ISH].rearrange("(c p) n -> p c n", p=96)
                                 ).then_inc(m_sh, 16)

                @block.gpsimd
                def _(pool):
                    pool.memset(before[:], 1.0).then_inc(m_c, 1)
                    pool.memset(ones[:], 1.0).then_inc(m_c, 1)
                    pool.memset(lower[:], 1.0).then_inc(m_c, 1)
                    pool.memset(fresh[:], 1.0).then_inc(m_c, 1)
                    pool.memset(endm[:], 0).then_inc(m_c, 1)
                    pool.iota(blk[:], pattern=[[1, NBLK]], base=0, channel_multiplier=0,
                              allow_small_or_imprecise_dtypes=True).then_inc(m_c, 1)
                    pool.wait_ge(m_c, 6)
                    pool.affine_select(out=before[:], in_=before[:], compare_op=ALU.is_gt, fill=0.0, base=0,
                                       pattern=[[1, P]], channel_multiplier=-1).then_inc(m_c, 1)
                    pool.affine_select(out=lower[:], in_=lower[:], compare_op=ALU.is_gt, fill=0.0, base=0,
                                       pattern=[[1, E], [-1, E]], channel_multiplier=0).then_inc(m_c, 1)
                    pool.affine_select(out=fresh[:], in_=fresh[:], compare_op=ALU.is_gt, fill=0.0, base=0,
                                       pattern=[[0, E], [1, TT]], channel_multiplier=0).then_inc(m_c, 1)

                    def shared(b, base, first):
                        for j in range(NSJ):
                            m, (_, n) = base + j // 2, SJ[j]
                            pool.wait_ge(s_sl[j % 2], 2 * m + 2)
                            if j == 0:
                                pool.wait_ge(m_c, 9)
                            pool.tensor_tensor(hsh[0:n, j, :], ssl[j % 2][0:n, :], suu[j % 2][0:n, :], ALU.mult
                                               ).then_inc(s_h[j % 2], 1)
                    with pool.Fori(0, NB // 2) as b:
                        shared(b, b * (NSJ // 2), None)
                    pool.wait_ge(m_pos, 1)
                    for p in range(2):
                        pool.wait_ge(m_te[p], TT // 2)
                    for t in range(TT):
                        for k in range(TOPK):
                            pool.indirect_dma_start(
                                out=Xe, out_offset=bass.IndirectOffsetOnAxis(ap=posk[:, t, k:k + 1], axis=0),
                                in_=rtok[:, t, :], in_offset=None, bounds_check=NBLK * P - 1, oob_is_err=False
                            ).then_inc(m_sc, 16)
                    pool.wait_ge(m_sc, 16 * TT * TOPK)

                @block.tensor
                def _(pe):
                    pe.wait_ge(m_in, 48)
                    for t in range(TT):
                        b, tt, p = t // NT, t % NT, t % 2
                        cols = slice(tt * P, tt * P + P)
                        pe.wait_ge(m_r, b + 1)
                        if t >= 2:
                            pe.wait_ge(m_te[p], t // 2)
                        for c in range(NC):
                            mm = pe.transpose(ps_t[p][:, c * P:c * P + P], R[:, b * NC + c, cols], ident[:])
                        mm.then_inc(m_t[p], 1)
                        for c in range(NC):
                            mm = pe.matmul(ps_l[:, t * 2 * E:(t + 1) * 2 * E], R[:, b * NC + c, cols], rw[:, c, :],
                                           start=c == 0, stop=c == NC - 1)
                    mm.then_inc(m_lg, 1)

                    def shared(b, base):
                        for j, (at, n) in enumerate(SJ):
                            p, m = j % 2, base + j // 2
                            pe.wait_ge(s_h[p], m)
                            for ps, w in ((ps_g[p], sg), (ps_u[p], su)):
                                for c in range(NC):
                                    mm = pe.matmul(ps[0:n, :], w[:, c, at:at + n], rview(b, c),
                                                   start=c == 0, stop=c == NC - 1)
                            mm.then_inc(s_gu[p], 1)
                        for p in range(2):
                            pe.wait_ge(s_h[p], base + NSJ // 2)
                        for c in range(NC):
                            p = c % 2
                            pe.wait_ge(s_yf[p], b * 2 + c // 2)
                            for j, (at, n) in enumerate(SJ):
                                mm = pe.matmul(ps_y[p][:], sd[0:n, j, c * P:c * P + P], hsh[0:n, j, :],
                                               start=j == 0, stop=j == NSJ - 1)
                            mm.then_inc(s_y[p], 1)

                    def rview(b, c):
                        return R[:].rearrange("p k t -> p (k t)")[:, bass.ds((b * NC + c) * T, T)]

                    pe.wait_ge(m_te[0], TT // 2)
                    pe.wait_ge(m_te[1], TT // 2)
                    pe.wait_ge(m_sh, 64)
                    shared(0, 0)
                    pe.wait_ge(m_M, 1)
                    pe.wait_ge(m_c, 9)
                    M = small["M"][:].rearrange("p t e -> p (t e)")
                    pe.matmul(ps_pre[:, 0:TT * E], before[:], M, start=True, stop=True)
                    pe.matmul(ps_pre[:, TT * E:2 * TT * E], ones[:], M, start=True, stop=True).then_inc(m_pre, 1)
                    with pe.Fori(1, NB) as b:
                        shared(b, b * (NSJ // 2))

                @block.scalar
                def _(act):
                    for b in range(NB):
                        xb = R[:].rearrange("p k t -> p (k t)")[:, b * NC * T:(b + 1) * NC * T]
                        act.activation(xb, X[:, b * NC * T:(b + 1) * NC * T], ACT.Sigmoid).then_inc(m_sig, 1)
                    for t in range(TT):
                        p = t % 2
                        act.wait_ge(m_t[p], t // 2 + 1)
                        act.activation(rtok[:, t, :], ps_t[p][:], ACT.Copy).then_inc(m_te[p], 1)
                    act.wait_ge(m_lg, 1)
                    act.activation(small["sl"][:], ps_l[:].rearrange("p (t e) -> p t e", t=TT)[:, :, 0:E], ACT.Silu
                                   ).then_inc(m_act, 1)
                    act.wait_ge(m_d, 1)
                    act.activation(small["ex"][:], small["s"][:], ACT.Exp).then_inc(m_act, 1)

                    def shared(b, copies):
                        for j, (_, n) in enumerate(SJ):
                            p, m = j % 2, b * (NSJ // 2) + j // 2
                            act.wait_ge(s_gu[p], m + 1)
                            act.activation(ssl[p][0:n, :], ps_g[p][0:n, :], ACT.Silu).then_inc(s_sl[p], 1)
                            if copies:
                                act.activation(suu[p][0:n, :], ps_u[p][0:n, :], ACT.Copy).then_inc(s_sl[p], 1)
                    with act.Fori(0, NB // 2) as b:
                        shared(b, True)
                    with act.Fori(NB // 2, NB) as b:
                        shared(b, False)

                @block.vector
                def _(dve):
                    own = Steps(dve, g["wk_own"])
                    own.n = 2 * NK * g["WKV_OWN"]
                    for b in range(NB):
                        xb = R[:].rearrange("p k t -> p (k t)")[:, b * NC * T:(b + 1) * NC * T]
                        dve.wait_ge(m_g, 16 * b + 16)
                        dve.wait_ge(m_sig, b + 1)
                        dve.tensor_tensor(xb, xb, gt[:], ALU.mult).then_inc(m_r, 1)
                    S = {k: v[:] for k, v in small.items()}
                    flat = {k: v[:].rearrange("p t e -> p (t e)") for k, v in small.items()}

                    def over_e(a):
                        return a[:].rearrange("p (t o) -> p t o", o=1).to_broadcast([P, TT, E])

                    def over_t(a):
                        return a[:].rearrange("p (o e) -> p o e", o=1).to_broadcast([P, TT, E])

                    def add_shared(b):
                        for c in range(NC):
                            p = c % 2
                            dve.wait_ge(s_y[p], b * 2 + c // 2 + 1)
                            xk = X[:, bass.ds((b * NC + c) * T, T)]
                            dve.tensor_tensor(xk, xk, ps_y[p][:], ALU.add).then_inc(s_yf[p], 1)
                    dve.wait_ge(m_act, 1)
                    own(dve.tensor_tensor(S["s"], ps_l[:].rearrange("p (t e) -> p t e", t=TT)[:, :, E:2 * E], S["sl"],
                                          ALU.mult)); own.sync()
                    own(dve.scalar_tensor_tensor(flat["t0"], flat["s"], -1.0, flat["s"], ALU.mult, ALU.max)); own.sync()
                    own(dve.tensor_reduce(rt1["m"][:], S["t0"], AX.X, ALU.max)); own.sync()
                    dve.tensor_tensor(S["s"], S["t0"], over_e(rt1["m"]), ALU.subtract).then_inc(m_d, 1)
                    dve.wait_ge(m_act, 2)
                    own(dve.tensor_reduce(rt1["sum"][:], S["ex"], AX.X, ALU.add)); own.sync()
                    own(dve.reciprocal(rt1["ri"][:], rt1["sum"][:])); own.sync()
                    own(dve.tensor_tensor(S["pr"], S["ex"], over_e(rt1["ri"]), ALU.mult)); own.sync()
                    dve.wait_ge(m_in, 48)
                    own(dve.tensor_tensor(S["bi"], S["pr"], over_t(ebias), ALU.add))
                    own(dve.tensor_tensor(S["t0"], S["pr"], over_t(escale), ALU.mult)); own.sync()
                    own(dve.tensor_scalar(flat["Wt"], flat["t0"], 1.0, None, ALU.add))
                    this = S["bi"].rearrange("p t (e o) -> p t e o", o=1).to_broadcast([P, TT, E, E])
                    other = S["bi"].rearrange("p t (o e) -> p t o e", o=1).to_broadcast([P, TT, E, E])
                    low = lower[:].rearrange("p (o e) f -> p o e f", o=1).to_broadcast([P, TT, E, E])
                    own(dve.tensor_tensor(big[0][:], other, this, ALU.is_equal)); own.sync()
                    dve.wait_ge(m_c, 9)
                    own(dve.tensor_tensor(big[0][:], big[0][:], low, ALU.mult))
                    own(dve.tensor_tensor(big[1][:], other, this, ALU.is_gt)); own.sync()
                    own(dve.tensor_tensor(big[0][:], big[0][:], big[1][:], ALU.add)); own.sync()
                    own(dve.tensor_reduce(flat["rank"], big[0][:].rearrange("p t e f -> p (t e) f"), AX.X, ALU.add))
                    own.sync()
                    dve.tensor_scalar(flat["M"], flat["rank"], TOPK - 0.5, None, ALU.is_lt).then_inc(m_M, 1)
                    add_shared(0)
                    dve.wait_ge(m_pre, 1)
                    tot_et = small["tot"][:].rearrange("p a b -> p (a b)").rearrange("p (e t) -> p e t", e=E)
                    own(dve.tensor_copy(tot_et, ps_pre[:, TT * E:2 * TT * E].rearrange("p (t e) -> p e t", t=TT)))
                    own.sync()
                    own(dve.tensor_tensor_scan(flat["inc"], fresh[:].rearrange("p e t -> p (e t)"), flat["tot"], 0.0,
                                               ALU.mult, ALU.add)); own.sync()
                    inc_et = flat["inc"].rearrange("p (e t) -> p e t", e=E)
                    own(dve.tensor_scalar(rowi[:], inc_et[:, :, TT - 1], float(P - 1), None, ALU.add)); own.sync()
                    own(dve.tensor_scalar(rowi[:], rowi[:], 7, None, ALU.arith_shift_right)); own.sync()
                    own(dve.tensor_scalar(row["nb"][:], rowi[:], 1.0, None, ALU.max)); own.sync()
                    own(dve.tensor_tensor_scan(row["end"][:], ones[:, 0:E], row["nb"][:], 0.0, ALU.mult, ALU.add))
                    own(dve.tensor_tensor(flat["t0"], flat["inc"], flat["tot"], ALU.subtract)); own.sync()
                    own(dve.tensor_tensor(row["c"][:], row["end"][:], row["nb"][:], ALU.subtract)); own.sync()
                    own(dve.tensor_scalar(row["base"][:], row["c"][:], float(P), None, ALU.mult)); own.sync()
                    own(dve.tensor_tensor(S["t1"], flat["t0"].rearrange("p (e t) -> p t e", e=E), over_t(row["base"]),
                                          ALU.add)); own.sync()
                    own(dve.tensor_tensor(flat["pos"], flat["t1"], ps_pre[:, 0:TT * E], ALU.add)); own.sync()
                    for k in range(TOPK):
                        own(dve.scalar_tensor_tensor(flat["t0"], flat["rank"], float(k), flat["pos"], ALU.is_equal,
                                                     ALU.mult))
                        own(dve.scalar_tensor_tensor(flat["t1"], flat["rank"], float(k), flat["Wt"], ALU.is_equal,
                                                     ALU.mult)); own.sync()
                        own(dve.tensor_reduce(rt1["m"][:], S["t0"], AX.X, ALU.add))
                        own(dve.tensor_reduce(wkk[:, :, k], S["t1"], AX.X, ALU.add)); own.sync()
                        own(dve.tensor_copy(posk[:, :, k], rt1["m"][:])); own.sync()
                    own(dve.tensor_copy(endm[:, 2:E + 2], row["end"][:]))
                    own(dve.tensor_tensor(ebc[:], row["end"][:].rearrange("p (o e) -> p o e", o=1).to_broadcast([P, NBLK, E]),
                                          blk[:].rearrange("p (n o) -> p n o", o=1).to_broadcast([P, NBLK, E]),
                                          ALU.is_le)); own.sync()
                    own(dve.tensor_reduce(ej[:], ebc[:], AX.X, ALU.add)); own.sync()
                    own(dve.tensor_scalar(eji[:], ej[:], float(E - 1), None, ALU.min)); own.sync()
                    own(dve.tensor_scalar(parity[:], eji[:], 1, None, ALU.bitwise_and)); own.sync()
                    dve.tensor_scalar(wload[:], eji[:], 64.0, 64.0, ALU.mult, ALU.add).then_inc(m_pos, 1)

                    add_shared(1)
                    with dve.Fori(NB // 2, NB) as b:
                        for j, (_, n) in enumerate(SJ):
                            p, m = j % 2, b * (NSJ // 2) + j // 2
                            dve.wait_ge(s_sl[p], m + NSJ // 2 * (NB // 2) + 1)
                            dve.wait_ge(s_gu[p], m + 1)
                            dve.tensor_tensor(hsh[0:n, j, :], ssl[p][0:n, :], ps_u[p][0:n, :], ALU.mult
                                              ).then_inc(s_h[p], 1)
                        add_shared(b)
                    g["own_after_router"] = own.n

        IJ = [(0, P), (P, P), (2 * P, I - 2 * P)]
        GW, DW = NC * I, len(IJ) * C
        b_x, b_tx, b_xt, b_gu, b_sl, b_h, b_st = (pair(n) for n in
                                                  ("b_x", "b_tx", "b_xt", "b_gu", "b_sl", "b_h", "b_st"))
        b_ht, b_hte, b_y, b_ye, b_w = (sem(n) for n in ("b_ht", "b_hte", "b_y", "b_ye", "b_w"))
        UN = 4
        with ExitStack() as st:
            g["wkv_buffers"](st, "b")
            wg = sb("wg", [P, 2 * GW], stack=st)
            wu = sb("wu", [P, 2 * GW], stack=st)
            wd = sb("wd", [P, 2 * DW], stack=st)
            xg = [sb(f"xg{s}", [P, C], stack=st) for s in range(2)]
            xgT = [sb(f"xgT{s}", [P, NC, P], stack=st) for s in range(2)]
            sl = [sb(f"bsl{s}", [P, I], stack=st) for s in range(2)]
            h = [sb(f"bh{s}", [P, I], stack=st) for s in range(2)]
            hT = [sb(f"hT{s}", [P, len(IJ), P], stack=st) for s in range(2)]
            ys = [sb(f"ys{s}", [P, C], stack=st) for s in range(2)]
            ps_x, ps_g, ps_u, ps_h, ps_y = psum[0:2], psum[2:4], psum[4:6], psum[6], psum[7]
            WITH = NK

            def wkv_at(i, s):
                return NK + i, 2 * NK + i * 2 + s
            with nc.Block() as block:
                @block.sync
                def _(sp):
                    def load(n, m, p):
                        sp.wait_ge(b_tx[p], m)
                        sp.dma_start(xg[p][:], Xe[bass.ds(n * P, P)]).then_inc(b_x[p], 16)

                    def store(n, p):
                        sp.wait_ge(b_ye, n + 1)
                        sp.dma_start(Ye[bass.ds(n * P, P)], ys[p][:]).then_inc(b_st[p], 16)
                    load(0, 0, 0)
                    load(1, 0, 1)

                    def tiles_load(i, half):
                        for s in range(2):
                            g["wkv_load"](sp, wkv_at(i, s)[0], s, i * 2 + s - half * NK)

                    for half in range(2):
                        with sp.Fori(half * 8, half * 8 + 8) as i:
                            tiles_load(i, half)
                            for q in range(UN):
                                load(i * UN + q + 2, i * (UN // 2) + q // 2 + 1, q % 2)
                                store(i * UN + q, q % 2)
                                if q >= 2:
                                    m, lk = wkv_at(i, q - 2)
                                    g["wkv_store"](sp, m, q - 2, lk)
                    with sp.Fori(16, NBLK // UN - 1) as i:
                        for q in range(UN):
                            load(i * UN + q + 2, i * (UN // 2) + q // 2 + 1, q % 2)
                            store(i * UN + q, q % 2)
                    for q in range(UN):
                        n = NBLK - UN + q
                        if q < 2:
                            load(n + 2, n // 2 + 1, q % 2)
                        store(n, q % 2)
                    for p in range(2):
                        sp.wait_ge(b_st[p], 16 * NBLK // 2)
                        sp.wait_ge(g["wk_store"][p], 16 * 2 * NK)

                @block.gpsimd
                def _(pool):
                    with pool.Fori(0, E // 2) as i:
                        for s in range(2):
                            e = i * 2 + s
                            done = pool.value_load(endm[0:1, bass.ds(e, 1)], min_val=0, max_val=NBLK)
                            pool.wait_ge(b_w, e * 64)
                            pool.wait_ge(b_y, done)
                            pool.wait_ge(m_pos, 1)
                            pool.dma_start(wg[:, s * GW:(s + 1) * GW].rearrange("p (a c n) -> p a c n", a=1, c=NC),
                                           io["WgT"][bass.ds(e, 1)].rearrange("a (c p) n -> p a c n", p=P)
                                           ).then_inc(b_w, 16)
                            pool.dma_start(wu[:, s * GW:(s + 1) * GW].rearrange("p (a c n) -> p a c n", a=1, c=NC),
                                           io["WuT"][bass.ds(e, 1)].rearrange("a (c p) n -> p a c n", p=P)
                                           ).then_inc(b_w, 16)
                            pool.dma_start(wd[:, s * DW:s * DW + 2 * C].rearrange("p (a c n) -> p a c n", a=1, c=2),
                                           io["WdT"][bass.ds(e, 1), 0:2 * P].rearrange("a (c p) n -> p a c n", p=P)
                                           ).then_inc(b_w, 16)
                            pool.dma_start(wd[0:I - 2 * P, s * DW + 2 * C:(s + 1) * DW],
                                           io["WdT"][bass.ds(e, 1), 2 * P:I].rearrange("a p n -> p (a n)")
                                           ).then_inc(b_w, 16)

                @block.tensor
                def _(pe):
                    def turn_x(n, m, p):
                        pe.wait_ge(b_x[p], m * 16 + 16)
                        pe.wait_ge(b_xt[p], m)
                        for c in range(NC):
                            mm = pe.transpose(ps_x[p][:, c * P:c * P + P], xg[p][:, c * P:c * P + P], ident[:])
                        mm.then_inc(b_tx[p], 1)

                    def gate(n, m, p, par):
                        pe.wait_ge(b_xt[p], m + 1)
                        pe.wait_ge(b_h[p], m)
                        for c in range(NC):
                            pe.matmul(ps_g[p][:, 0:I], xgT[p][:, c, :], wg[:, bass.ds(par * GW + c * I, I)],
                                      start=c == 0, stop=c == NC - 1)

                    def up(n, m, p, par):
                        for c in range(NC):
                            mm = pe.matmul(ps_u[p][:, 0:I], xgT[p][:, c, :], wu[:, bass.ds(par * GW + c * I, I)],
                                           start=c == 0, stop=c == NC - 1)
                        mm.then_inc(b_gu[p], 1)

                    def turn_h(n, m, p):
                        pe.wait_ge(b_h[p], m + 1)
                        pe.wait_ge(b_hte, n)
                        for j, (at, w) in enumerate(IJ):
                            mm = pe.transpose(ps_h[0:w, j * P:j * P + P], h[p][:, at:at + w], ident[:])
                        mm.then_inc(b_ht, 1)

                    def down(n, m, p, par):
                        pe.wait_ge(b_hte, n + 1)
                        pe.wait_ge(b_ye, n)
                        for j, (at, w) in enumerate(IJ):
                            mm = pe.matmul(ps_y[:], hT[p][0:w, j, :], wd[0:w, bass.ds(par * DW + j * C, C)],
                                           start=j == 0, stop=j == len(IJ) - 1)
                        mm.then_inc(b_y, 1)

                    with pe.Fori(0, NBLK // UN) as i:
                        pars = []
                        turn_x(i * UN, i * 2, 0)
                        for q in range(UN + 1):
                            n, m, p = i * UN + q, i * 2 + q // 2, q % 2
                            if q < UN:
                                need = pe.value_load(wload[0:1, bass.ds(n, 1)], min_val=0, max_val=64 * E)
                                pars.append(pe.value_load(parity[0:1, bass.ds(n, 1)], min_val=0, max_val=1))
                                pe.wait_ge(b_w, need)
                                gate(n, m, p, pars[q])
                            if q:
                                turn_h(n - 1, i * 2 + (q - 1) // 2, (q - 1) % 2)
                            if q < UN:
                                up(n, m, p, pars[q])
                            if q + 1 < UN:
                                turn_x(n + 1, i * 2 + (q + 1) // 2, (q + 1) % 2)
                            if q:
                                down(n - 1, i * 2 + (q - 1) // 2, (q - 1) % 2, pars[q - 1])

                @block.scalar
                def _(act):
                    def evict_x(n, m, p):
                        act.wait_ge(b_tx[p], m + 1)
                        act.activation(xgT[p][:].rearrange("p c t -> p (c t)"), ps_x[p][:], ACT.Copy
                                       ).then_inc(b_xt[p], 1)

                    def evict_y(n, m, p):
                        act.wait_ge(b_y, n + 1)
                        act.wait_ge(b_st[p], m * 16)
                        act.activation(ys[p][:], ps_y[:], ACT.Copy).then_inc(b_ye, 1)

                    def body(i, tiles):
                        evict_x(i * UN, i * 2, 0)
                        for q in range(UN + 1):
                            n, m, p = i * UN + q, i * 2 + q // 2, q % 2
                            if q < UN:
                                act.wait_ge(b_gu[p], m + 1)
                                act.activation(sl[p][:], ps_g[p][:, 0:I], ACT.Silu).then_inc(b_sl[p], 1)
                            if q + 1 < UN:
                                evict_x(n + 1, i * 2 + (q + 1) // 2, (q + 1) % 2)
                            if q:
                                evict_y(n - 1, i * 2 + (q - 1) // 2, (q - 1) % 2)
                            if tiles and q in (0, 2):
                                g["wkv_scalar"](act, wkv_at(i, q // 2)[0], q // 2)
                    with act.Fori(0, WITH) as i:
                        body(i, True)
                    with act.Fori(WITH, NBLK // UN) as i:
                        body(i, False)

                @block.vector
                def _(dve):
                    own = Steps(dve, g["wk_own"])
                    own.n = g["own_after_router"]

                    def evict_h(n, m, p):
                        dve.wait_ge(b_ht, n + 1)
                        own(dve.tensor_copy(hT[p][:, 0:2, :].rearrange("p c t -> p (c t)"), ps_h[:, 0:2 * P]))
                        w = IJ[2][1]
                        own.sync()
                        dve.tensor_copy(hT[p][0:w, 2, :], ps_h[0:w, 2 * P:3 * P]).then_inc(b_hte, 1)

                    def body(i, tiles):
                        per = UN
                        if tiles:
                            per += 2 * (g["WKV_OWN"] + 1)
                        own.enter(i - (0 if tiles else WITH), per)
                        for q in range(UN + 1):
                            n, m, p = i * UN + q, i * 2 + q // 2, q % 2
                            if q < UN:
                                if tiles and q % 2 == 0:
                                    tile = g["wkv_vector"](dve, *[wkv_at(i, q // 2)[0], q // 2, wkv_at(i, q // 2)[1]],
                                                           own, euv_here=True)
                                if tiles:
                                    for _ in range(2 if q % 2 == 0 else 6):
                                        next(tile, None)
                                dve.wait_ge(b_sl[p], m + 1)
                                dve.wait_ge(b_gu[p], m + 1)
                                dve.tensor_tensor(h[p][:], sl[p][:], ps_u[p][:, 0:I], ALU.mult).then_inc(b_h[p], 1)
                            if q:
                                evict_h(n - 1, i * 2 + (q - 1) // 2, (q - 1) % 2)
                            if tiles and q < UN:
                                for _ in range(2 if q % 2 == 0 else 6):
                                    next(tile, None)
                        own.leave(WITH if tiles else NBLK // UN - WITH)
                    with dve.Fori(0, WITH) as i:
                        body(i, True)
                    with dve.Fori(WITH, NBLK // UN) as i:
                        body(i, False)
                    g["own_after_blocks"] = own.n

        d_y = pair("d_y")
        d_dg, d_done, d_b, d_f = (pair(n) for n in ("d_dg", "d_done", "d_b", "d_f"))
        with ExitStack() as st:
            yk = [[sb(f"yk{s}{k}", [P, C], stack=st) for k in range(TOPK)] for s in range(2)]
            dg = [[sb(f"dg{s}{k}", [P, P], stack=st) for k in range(TOPK)] for s in range(2)]
            with nc.Block() as block:
                @block.gpsimd
                def _(pool):
                    for t in range(TT):
                        p = t % 2
                        if t >= 2:
                            pool.wait_ge(d_done[p], t // 2)
                        for k in range(TOPK):
                            pool.indirect_dma_start(
                                out=yk[p][k][:], out_offset=None, in_=Ye,
                                in_offset=bass.IndirectOffsetOnAxis(ap=posk[:, t, k:k + 1], axis=0),
                                bounds_check=NBLK * P - 1, oob_is_err=False).then_inc(d_y[p], 16)

                @block.tensor
                def _(pe):
                    for t in range(TT):
                        p, b, tt = t % 2, t // NT, t % NT
                        pe.wait_ge(d_y[p], 16 * TOPK * (t // 2 + 1))
                        pe.wait_ge(d_dg[p], TOPK * (t // 2 + 1))
                        if tt == 0 and b >= 2:
                            pe.wait_ge(d_f[b % 2], b // 2)
                        for c in range(NC):
                            for k in range(TOPK):
                                mm = pe.matmul(psum[b % 2 * NC + c][:, tt * P:tt * P + P], yk[p][k][:, c * P:c * P + P],
                                               dg[p][k][:], start=k == 0, stop=k == TOPK - 1)
                        mm.then_inc(d_done[p], 1)

                def add(dve, b):
                    for p in range(2):
                        dve.wait_ge(d_done[p], (b + 1) * 2)
                    for c in range(NC):
                        k = b * NC + c
                        ins = dve.tensor_tensor(X[:, k * T:(k + 1) * T], X[:, k * T:(k + 1) * T],
                                                psum[b % 2 * NC + c][:], ALU.add)
                    ins.then_inc(d_f[b % 2], 1)

                @block.vector
                def _(dve):
                    for t in range(TT):
                        p, b = t % 2, t // NT
                        if t >= 2:
                            dve.wait_ge(d_done[p], t // 2)
                        for k in range(TOPK):
                            dve.tensor_scalar(dg[p][k][:], ident[:], wkk[:, t, k:k + 1], None, ALU.mult
                                              ).then_inc(d_dg[p], 1)
                        if t % NT == 1 and b:
                            add(dve, b - 1)
                    add(dve, NB - 1)

def state_space(nc, io, g):
    sb, sem, pair, X, ident, psum, G_dram = (g[k] for k in ("sb", "sem", "pair", "X", "ident", "psum", "G_dram"))
    BC_dram = nc.dram_tensor("BC_scratch", [2 * NS, T], F32, kind="Internal").ap()
    RING = 8
    TAPS = 4
    v_in, v_c, v_g, v_sig, v_r, v_u, v_x, v_dt, v_bc, v_bcs, v_dl, v_abs, v_ln, v_du = (
        sem(n) for n in ("v_in", "v_c", "v_g", "v_sig", "v_r", "v_u", "v_x", "v_dt", "v_bc", "v_bcs", "v_dl", "v_abs",
                         "v_ln", "v_du"))
    v_ring = [sem(f"v_ring{j}") for j in range(RING)]
    v_da, v_h, v_hc, v_y, v_out, v_a = (sem(n) for n in ("v_da", "v_h", "v_hc", "v_y", "v_out", "v_a"))
    v_own = sem("v_own")
    v_rel = sem("v_rel")
    with ExitStack() as st:
        gt = sb("v_gt", [P, NC, T], stack=st)
        sig = sb("v_sigx", [P, NC, T], stack=st)
        r = sb("v_r", [P, NC, TAPS - 1 + T], stack=st)
        u = sb("v_u", [P, NC, T], stack=st)
        du = sb("v_dut", [P, NC, T], stack=st)
        delta = sb("v_delta", [P, NC, T], stack=st)
        soft = sb("v_soft", [P, NC, T], stack=st)
        relu = sb("v_relu", [P, NC, T], stack=st)
        dtT = sb("v_dtT", [P, T], stack=st)
        bcT = sb("v_bcT", [2 * NS, T], stack=st)
        ring = [sb(f"v_bc{j}", [P, 2, T], stack=st) for j in range(RING)]
        dA, dBu, h, hC = ([sb(f"v_{n}{s}", [P, NC, T], stack=st) for s in range(2)] for n in ("dA", "dBu", "h", "hC"))
        xw = sb("v_xw", [P, NC, DTR + 2 * NS], stack=st)
        dw = sb("v_dw", [P, C], stack=st)
        taps = sb("v_taps", [P, NC, TAPS], stack=st)
        cvec = sb("v_cvec", [P, 3, NC], stack=st)
        alog = sb("v_alog", [P, NC, NS], stack=st)
        aexp = sb("v_aexp", [P, NC, NS], stack=st)
        A = sb("v_A", [P, NC, NS], stack=st)
        ps_y, ps_dt, ps_bc, ps_dl = psum[0:4], psum[4], psum[5], psum[6:8]
        with nc.Block() as block:
            @block.sync
            def _(sp):
                sp.dma_start(xw[:], io["xprojT"].rearrange("(c p) n -> p c n", p=P)).then_inc(v_in, 16)
                sp.dma_start(dw[:], io["dtprojT"]).then_inc(v_in, 16)
                sp.dma_start(taps[:], io["taps"]).then_inc(v_in, 16)
                sp.dma_start(cvec[:], io["cvec"]).then_inc(v_in, 16)
                sp.dma_start(alog[:], io["alog"]).then_inc(v_in, 16)
                with sp.Fori(0, NB) as b:
                    sp.wait_ge(v_r, b)
                    sp.dma_start(gt[:], G_dram[bass.ds(b * NC + 2 * NK, NC)].rearrange("c p t -> p c t")
                                 ).then_inc(v_g, 16)
                    sp.wait_ge(v_bc, b + 1)
                    sp.dma_start(BC_dram, bcT[:]).then_inc(v_bcs, 16)
                    sp.wait_ge(v_bcs, b * 16 + 16)
                    for n in range(NS):
                        sp.wait_ge(v_hc, b * NS if n < RING else b * NS + (n - RING + 1))
                        sp.dma_start(ring[n % RING][:],
                                     BC_dram.rearrange("(a n) t -> n a t", a=2)[n:n + 1].to_broadcast([P, 2, T])
                                     ).then_inc(v_ring[n % RING], 16)

            @block.gpsimd
            def _(pool):
                pool.memset(r[:, :, 0:TAPS - 1], 0.0).then_inc(v_c, 1)
                with pool.Fori(0, NB) as b:
                    for n in range(NS):
                        p = n % 2
                        pool.wait_ge(v_ring[n % RING], (b * (NS // RING) + n // RING) * 16 + 16)
                        pool.wait_ge(v_y, b * NS if n < 2 else b * NS + n - 1)
                        pool.wait_ge(v_h, b * NS + n + 1)
                        pool.tensor_tensor(hC[p][:], h[p][:], ring[n % RING][:, 1:2, :].to_broadcast([P, NC, T]),
                                           ALU.mult).then_inc(v_hc, 1)

            @block.tensor
            def _(pe):
                pe.wait_ge(v_in, 80)
                with pe.Fori(0, NB) as b:
                    pe.wait_ge(v_u, b + 1)
                    pe.wait_ge(v_x, b * 2)
                    for c in range(NC):
                        mm = pe.matmul(ps_bc[0:2 * NS, :], xw[:, c, DTR:], u[:, c, :], start=c == 0, stop=c == NC - 1)
                    for c in range(NC):
                        mm = pe.matmul(ps_dt[:], xw[:, c, 0:DTR], u[:, c, :], start=c == 0, stop=c == NC - 1)
                    mm.then_inc(v_dt, 1)
                    pe.wait_ge(v_x, b * 2 + 2)
                    for c in range(NC):
                        pe.wait_ge(v_abs, b * NC + max(c - 1, 0))
                        pe.wait_ge(v_rel, b * NC + max(c - 1, 0))
                        pe.matmul(ps_dl[c % 2][:], dw[:, c * P:c * P + P], dtT[:], start=True, stop=True
                                  ).then_inc(v_dl, 1)
                    pe.wait_ge(v_out, b * NC)
                    for n in range(NS):
                        pe.wait_ge(v_hc, b * NS + n + 1)
                        for c in range(NC):
                            mm = pe.matmul(ps_y[c][:], ident[:], hC[n % 2][:, c, :], start=n == 0, stop=n == NS - 1,
                                           skip_group_check=True)
                        mm.then_inc(v_y, 1)

            @block.scalar
            def _(act):
                act.wait_ge(v_in, 80)
                act.activation(aexp[:], alog[:], ACT.Exp).then_inc(v_a, 1)
                act.wait_ge(v_a, 1)
                act.activation(A[:], aexp[:], ACT.Copy, scale=-1.0).then_inc(v_a, 1)
                act.wait_ge(v_a, 2)
                with act.Fori(0, NB) as b:
                    act.activation(sig[:].rearrange("p c t -> p (c t)"), X[:, bass.ds(b * NC * T, NC * T)], ACT.Sigmoid
                                   ).then_inc(v_sig, 1)
                    act.wait_ge(v_dt, b + 1)
                    act.activation(bcT[:], ps_bc[0:2 * NS, :], ACT.Copy).then_inc(v_bc, 1)
                    act.activation(dtT[:], ps_dt[:], ACT.Copy).then_inc(v_x, 2)
                    for c in range(NC):
                        act.wait_ge(v_dl, b * NC + c + 1)
                        act.activation(soft[:, c, :], ps_dl[c % 2][:], ACT.Abs, bias=cvec[:, 1, c:c + 1]
                                       ).then_inc(v_abs, 1)
                    act.wait_ge(v_abs, b * NC + NC)
                    flat = soft[:].rearrange("p c t -> p (c t)")
                    act.activation(flat, flat, ACT.Exp, scale=-1.0).then_inc(v_ln, 1)
                    act.wait_ge(v_ln, b * 2 + 1)
                    act.activation(flat, flat, ACT.Ln, bias=1.0).then_inc(v_ln, 1)
                    act.wait_ge(v_du, b + 1)
                    for n in range(NS):
                        act.wait_ge(v_h, b * NS if n < 2 else b * NS + n - 1)
                        for c in range(NC):
                            ins = act.activation(dA[n % 2][:, c, :], delta[:, c, :], ACT.Exp, scale=A[:, c, n:n + 1])
                        ins.then_inc(v_da, 1)

            @block.vector
            def _(dve):
                own = Steps(dve, v_own)
                dve.wait_ge(v_in, 80)
                dve.wait_ge(v_c, 1)
                with dve.Fori(0, NB) as b:
                    own.enter(b, NC * TAPS + NS * NC + NC)
                    dve.wait_ge(v_g, b * 16 + 16)
                    dve.wait_ge(v_sig, b + 1)
                    dve.tensor_tensor(r[:, :, TAPS - 1:], sig[:], gt[:], ALU.mult).then_inc(v_r, 1)
                    dve.wait_ge(v_r, b + 1)
                    for j in range(TAPS):
                        for c in range(NC):
                            tap, src = taps[:, c, j:j + 1], r[:, c, j:j + T]
                            if j == 0:
                                own(dve.tensor_scalar(u[:, c, :], src, tap, cvec[:, 0, c:c + 1], ALU.mult, ALU.add))
                            else:
                                ins = dve.scalar_tensor_tensor(u[:, c, :], src, tap, u[:, c, :], ALU.mult, ALU.add)
                                if j < TAPS - 1 or c < NC - 1:
                                    own(ins)
                                else:
                                    ins.then_inc(v_u, 1)
                        if j < TAPS - 1:
                            own.sync()
                    for c in range(NC):
                        dve.wait_ge(v_abs, b * NC + c + 1)
                        dve.tensor_scalar(relu[:, c, :], ps_dl[c % 2][:], cvec[:, 1, c:c + 1], 0.0, ALU.add, ALU.max
                                          ).then_inc(v_rel, 1)
                    dve.wait_ge(v_rel, b * NC + NC)
                    dve.wait_ge(v_ln, b * 2 + 2)
                    dve.tensor_tensor(delta[:], relu[:], soft[:], ALU.add).then_inc(v_du, 1)
                    dve.wait_ge(v_du, b + 1)
                    dve.wait_ge(v_u, b + 1)
                    own(dve.tensor_tensor(du[:], delta[:], u[:], ALU.mult))
                    for n in range(NS):
                        p = n % 2
                        own.sync()
                        dve.wait_ge(v_ring[n % RING], (b * (NS // RING) + n // RING) * 16 + 16)
                        own(dve.tensor_tensor(dBu[p][:], du[:], ring[n % RING][:, 0:1, :].to_broadcast([P, NC, T]),
                                              ALU.mult))
                        own.sync()
                        dve.wait_ge(v_da, b * NS + n + 1)
                        dve.wait_ge(v_hc, b * NS if n < 2 else b * NS + n - 1)
                        for c in range(NC):
                            ins = dve.tensor_tensor_scan(h[p][:, c, :], dA[p][:, c, :], dBu[p][:, c, :], 0.0,
                                                         ALU.mult, ALU.add)
                            if c < NC - 1:
                                own(ins)
                        ins.then_inc(v_h, 1)
                    dve.wait_ge(v_y, b * NS + NS)
                    for c in range(NC):
                        own(dve.scalar_tensor_tensor(u[:, c, :], u[:, c, :], cvec[:, 2, c:c + 1], ps_y[c][:],
                                                     ALU.mult, ALU.add))
                    own.sync()
                    for c in range(NC):
                        xk = X[:, bass.ds((b * NC + c) * T, T)]
                        dve.tensor_tensor(xk, xk, u[:, c, :], ALU.add).then_inc(v_out, 1)
                    own.leave(NB)


def linear_attention(nc, io, g):
    sb, sem, pair, X, ident, psum, G_dram = (g[k] for k in ("sb", "sem", "pair", "X", "ident", "psum", "G_dram"))
    L = NB
    DK = C // 2
    HK, HV = DK // HEADS, C // HEADS
    f_in, f_g, f_sig, f_r, f_cv, f_xs, f_own, f_o, f_sq, f_std, f_sc, f_d, f_st, f_var, f_out = (
        sem(n) for n in ("f_in", "f_g", "f_sig", "f_r", "f_cv", "f_xs", "f_own", "f_o", "f_sq", "f_std", "f_sc", "f_d",
                         "f_st", "f_var", "f_out"))
    f_p, f_pf = ([sem(f"{n}{j}") for j in range(4)] for n in ("f_p", "f_pf"))
    f_t, f_te, f_w, f_wf = (pair(n) for n in ("f_t", "f_te", "f_w", "f_wf"))
    with ExitStack() as st:
        wqk, wv, wg, wo = (sb(f"f_w{n}", [P, NC, C], stack=st) for n in ("qk", "v", "g", "o"))
        gt = sb("f_gt", [P, NK, P], stack=st)
        r = sb("f_rt", [P, NK, P], stack=st)
        cv = sb("f_conv", [P, NK, P], stack=st)
        xs = sb("f_xst", [P, NK, P], stack=st)
        qk = sb("f_qk", [P, L, 2 * DK], stack=st)
        v = sb("f_v", [P, L, C], stack=st)
        gate = sb("f_gate", [P, L, C], stack=st)
        ra = sb("f_ra", [P, L, 2 * HEADS, HK // 2], stack=st)
        rb = sb("f_rb", [P, L, 2 * HEADS, HK // 2], stack=st)
        rot = sb("f_rot", [P, L, 2 * HEADS, HK], stack=st)
        vw = sb("f_vw", [P, L, C], stack=st)
        o = sb("f_ot", [P, L, C], stack=st)
        oT = sb("f_oT", [P, NC, L * P], stack=st)
        xo = sb("f_xo", [P, NK, P], stack=st)
        cs = sb("f_cs", [P, 2, L, HK // 2], stack=st)
        taps = sb("f_taps", [P, NC, 2], stack=st)
        rr = sb("f_rr", [P, 2, C], stack=st)
        rd = sb("f_rd", [P, C], stack=st)
        eps = sb("f_eps", [P, 1], stack=st)
        tiny = {n: sb(f"f_{n}", [P, L * HEADS], stack=st) for n in
                ("dd", "ad", "sel", "sc_", "cnt", "rc", "fl", "mu", "var_", "std_", "rs")}
        same = sb("f_same", [P, L, L, HEADS], stack=st)
        dots = sb("f_dots", [P, L, L, HEADS], stack=st)
        ps_p, ps_t, ps_w = psum[0:4], psum[4:6], psum[6:8]
        JT = T // P
        with nc.Block() as block:
            @block.sync
            def _(sp):
                for w, n in ((wqk, "Wqk"), (wv, "fWv"), (wg, "fWg"), (wo, "fWout")):
                    sp.dma_start(w[:], io[n].rearrange("(c p) n -> p c n", p=P)).then_inc(f_in, 16)
                sp.dma_start(taps[:], io["ftaps"]).then_inc(f_in, 16)
                sp.dma_start(cs[:].rearrange("p a l d -> p (a l d)"), io["cs"].to_broadcast([P, 2 * L * HK // 2])
                             ).then_inc(f_in, 16)
                sp.dma_start(rr[:].rearrange("p a c -> p (a c)"), io["fr"].to_broadcast([P, 2 * C])).then_inc(f_in, 16)
                for t in range(JT):
                    if t:
                        sp.wait_ge(f_r, t)
                    sp.dma_start(gt[:], G_dram[3 * NK:4 * NK].rearrange("k p t -> p k t")[:, :, t * P:t * P + P]
                                 ).then_inc(f_g, 16)
                    sp.wait_ge(f_out, t * NC + NC)
                    sp.dma_start(io["out"].rearrange("k p t -> p k t")[:, :, t * P:t * P + P], xo[:]
                                 ).then_inc(f_st, 16)
                sp.wait_ge(f_st, 16 * JT)

            @block.tensor
            def _(pe):
                pe.wait_ge(f_in, 112)
                with pe.Fori(0, JT) as t:
                    pe.wait_ge(f_xs, t + 1)
                    for l in range(L):
                        for j, w in enumerate((wqk, wv, wg)):
                            use = l * 3 + j
                            pe.wait_ge(f_pf[use % 4], t * 3 + use // 4)
                            for c in range(NC):
                                mm = pe.matmul(ps_p[use % 4][:], xs[:, l * NC + c, :], w[:, c, :],
                                               start=c == 0, stop=c == NC - 1)
                            mm.then_inc(f_p[use % 4], 1)
                    pe.wait_ge(f_o, t + 1)
                    for l in range(L):
                        pe.wait_ge(f_te[l % 2], t * 2 + l // 2)
                        for c in range(NC):
                            mm = pe.transpose(ps_t[l % 2][:, c * P:c * P + P], o[:, l, c * P:c * P + P], ident[:])
                        mm.then_inc(f_t[l % 2], 1)
                    for p in range(2):
                        pe.wait_ge(f_te[p], t * 2 + 2)
                    for m in range(NC):
                        pe.wait_ge(f_wf[m % 2], t * 2 + m // 2)
                        for c in range(NC):
                            mm = pe.matmul(ps_w[m % 2][:], wo[:, c, m * P:m * P + P], oT[:, c, :],
                                           start=c == 0, stop=c == NC - 1)
                        mm.then_inc(f_w[m % 2], 1)

            @block.scalar
            def _(act):
                with act.Fori(0, JT) as t:
                    act.activation(r[:], X[:].rearrange("p (k t) -> p k t", k=NK)[:, :, bass.ds(t * P, P)], ACT.Sigmoid
                                   ).then_inc(f_sig, 1)
                    act.wait_ge(f_cv, t + 1)
                    act.activation(xs[:], cv[:], ACT.Silu).then_inc(f_xs, 1)
                    for l in range(L):
                        for j in range(3):
                            use = l * 3 + j
                            act.wait_ge(f_p[use % 4], t * 3 + use // 4 + 1)
                            ps = ps_p[use % 4]
                            if j == 0:
                                act.activation(qk[:, l, 0:DK], ps[:, 0:DK], ACT.Silu).then_inc(f_sq, 1)
                                ins = act.activation(qk[:, l, DK:], ps[:, DK:], ACT.Copy)
                            elif j == 1:
                                ins = act.activation(v[:, l, :], ps[:], ACT.Copy)
                            else:
                                ins = act.activation(gate[:, l, :], ps[:], ACT.Silu)
                            ins.then_inc(f_pf[use % 4], 1)
                    act.wait_ge(f_d, t * 2 + 1)
                    act.activation(tiny["sc_"][:], tiny["ad"][:], ACT.Sigmoid).then_inc(f_sc, 1)
                    act.wait_ge(f_d, t * 2 + 2)
                    act.activation(vw[:], o[:], ACT.Square).then_inc(f_sc, 1)
                    act.wait_ge(f_var, t + 1)
                    act.activation(tiny["std_"][:], tiny["var_"][:], ACT.Sqrt, bias=eps[:], scale=1.0 / HV
                                   ).then_inc(f_std, 1)
                    for l in range(L):
                        act.wait_ge(f_t[l % 2], t * 2 + l // 2 + 1)
                        act.activation(oT[:, :, l * P:l * P + P], ps_t[l % 2][:].rearrange("p (c t) -> p c t", c=NC),
                                       ACT.Copy).then_inc(f_te[l % 2], 1)

            @block.vector
            def _(dve):
                own = Steps(dve, f_own)
                dve.wait_ge(f_in, 112)
                own(dve.memset(eps[:], EPS))
                own(dve.tensor_tensor(rd[:], rr[:, 1, :], rr[:, 0, :], ALU.subtract))
                own.sync()
                K = {k: x[:] for k, x in tiny.items()}
                with dve.Fori(0, JT) as t:
                    own.enter(t, OWN_F)
                    do = lambda ins: (own(ins), own.sync())
                    dve.wait_ge(f_g, t * 16 + 16)
                    dve.wait_ge(f_sig, t + 1)
                    dve.tensor_tensor(r[:], r[:], gt[:], ALU.mult).then_inc(f_r, 1)
                    dve.wait_ge(f_r, t + 1)
                    for c in range(NC):
                        own(dve.tensor_scalar(cv[:, c::NC, :], r[:, c::NC, :], taps[:, c, 1:2], None, ALU.mult))
                    own.sync()
                    for c in range(NC):
                        own(dve.scalar_tensor_tensor(cv[:, NC + c::NC, :], r[:, c:NK - NC:NC, :], taps[:, c, 0:1],
                                                     cv[:, NC + c::NC, :], ALU.mult, ALU.add))
                    own.sync()
                    dve.tensor_copy(r[:, 0, 0:1], r[:, 0, 0:1]).then_inc(f_cv, 1)
                    for j in range(4):
                        dve.wait_ge(f_pf[j], t * 3 + 3)
                    dve.wait_ge(f_sq, t * L + L)
                    vf, vwf = v[:].rearrange("p l c -> p l c"), vw[:]
                    do(dve.tensor_tensor(vwf, vf, rd[:].rearrange("p (o c) -> p o c", o=1).to_broadcast([P, L, C]),
                                         ALU.mult))
                    do(dve.tensor_reduce(K["dd"], vw[:].rearrange("p l (h d) -> p (l h) d", d=HV), AX.X, ALU.add))
                    own(dve.tensor_scalar(K["sel"], K["dd"], 0.0, None, ALU.is_gt))
                    dve.scalar_tensor_tensor(K["ad"], K["dd"], -1.0, K["dd"], ALU.mult, ALU.max).then_inc(f_d, 1)
                    q4 = qk[:].rearrange("p l (h d) -> p l h d", d=HK)
                    x1, x2 = q4[:, :, :, 0:HK // 2], q4[:, :, :, HK // 2:]
                    cos, sin = (cs[:, a].rearrange("p l (o d) -> p l o d", o=1).to_broadcast([P, L, 2 * HEADS, HK // 2])
                                for a in range(2))
                    own(dve.tensor_tensor(ra[:], x1, cos, ALU.mult))
                    do(dve.tensor_tensor(rb[:], x2, sin, ALU.mult))
                    do(dve.tensor_tensor(rot[:, :, :, 0:HK // 2], ra[:], rb[:], ALU.subtract))
                    own(dve.tensor_tensor(ra[:], x2, cos, ALU.mult))
                    do(dve.tensor_tensor(rb[:], x1, sin, ALU.mult))
                    do(dve.tensor_tensor(rot[:, :, :, HK // 2:], ra[:], rb[:], ALU.add))
                    sel = K["sel"].rearrange("p (l h) -> p l h", l=L)
                    for l in range(L):
                        n = l + 1
                        ql = rot[:, l:l + 1, 0:HEADS, :].rearrange("p o h d -> p o (h d)").to_broadcast([P, n, DK])
                        km = rot[:, 0:n, HEADS:, :].rearrange("p m h d -> p m (h d)")
                        do(dve.tensor_tensor(vw[:, 0:n, 0:DK], km, ql, ALU.mult))
                        own(dve.tensor_reduce(dots[:, l, 0:n, :], vw[:, 0:n, 0:DK].rearrange("p m (h d) -> p m h d", d=HK),
                                              AX.X, ALU.add))
                        do(dve.tensor_tensor(same[:, l, 0:n, :], sel[:, 0:n, :],
                                             sel[:, l:l + 1, :].to_broadcast([P, n, HEADS]), ALU.is_equal))
                        own(dve.tensor_reduce(K["cnt"].rearrange("p (l h) -> p l h", l=L)[:, l, :],
                                              same[:, l, 0:n, :].rearrange("p m h -> p h m"), AX.X, ALU.add))
                        do(dve.tensor_tensor(dots[:, l, 0:n, :], dots[:, l, 0:n, :], same[:, l, 0:n, :], ALU.mult))
                    do(dve.reciprocal(K["rc"], K["cnt"]))
                    dve.wait_ge(f_sc, t * 2 + 1)
                    do(dve.scalar_tensor_tensor(K["fl"], K["sc_"], float(HK) ** -0.5, K["rc"], ALU.mult, ALU.mult))
                    fl = K["fl"].rearrange("p (l h) -> p l h", l=L)
                    for l in range(L):
                        n = l + 1
                        do(dve.tensor_tensor(dots[:, l, 0:n, :], dots[:, l, 0:n, :],
                                             fl[:, l:l + 1, :].to_broadcast([P, n, HEADS]), ALU.mult))
                        do(dve.tensor_tensor(vw[:, 0:n, :].rearrange("p m (h d) -> p m h d", d=HV),
                                             v[:, 0:n, :].rearrange("p m (h d) -> p m h d", d=HV),
                                             dots[:, l, 0:n, :].rearrange("p m (h o) -> p m h o", o=1)
                                             .to_broadcast([P, n, HEADS, HV]), ALU.mult))
                        do(dve.tensor_reduce(o[:, l, :], vw[:, 0:n, :].rearrange("p m c -> p c m"), AX.X, ALU.add))
                    o3 = o[:].rearrange("p l (h d) -> p (l h) d", d=HV)

                    def wide(a):
                        return a.rearrange("p (n o) -> p n o", o=1).to_broadcast([P, L * HEADS, HV])
                    do(dve.tensor_reduce(K["mu"], o3, AX.X, ALU.add))
                    do(dve.tensor_scalar(K["mu"], K["mu"], 1.0 / HV, None, ALU.mult))
                    dve.tensor_tensor(o3, o3, wide(K["mu"]), ALU.subtract).then_inc(f_d, 1)
                    dve.wait_ge(f_sc, t * 2 + 2)
                    dve.tensor_reduce(K["var_"], vw[:].rearrange("p l (h d) -> p (l h) d", d=HV), AX.X, ALU.add
                                      ).then_inc(f_var, 1)
                    dve.wait_ge(f_std, t + 1)
                    do(dve.reciprocal(K["rs"], K["std_"]))
                    do(dve.tensor_tensor(o3, o3, wide(K["rs"]), ALU.mult))
                    dve.tensor_tensor(o[:], o[:], gate[:], ALU.mult).then_inc(f_o, 1)
                    dve.wait_ge(f_st, t * 16)
                    for m in range(NC):
                        dve.wait_ge(f_w[m % 2], t * 2 + m // 2 + 1)
                        dve.tensor_tensor(xo[:, m::NC, :],
                                          X[:].rearrange("p (k t) -> p k t", k=NK)[:, m::NC, bass.ds(t * P, P)],
                                          ps_w[m % 2][:].rearrange("p (l t) -> p l t", l=L), ALU.add)\
                            .then_inc(f_out, 1)
                        dve.wait_ge(f_out, t * NC + m + 1)
                        dve.tensor_copy(tiny["mu"][:, 0:1], tiny["mu"][:, 0:1]).then_inc(f_wf[m % 2], 1)
                    own.leave(JT)


def rotary():
    import numpy as np

    hk = C // 2 // HEADS
    inv = (1.0 / 10000.0 ** (np.arange(0, hk, 2, dtype=np.float32) / hk)).astype(np.float32)
    a = np.arange(NB, dtype=np.float32)[:, None] * inv[None, :]
    return np.stack([np.cos(a), np.sin(a)]).astype(np.float32).reshape(1, -1)


def prepare(inputs):
    import numpy as np

    n = {k: np.asarray(v) for k, v in inputs.items()}

    def tiles(a):
        return np.ascontiguousarray(a.reshape(NB, T, NC, P).transpose(0, 2, 3, 1).reshape(NK, P, T))

    def columns(a):
        return np.ascontiguousarray(a.reshape(-1, P).T)

    names = ["L0_cond", "L0_cond2", "L1_cond", "L1_cond2"]
    return {
        "x": tiles(n["x"]),
        "f": tiles(n["fside_BxSxS_0"]),
        "condT": np.ascontiguousarray(n["cond_512"].T),
        "w": columns(np.stack([n[k + "_w"] for k in names])),
        "u": columns(np.stack([n[k + "_u"] for k in names])),
        "Wq": n["L0_attn_Wq"], "Wk": n["L0_attn_Wk"], "Wv": n["L0_attn_Wv"], "Wo": n["L0_attn_Wo"],
        "bo": columns(n["L0_attn_bo"]),
        "rw": np.ascontiguousarray(np.concatenate([n["L0_ffn_rg_w"].T, n["L0_ffn_ru_w"].T], 1)),
        "ebias": n["L0_ffn_extra_bias"].reshape(1, E), "escale": n["L0_ffn_extra_scale"].reshape(1, E),
        "SgT": np.ascontiguousarray(n["L0_ffn_Sg"].T), "SuT": np.ascontiguousarray(n["L0_ffn_Su"].T),
        "SdT": np.ascontiguousarray(n["L0_ffn_Sd"].T),
        "xprojT": np.ascontiguousarray(n["L1_attn_xproj_w"].T), "dtprojT": np.ascontiguousarray(n["L1_attn_dtproj_w"].T),
        "taps": np.ascontiguousarray(n["L1_attn_conv_w"].reshape(NC, P, 4).transpose(1, 0, 2)),
        "cvec": columns(np.stack([n["L1_attn_conv_b"], n["L1_attn_dtproj_b"], n["L1_attn_D_skip"]])).reshape(P, 3, NC),
        "alog": np.ascontiguousarray(n["L1_attn_A_log"].reshape(NC, P, NS).transpose(1, 0, 2)),
        "Wqk": np.ascontiguousarray(np.concatenate([n["L1_ffn_Wq"], n["L1_ffn_Wk"]], 1)),
        "fWv": n["L1_ffn_Wv"], "fWg": n["L1_ffn_Wg"], "fWout": n["L1_ffn_Wout"],
        "ftaps": np.ascontiguousarray(n["L1_ffn_conv_w"].reshape(NC, P, 2).transpose(1, 0, 2)),
        "fr": np.ascontiguousarray(n["L1_ffn_router_w"].reshape(C, 2).T).reshape(1, 2 * C),
        "cs": rotary(),
        "WgT": np.ascontiguousarray(n["L0_ffn_Wg"].transpose(0, 2, 1)),
        "WuT": np.ascontiguousarray(n["L0_ffn_Wu"].transpose(0, 2, 1)),
        "WdT": np.ascontiguousarray(n["L0_ffn_Wd"].transpose(0, 2, 1)),
    }


def kernel(**inputs):
    import numpy as np
    import concourse.bacc as bacc
    from concourse.bass_utils import run_bass_kernel_spmd as run

    nc = bacc.Bacc("TRN2", target_bir_lowering=False, num_devices=1)
    arrays = prepare(inputs)
    io = {k: nc.dram_tensor("in_" + k, a.shape, mybir.dt.from_np(a.dtype), kind="ExternalInput").ap()
          for k, a in arrays.items()}
    io["out"] = nc.dram_tensor("out", (NK, P, T), F32, kind="ExternalOutput").ap()
    build(nc, io)
    got = run(nc, [{"in_" + k: a for k, a in arrays.items()}], core_ids=[0]).results[0]["out"]
    return np.ascontiguousarray(got.reshape(NB, NC, P, T).transpose(0, 3, 1, 2).reshape(NB, T, C))
```

```python
from contextlib import ExitStack

import concourse.bass as bass
from concourse import mybir

F32 = mybir.dt.float32
I32 = mybir.dt.int32
U32 = mybir.dt.uint32
BF16 = mybir.dt.bfloat16
ALU = mybir.AluOpType
ACT = mybir.ActivationFunctionType
AX = mybir.AxisListType

P = 128
NB = 4
T = 512
C = 512
NC = C // P
NT = T // P
NK = NB * NC
NLAYER = 4
HEADS = 16
DH = C // HEADS
HG = P // DH
MASKED = -1.0e30
NS = 16
DTR = 128
EPS = 1e-5
E = 16
TOPK = 4
I = 352
ISH = 704
NTOK = NB * T
TT = NTOK // P
NBLK = NTOK * TOPK // P + E
WBUF = 3
ZB = 5
FIRST = NC
BESIDE = 8
LATER = NLAYER * NK - FIRST - NB * BESIDE


class Steps:

    def __init__(self, eng, sem):
        self.eng, self.sem, self.base, self.n = eng, sem, 0, 0

    def __call__(self, ins):
        ins.then_inc(self.sem, 1)
        self.n += 1
        return ins

    def sync(self):
        self.eng.wait_ge(self.sem, self.base + self.n)

    def enter(self, i, per_iteration):
        self.outer = (self.base, self.n, per_iteration)
        self.base, self.n = self.base + self.n + i * per_iteration, 0

    def leave(self, iterations):
        base, n, per = self.outer
        assert self.n == per, (self.n, per)
        self.base, self.n = base, n + per * iterations


def build(nc, io):
    ctx = ExitStack()
    with ctx:
        def sem(name):
            return ctx.enter_context(nc.semaphore(name))

        def sb(name, shape, dt=F32, stack=None):
            return (stack or ctx).enter_context(nc.sbuf_tensor(name, shape, dt))

        def pair(name):
            return [sem(f"{name}0"), sem(f"{name}1")]

        def recycle(stack, held):
            with nc.Block() as block:
                @block.sync
                def _(sp):
                    for s in held:
                        sp.sem_clear(s)
            stack.close()

        X = sb("X", [P, NK * T])
        ident = sb("ident", [P, P])
        par = sb("par", [P, NLAYER * NK, 3])
        psum = [ctx.enter_context(nc.psum_tensor(f"bank{i}", [P, T], F32)) for i in range(8)]
        Xe = nc.dram_tensor("Xe_scratch", [NBLK * P, C], F32, kind="Internal").ap()
        Ye = nc.dram_tensor("Ye_scratch", [NBLK * P, C], F32, kind="Internal").ap()
        G_dram = nc.dram_tensor("G_scratch", [NLAYER * NK, P, T], F32, kind="Internal").ap()

        wk_load = pair("wk_load")
        wk_min = pair("wk_min")
        wk_exp = pair("wk_exp")
        wk_euv = pair("wk_euv")
        wk_out = pair("wk_out")
        wk_store = pair("wk_store")
        wk_own = sem("wk_own")
        W = [{}, {}]

        def wkv_buffers(stack, phase):
            for s in range(2):
                for n in ["f", "fm", "um", "ek", "eu", "ekv", "nf", "nb", "df", "db", "p", "g"]:
                    W[s][n] = sb(f"wk{phase}_{n}{s}", [P, T], stack=stack)
                W[s]["par"] = sb(f"wk{phase}_par{s}", [P, 3], stack=stack)

        def wkv_load(sp, m, s, k):
            sp.wait_ge(wk_out[s], m)
            sp.dma_start(W[s]["f"][:], io["f"][bass.ds(k, 1)].rearrange("a p t -> p (a t)")
                         ).then_inc(wk_load[s], 16)

        def wkv_store(sp, m, s, lk):
            sp.wait_ge(wk_out[s], m + 1)
            sp.dma_start(G_dram[bass.ds(lk, 1)].rearrange("a p t -> p (a t)"), W[s]["g"][:]
                         ).then_inc(wk_store[s], 16)

        def wkv_scalar(act, m, s):
            w = W[s]
            act.wait_ge(wk_min[s], 2 * m + 2)
            act.activation(w["ek"][:], w["fm"][:], ACT.Exp).then_inc(wk_exp[s], 1)
            act.activation(w["eu"][:], w["um"][:], ACT.Exp).then_inc(wk_exp[s], 1)

        def wkv_gpsimd(pool, m, s):
            w = W[s]
            pool.wait_ge(wk_exp[s], 2 * m + 2)
            pool.tensor_tensor(w["p"][:], w["eu"][:], w["f"][:], ALU.mult).then_inc(wk_euv[s], 1)

        WKV_STEPS = 14

        def wkv_vector(dve, m, s, lk, own, euv_here=False):
            w = W[s]
            own.sync()
            own(dve.tensor_copy(w["par"][:], par[:].rearrange("p a b -> p (a b)")[:, bass.ds(lk * 3, 3)]))
            decay, u, scale = (w["par"][:, j:j + 1] for j in range(3))
            yield
            dve.wait_ge(wk_load[s], 16 * m + 16)
            dve.tensor_scalar(w["fm"][:], w["f"][:], 30.0, None, ALU.min).then_inc(wk_min[s], 1)
            own.sync()
            dve.tensor_scalar(w["um"][:], w["f"][:], u, 30.0, ALU.add, ALU.min).then_inc(wk_min[s], 1)
            yield
            dve.wait_ge(wk_exp[s], 2 * m + 1)
            own(dve.tensor_tensor(w["ekv"][:], w["ek"][:], w["f"][:], ALU.mult))
            d = decay.to_broadcast([P, T])
            yield
            own(dve.tensor_tensor_scan(w["df"][:], d, w["ek"][:], 0.0, ALU.mult, ALU.add))
            yield
            own(dve.tensor_tensor_scan(w["db"][:, ::-1], d, w["ek"][:, ::-1], 0.0, ALU.mult, ALU.add))
            yield
            own.sync()
            own(dve.tensor_tensor_scan(w["nf"][:], d, w["ekv"][:], 0.0, ALU.mult, ALU.add))
            yield
            own(dve.tensor_tensor_scan(w["nb"][:, ::-1], d, w["ekv"][:, ::-1], 0.0, ALU.mult, ALU.add))
            yield
            own.sync()
            own(dve.scalar_tensor_tensor(w["df"][:, 0:T - 1], w["db"][:, 1:T], decay, w["df"][:, 0:T - 1],
                                         ALU.mult, ALU.add))
            yield
            own(dve.scalar_tensor_tensor(w["nf"][:, 0:T - 1], w["nb"][:, 1:T], decay, w["nf"][:, 0:T - 1],
                                         ALU.mult, ALU.add))
            dve.wait_ge(wk_exp[s], 2 * m + 2)
            yield
            if euv_here:
                own(dve.tensor_tensor(w["p"][:], w["eu"][:], w["f"][:], ALU.mult))
            own.sync()
            own(dve.tensor_tensor(w["df"][:], w["df"][:], w["eu"][:], ALU.add))
            yield
            own.sync()
            own(dve.tensor_scalar(w["df"][:], w["df"][:], 1e-8, None, ALU.max))
            yield
            if not euv_here:
                dve.wait_ge(wk_euv[s], m + 1)
            own(dve.tensor_tensor(w["nf"][:], w["nf"][:], w["p"][:], ALU.add))
            yield
            own.sync()
            own(dve.reciprocal(w["db"][:], w["df"][:]))
            yield
            own.sync()
            dve.wait_ge(wk_store[s], 16 * m)
            dve.scalar_tensor_tensor(w["g"][:], w["nf"][:], scale, w["db"][:], ALU.mult, ALU.mult
                                     ).then_inc(wk_out[s], 1)
            yield

        WKV_OWN = 12

        c_in = sem("c_in")
        c_x = sem("c_x")
        c_pool = sem("c_pool")
        c_act = sem("c_act")
        c_dve = sem("c_dve")
        c_pe = sem("c_pe")
        with ExitStack() as st:
            wkv_buffers(st, "c")
            wst = sb("wst", [P, NLAYER * NC], stack=st)
            ust = sb("ust", [P, NLAYER * NC], stack=st)
            condT = sb("condT", [P, NB], stack=st)
            ones = sb("ones", [P, P], stack=st)
            ew = sb("ew", [P, NLAYER * NC], stack=st)
            dcy = sb("dcy", [P, NLAYER * NC], stack=st)
            tf = sb("tf", [P, NB], stack=st)
            tfh = sb("tfh", [P, NB], stack=st)
            tfs = sb("tfs", [P, NB], stack=st)
            par5 = par[:].rearrange("p (l b c) f -> p l b c f", l=NLAYER, b=NB)
            with nc.Block() as block:
                @block.sync
                def _(sp):
                    sp.dma_start(wst[:], io["w"]).then_inc(c_in, 16)
                    sp.dma_start(ust[:], io["u"]).then_inc(c_in, 16)
                    sp.dma_start(condT[:], io["condT"]).then_inc(c_in, 16)
                    for s in range(2):
                        wkv_load(sp, 0, s, s)
                    for b in range(NB):
                        sp.dma_start(X[:, b * NC * T:(b + 1) * NC * T].rearrange("p (k t) -> p k t", k=NC),
                                     io["x"][b * NC:b * NC + NC].rearrange("k p t -> p k t")).then_inc(c_x, 16)
                        if b == 0:
                            for s in range(2):
                                wkv_store(sp, 0, s, s)
                                wkv_load(sp, 1, s, 2 + s)
                    for s in range(2):
                        wkv_store(sp, 1, s, 2 + s)
                    sp.wait_ge(c_x, 16 * NB)
                    for s in range(2):
                        sp.wait_ge(wk_store[s], 16 * 2)

                @block.gpsimd
                def _(pool):
                    pool.memset(ones[:], 1.0).then_inc(c_pool, 1)
                    pool.memset(ident[:], 0.0).then_inc(c_pool, 1)
                    pool.wait_ge(c_pool, 2)
                    pool.affine_select(out=ident[:], in_=ident[:], compare_op=ALU.not_equal, fill=1.0, base=0,
                                       pattern=[[-1, P]], channel_multiplier=1).then_inc(c_pool, 1)
                    with pool.Fori(0, FIRST // 2) as i:
                        for s in range(2):
                            wkv_gpsimd(pool, i, s)

                @block.tensor
                def _(pe):
                    pe.wait_ge(c_pool, 1)
                    pe.wait_ge(c_in, 48)
                    pe.matmul(psum[0][:, 0:NB], ones[:], condT[:], start=True, stop=True).then_inc(c_pe, 1)

                @block.scalar
                def _(act):
                    act.wait_ge(c_pe, 1)
                    act.activation(tf[:], psum[0][:, 0:NB], ACT.Sigmoid).then_inc(c_act, 1)
                    act.activation(ew[:], wst[:], ACT.Exp).then_inc(c_act, 1)
                    act.wait_ge(c_act, 2)
                    act.activation(dcy[:], ew[:], ACT.Exp, scale=-1.0).then_inc(c_act, 1)
                    with act.Fori(0, FIRST // 2) as i:
                        for s in range(2):
                            wkv_scalar(act, i, s)

                @block.vector
                def _(dve):
                    own = Steps(dve, c_dve)
                    dve.wait_ge(c_act, 3)
                    dve.wait_ge(c_in, 48)
                    own(dve.tensor_scalar(tfh[:], tf[:], 0.5, 0.5, ALU.mult, ALU.add))
                    own(dve.tensor_scalar(tfs[:], tf[:], 0.2, 0.8, ALU.mult, ALU.add))
                    own.sync()
                    view = [x[:].rearrange("p (l c) -> p l c", l=NLAYER) for x in (dcy, ust)]
                    for b in range(NB):
                        own(dve.tensor_scalar(par5[:, :, b, :, 0], view[0], tfh[:, b:b + 1], None, ALU.mult))
                        own(dve.tensor_copy(par5[:, :, b, :, 1], view[1]))
                        own(dve.tensor_scalar(par5[:, :, b, :, 2], view[0], 0.0, tfs[:, b:b + 1], ALU.mult, ALU.add))
                    own.sync()
                    wk = Steps(dve, wk_own)
                    with dve.Fori(0, FIRST // 2) as i:
                        wk.enter(i, 2 * WKV_OWN)
                        for s in range(2):
                            for _ in wkv_vector(dve, i, s, i * 2 + s, wk):
                                pass
                        wk.leave(FIRST // 2)

        stage, held = ExitStack(), []

        def stage_sem(name):
            held.append(stage.enter_context(nc.semaphore(name)))
            return held[-1]
        attention(nc, io, {**locals(), "sem": stage_sem, "pair": lambda n: [stage_sem(n + "0"), stage_sem(n + "1")]})
        recycle(stage, held)
        experts(nc, io, locals())
        state_space(nc, io, locals())
        linear_attention(nc, io, locals())


def attention(nc, io, g):
    sb, sem, pair, X, ident, psum, G_dram = (g[k] for k in ("sb", "sem", "pair", "X", "ident", "psum", "G_dram"))
    wk_own = g["wk_own"]
    ps_s, ps_t, ps_p, ps_c = psum[0:2], psum[2:4], psum[4:6], psum[6:8]
    STEPS = HEADS * NT
    HALF = STEPS // 2
    NZ = NBLK // ZB // NB
    PACE = STEPS // BESIDE
    with ExitStack() as st:
        g["wkv_buffers"](st, "a")
        zeros = sb("zeros", [P, C], stack=st)
        a_z = sem("a_z")
        wq, wk, wv, wo = (sb(f"at_w{n}", [P, NC, C], stack=st) for n in "qkvo")
        bo = sb("bo", [P, NC], stack=st)
        mask = sb("mask", [P, P], stack=st)
        gt = sb("gt", [P, NC * T], stack=st)
        r = sb("at_r", [P, NC, T], stack=st)
        qT = [sb(f"qT{s}", [P, T], stack=st) for s in range(2)]
        kT = [sb(f"kT{s}", [P, T], stack=st) for s in range(2)]
        v = sb("v", [P, NT, C], stack=st)
        prob = [sb(f"prob{s}", [P, T], stack=st) for s in range(2)]
        probT = [sb(f"probT{s}", [P, NT, T], stack=st) for s in range(2)]
        cT = sb("cT", [P, NC, T], stack=st)
        nmax = [sb(f"nmax{s}", [P, 1], stack=st) for s in range(2)]
        rsum = [sb(f"rsum{s}", [P, 1], stack=st) for s in range(2)]
        rinv = [sb(f"rinv{s}", [P, 1], stack=st) for s in range(2)]
        a_w = sem("a_w")
        a_mask = sem("a_mask")
        a_g = sem("a_g")
        a_sig = sem("a_sig")
        a_r = sem("a_r")
        a_pr = pair("a_pr")
        a_pf = pair("a_pf")
        a_s = pair("a_s")
        a_nm = pair("a_nm")
        a_exp = pair("a_exp")
        a_ri = pair("a_ri")
        a_pn = pair("a_pn")
        a_t = pair("a_t")
        a_te = pair("a_te")
        a_pv = sem("a_pv")
        a_c = pair("a_c")
        a_x = sem("a_x")
        use_v, use_q, use_k, use_o = [0, 1, 2, 3], [4, 6, 8, 10], [5, 7, 9, 11], [12, 13, 14, 15]
        with nc.Block() as block:
            @block.sync
            def _(sp):
                for w, n in ((wv, "Wv"), (wq, "Wq"), (wk, "Wk"), (wo, "Wo")):
                    sp.dma_start(w[:], io[n].rearrange("(c p) n -> p c n", p=P)).then_inc(a_w, 16)
                sp.dma_start(bo[:], io["bo"]).then_inc(a_w, 16)
                def load_g(k):
                    sp.dma_start(gt[:].rearrange("p (c t) -> p c t", c=NC),
                                 G_dram[bass.ds(k, NC)].rearrange("c p t -> p c t")).then_inc(a_g, 16)
                load_g(0)
                sp.wait_ge(a_mask, 3)
                for b in range(NB):
                    first, m = FIRST + b * BESIDE, (FIRST + b * BESIDE) // 2
                    for n in range(b * NZ, b * NZ + NZ):
                        sp.dma_start(g["Xe"][n * ZB * P:(n + 1) * ZB * P].rearrange("(a p) d -> p a d", p=P),
                                     zeros[:].rearrange("p (a d) -> p a d", a=1).to_broadcast([P, ZB, C])
                                     ).then_inc(a_z, 16)
                    for j in range(2):
                        g["wkv_load"](sp, m, j, (first + j) % NK)
                    for j in range(BESIDE):
                        g["wkv_store"](sp, m + j // 2, j % 2, first + j)
                        if j + 2 < BESIDE:
                            g["wkv_load"](sp, m + j // 2 + 1, j % 2, (first + j + 2) % NK)
                        if j == NC and b + 1 < NB:
                            for p in range(2):
                                sp.wait_ge(g["wk_store"][p], 16 * (m + 2))
                            sp.wait_ge(a_r, b + 1)
                            load_g((b + 1) * NC)
                sp.wait_ge(a_z, 16 * (NBLK // ZB))
                for s in range(2):
                    sp.wait_ge(g["wk_store"][s], 16 * (FIRST + NB * BESIDE) // 2)

            @block.gpsimd
            def _(pool):
                pool.memset(mask[:], 0.0).then_inc(a_mask, 1)
                pool.memset(zeros[:], 0.0).then_inc(a_mask, 1)
                pool.wait_ge(a_mask, 2)
                pool.affine_select(out=mask[:], in_=mask[:], compare_op=ALU.is_ge, fill=MASKED, base=0,
                                   pattern=[[-1, P]], channel_multiplier=1).then_inc(a_mask, 1)
                with pool.Fori(0, NB) as b:
                    for j in range(BESIDE):
                        g["wkv_gpsimd"](pool, FIRST // 2 + b * (BESIDE // 2) + j // 2, j % 2)

            @block.tensor
            def _(pe):
                def project(b, use, lhs, rhs):
                    p = use % 2
                    pe.wait_ge(a_pf[p], b * 8 + use // 2)
                    for c in range(NC):
                        mm = pe.matmul(ps_p[p][:], lhs(c), rhs(c), start=c == 0, stop=c == NC - 1)
                    mm.then_inc(a_pr[p], 1)

                def project_qk(b, hg):
                    cols = slice(hg * P, hg * P + P)
                    project(b, use_q[hg], lambda c: wq[:, c, cols], lambda c: r[:, c, :])
                    project(b, use_k[hg], lambda c: wk[:, c, cols], lambda c: r[:, c, :])

                def scores(b, s):
                    hg, hh, qt, p = s // 16, s // 4 % 4, s % 4, s % 2
                    if s % 16 == 0:
                        pe.wait_ge(a_pf[0], b * 8 + use_q[hg] // 2 + 1)
                        pe.wait_ge(a_pf[1], b * 8 + use_k[hg] // 2 + 1)
                    pe.wait_ge(a_exp[p], b * HALF + s // 2)
                    rows, n = slice(hh * DH, hh * DH + DH), (qt + 1) * P
                    pe.matmul(ps_s[p][:, 0:n], qT[hg % 2][rows, qt * P:n], kT[hg % 2][rows, 0:n],
                              start=True, stop=True)
                    pe.matmul(ps_s[p][:, qt * P:n], ident[:], mask[:], start=False, stop=True,
                              skip_group_check=True).then_inc(a_s[p], 1)

                def transposes(b, s):
                    p, qt = s % 2, s % 4
                    pe.wait_ge(a_pn[p], b * HALF + s // 2 + 1)
                    pe.wait_ge(a_te[p], b * HALF + s // 2)
                    for kb in range(qt + 1):
                        mm = pe.transpose(ps_t[p][:, kb * P:kb * P + P], prob[p][:, kb * P:kb * P + P], ident[:])
                    mm.then_inc(a_t[p], 1)

                def context(b, h):
                    hg, hh = h // HG, h % HG
                    last = 4 * h + 3
                    pe.wait_ge(a_te[0], b * HALF + last // 2 + 1)
                    pe.wait_ge(a_te[1], b * HALF + last // 2 + 1)
                    if hh == 0:
                        pe.wait_ge(a_c[hg % 2], b * 2 + hg // 2)
                    for kb in range(NT):
                        mm = pe.matmul(ps_c[hg % 2][hh * DH:hh * DH + DH, kb * P:T],
                                       v[:, kb, h * DH:h * DH + DH], probT[h % 2][:, kb, kb * P:T],
                                       start=kb == 0, stop=kb == NT - 1, skip_group_check=True)
                    mm.then_inc(a_pv, 1)

                pe.wait_ge(a_w, 16 * 5)
                pe.wait_ge(a_mask, 3)
                with pe.Fori(0, NB) as b:
                    pe.wait_ge(a_r, b + 1)
                    for tt in range(NT):
                        project(b, use_v[tt], lambda c: r[:, c, tt * P:tt * P + P], lambda c: wv[:, c, :])
                    project_qk(b, 0)
                    for s in range(STEPS + 3):
                        if s < STEPS:
                            scores(b, s)
                        if s >= 6 and s % 4 == 2:
                            context(b, (s - 6) // 4)
                        if 2 <= s < STEPS + 2:
                            transposes(b, s - 2)
                        if s % 16 == 8 and s // 16 + 1 < NC:
                            project_qk(b, s // 16 + 1)
                    for p in range(2):
                        pe.wait_ge(a_c[p], b * 2 + 2)
                    for m in range(NC):
                        project(b, use_o[m], lambda c: wo[:, c, m * P:m * P + P], lambda c: cT[:, c, :])

            @block.scalar
            def _(act):
                def evict(b, use, out, scale=1.0):
                    act.wait_ge(a_pr[use % 2], b * 8 + use // 2 + 1)
                    act.activation(out, ps_p[use % 2][:], ACT.Copy, scale=scale).then_inc(a_pf[use % 2], 1)

                def evict_qk(b, hg):
                    evict(b, use_q[hg], qT[hg % 2][:], float(DH) ** -0.5)
                    evict(b, use_k[hg], kT[hg % 2][:])

                with act.Fori(0, NB) as b:
                    act.activation(r[:].rearrange("p c t -> p (c t)"), X[:, bass.ds(b * NC * T, NC * T)], ACT.Sigmoid
                                   ).then_inc(a_sig, 1)
                    for tt in range(NT):
                        evict(b, use_v[tt], v[:, tt, :])
                    evict_qk(b, 0)
                    for s in range(STEPS + 3):
                        if s < STEPS:
                            p, n = s % 2, (s % NT + 1) * P
                            act.wait_ge(a_nm[p], b * HALF + s // 2 + 1)
                            act.wait_ge(a_t[p], b * HALF + s // 2)
                            act.activation(prob[p][:, 0:n], ps_s[p][:, 0:n], ACT.Exp, bias=nmax[p][:],
                                           accum_out=rsum[p][:]).then_inc(a_exp[p], 1)
                        if s % PACE == 1 and s < STEPS:
                            j = s // PACE
                            g["wkv_scalar"](act, FIRST // 2 + b * (BESIDE // 2) + j // 2, j % 2)
                        if s % 16 == 8 and s // 16 + 1 < NC:
                            evict_qk(b, s // 16 + 1)
                        if s >= 18 and s % 16 == 2:
                            hg = (s - 18) // 16
                            act.wait_ge(a_pv, b * HEADS + hg * HG + HG)
                            act.activation(cT[:, hg, :], ps_c[hg % 2][:], ACT.Copy).then_inc(a_c[hg % 2], 1)

            @block.vector
            def _(dve):
                own = Steps(dve, wk_own)
                own.n = FIRST * g["WKV_OWN"]
                dve.wait_ge(a_w, 16 * 5)
                with dve.Fori(0, NB) as b:
                    own.enter(b, BESIDE * g["WKV_OWN"])
                    dve.wait_ge(a_g, b * 16 + 16)
                    dve.wait_ge(a_sig, b + 1)
                    dve.tensor_tensor(r[:].rearrange("p c t -> p (c t)"), r[:].rearrange("p c t -> p (c t)"), gt[:],
                                      ALU.mult).then_inc(a_r, 1)
                    for s in range(STEPS + 2):
                        if s < STEPS:
                            p, n = s % 2, (s % NT + 1) * P
                            dve.wait_ge(a_s[p], b * HALF + s // 2 + 1)
                            dve.tensor_reduce(nmax[p][:], ps_s[p][:, 0:n], AX.X, ALU.max, negate=True
                                              ).then_inc(a_nm[p], 1)
                        if 1 <= s <= STEPS:
                            p = (s - 1) % 2
                            dve.wait_ge(a_exp[p], b * HALF + (s - 1) // 2 + 1)
                            dve.reciprocal(rinv[p][:], rsum[p][:]).then_inc(a_ri[p], 1)
                            n = ((s - 1) % NT + 1) * P
                            dve.wait_ge(a_ri[p], b * HALF + (s - 1) // 2 + 1)
                            dve.tensor_scalar(prob[p][:, 0:n], prob[p][:, 0:n], rinv[p][:], None, ALU.mult
                                              ).then_inc(a_pn[p], 1)
                        if s >= 2:
                            q = s - 2
                            p, h, qt = q % 2, q // 4, q % 4
                            if qt == 0:
                                dve.wait_ge(a_pv, b * HEADS + max(h - 1, 0))
                            dve.wait_ge(a_t[p], b * HALF + q // 2 + 1)
                            dve.tensor_copy(probT[h % 2][:, 0:qt + 1, qt * P:qt * P + P],
                                            ps_t[p][:, 0:(qt + 1) * P].rearrange("p (k q) -> p k q", q=P)
                                            ).then_inc(a_te[p], 1)
                        if s < STEPS:
                            if s % PACE == 0:
                                j = s // PACE
                                tile = g["wkv_vector"](dve, FIRST // 2 + b * (BESIDE // 2) + j // 2, j % 2,
                                                       FIRST + b * BESIDE + j, own)
                            if s % PACE != 1:
                                next(tile)
                                next(tile)
                    for m in range(NC):
                        use = use_o[m]
                        dve.wait_ge(a_pr[use % 2], b * 8 + use // 2 + 1)
                        xk = X[:, bass.ds((b * NC + m) * T, T)]
                        dve.scalar_tensor_tensor(xk, ps_p[use % 2][:], bo[:, m:m + 1], xk, ALU.add, ALU.add
                                                 ).then_inc(a_pf[use % 2], 1)
                    own.leave(NB)


def experts(nc, io, g):
    sb, sem, pair, X, ident, psum, G_dram = (g[k] for k in ("sb", "sem", "pair", "X", "ident", "psum", "G_dram"))
    Xe, Ye = g["Xe"], g["Ye"]
    SJ = [(0, 128), (128, 128), (256, 128), (384, 128), (512, 96), (608, 96)]
    NSJ = len(SJ)
    with ExitStack() as keep:
        posk = sb("posk", [P, TT, TOPK], U32, stack=keep)
        wkk = sb("wkk", [P, TT, TOPK], stack=keep)
        endm = sb("endm", [P, E + WBUF], I32, stack=keep)
        slot = sb("slot", [P, NBLK], I32, stack=keep)
        wload = sb("wload", [P, NBLK], I32, stack=keep)
        m_in = sem("m_in")
        m_sh = sem("m_sh")
        m_g = sem("m_g")
        m_sig = sem("m_sig")
        m_r = sem("m_r")
        m_t = pair("m_t")
        m_te = pair("m_te")
        m_lg = sem("m_lg")
        m_c = sem("m_c")
        m_act = sem("m_act")
        m_d = sem("m_d")
        m_M = sem("m_M")
        m_pre = sem("m_pre")
        m_pos = sem("m_pos")
        m_sc = sem("m_sc")
        s_gu, s_sl, s_h, s_y, s_yf = (pair(n) for n in ("s_gu", "s_sl", "s_h", "s_y", "s_yf"))
        s_hall = sem("s_hall")
        with ExitStack() as st:
            R = sb("m_R", [P, NK, T], stack=st)
            rtok = sb("rtok", [P, TT, C], stack=st)
            gt = sb("m_gt", [P, NC * T], stack=st)
            rw = sb("rw", [P, NC, 2 * E], stack=st)
            ebias = sb("ebias", [P, E], stack=st)
            escale = sb("escale", [P, E], stack=st)
            sg = sb("sg", [P, NC, ISH], stack=st)
            su = sb("su", [P, NC, ISH], stack=st)
            sd = sb("sd", [P, NSJ, C], stack=st)
            ssl = [sb(f"ssl{s}", [P, T], stack=st) for s in range(2)]
            suu = [sb(f"suu{s}", [P, T], stack=st) for s in range(2)]
            hsh = sb("hsh", [P, NSJ, T], stack=st)
            before = sb("before", [P, P], stack=st)
            ones = sb("m_ones", [P, P], stack=st)
            lower = sb("lower", [P, E, E], stack=st)
            fresh = sb("fresh", [P, E, TT], stack=st)
            blk = sb("blk", [P, NBLK], stack=st)
            big = [sb(f"big{j}", [P, TT, E, E], BF16, stack=st) for j in range(2)]
            small = {n: sb(f"rt_{n}", [P, TT, E], stack=st) for n in
                     ("sl", "s", "ex", "pr", "bi", "rank", "M", "Wt", "tot", "inc", "pos", "t0", "t1")}
            row = {n: sb(f"rr_{n}", [P, E], stack=st) for n in ("nb", "end", "base", "c")}
            rowi = sb("rowi", [P, E], I32, stack=st)
            rt1 = {n: sb(f"r1_{n}", [P, TT], stack=st) for n in ("m", "sum", "ri")}
            ebc = sb("ebc", [P, NBLK, E], BF16, stack=st)
            ej = sb("ej", [P, NBLK], stack=st)
            eji = sb("eji", [P, NBLK], I32, stack=st)
            third = sb("third", [P, NBLK], I32, stack=st)
            ps_t, ps_l, ps_pre = psum[0:2], psum[2], psum[3]
            ps_g, ps_u, ps_y = psum[4:6], psum[6:8], psum[0:2]
            with nc.Block() as block:
                @block.sync
                def _(sp):
                    sp.dma_start(rw[:], io["rw"].rearrange("(c p) e -> p c e", p=P)).then_inc(m_in, 16)
                    sp.dma_start(ebias[:], io["ebias"].to_broadcast([P, E])).then_inc(m_in, 16)
                    sp.dma_start(escale[:], io["escale"].to_broadcast([P, E])).then_inc(m_in, 16)
                    for b in range(NB):
                        if b:
                            sp.wait_ge(m_r, b)
                        sp.dma_start(gt[:].rearrange("p (c t) -> p c t", c=NC),
                                     G_dram[NK + b * NC:NK + b * NC + NC].rearrange("c p t -> p c t")
                                     ).then_inc(m_g, 16)
                    sp.dma_start(sg[:], io["SgT"].rearrange("(c p) n -> p c n", p=P)).then_inc(m_sh, 16)
                    sp.dma_start(su[:], io["SuT"].rearrange("(c p) n -> p c n", p=P)).then_inc(m_sh, 16)
                    sp.dma_start(sd[:, 0:4, :], io["SdT"][0:4 * P].rearrange("(c p) n -> p c n", p=P)
                                 ).then_inc(m_sh, 16)
                    sp.dma_start(sd[0:96, 4:6, :], io["SdT"][4 * P:ISH].rearrange("(c p) n -> p c n", p=96)
                                 ).then_inc(m_sh, 16)

                @block.gpsimd
                def _(pool):
                    pool.memset(before[:], 1.0).then_inc(m_c, 1)
                    pool.memset(ones[:], 1.0).then_inc(m_c, 1)
                    pool.memset(lower[:], 1.0).then_inc(m_c, 1)
                    pool.memset(fresh[:], 1.0).then_inc(m_c, 1)
                    pool.memset(endm[:], 0).then_inc(m_c, 1)
                    pool.iota(blk[:], pattern=[[1, NBLK]], base=0, channel_multiplier=0,
                              allow_small_or_imprecise_dtypes=True).then_inc(m_c, 1)
                    pool.wait_ge(m_c, 6)
                    pool.affine_select(out=before[:], in_=before[:], compare_op=ALU.is_gt, fill=0.0, base=0,
                                       pattern=[[1, P]], channel_multiplier=-1).then_inc(m_c, 1)
                    pool.affine_select(out=lower[:], in_=lower[:], compare_op=ALU.is_gt, fill=0.0, base=0,
                                       pattern=[[1, E], [-1, E]], channel_multiplier=0).then_inc(m_c, 1)
                    pool.affine_select(out=fresh[:], in_=fresh[:], compare_op=ALU.is_gt, fill=0.0, base=0,
                                       pattern=[[0, E], [1, TT]], channel_multiplier=0).then_inc(m_c, 1)

                    def shared(b, base, first):
                        for j in range(NSJ):
                            m, (_, n) = base + j // 2, SJ[j]
                            pool.wait_ge(s_sl[j % 2], 2 * m + 2)
                            if j == 0:
                                pool.wait_ge(m_c, 9)
                            pool.tensor_tensor(hsh[0:n, j, :], ssl[j % 2][0:n, :], suu[j % 2][0:n, :], ALU.mult
                                               ).then_inc(s_h[j % 2], 1)
                    with pool.Fori(0, NB // 2) as b:
                        shared(b, b * (NSJ // 2), None)
                    pool.wait_ge(m_pos, 1)
                    for p in range(2):
                        pool.wait_ge(m_te[p], TT // 2)
                    for t in range(TT):
                        for k in range(TOPK):
                            pool.indirect_dma_start(
                                out=Xe, out_offset=bass.IndirectOffsetOnAxis(ap=posk[:, t, k:k + 1], axis=0),
                                in_=rtok[:, t, :], in_offset=None, bounds_check=NBLK * P - 1, oob_is_err=False
                            ).then_inc(m_sc, 16)
                    pool.wait_ge(m_sc, 16 * TT * TOPK)

                @block.tensor
                def _(pe):
                    pe.wait_ge(m_in, 48)
                    for t in range(TT):
                        b, tt, p = t // NT, t % NT, t % 2
                        cols = slice(tt * P, tt * P + P)
                        pe.wait_ge(m_r, b + 1)
                        if t >= 2:
                            pe.wait_ge(m_te[p], t // 2)
                        for c in range(NC):
                            mm = pe.transpose(ps_t[p][:, c * P:c * P + P], R[:, b * NC + c, cols], ident[:])
                        mm.then_inc(m_t[p], 1)
                        for c in range(NC):
                            mm = pe.matmul(ps_l[:, t * 2 * E:(t + 1) * 2 * E], R[:, b * NC + c, cols], rw[:, c, :],
                                           start=c == 0, stop=c == NC - 1)
                    mm.then_inc(m_lg, 1)

                    def shared(b, base):
                        for j, (at, n) in enumerate(SJ):
                            p, m = j % 2, base + j // 2
                            pe.wait_ge(s_h[p], m)
                            for ps, w in ((ps_g[p], sg), (ps_u[p], su)):
                                for c in range(NC):
                                    mm = pe.matmul(ps[0:n, :], w[:, c, at:at + n], rview(b, c),
                                                   start=c == 0, stop=c == NC - 1)
                            mm.then_inc(s_gu[p], 1)
                        for p in range(2):
                            pe.wait_ge(s_h[p], base + NSJ // 2)
                        for c in range(NC):
                            p = c % 2
                            pe.wait_ge(s_yf[p], b * 2 + c // 2)
                            for j, (at, n) in enumerate(SJ):
                                mm = pe.matmul(ps_y[p][:], sd[0:n, j, c * P:c * P + P], hsh[0:n, j, :],
                                               start=j == 0, stop=j == NSJ - 1)
                            mm.then_inc(s_y[p], 1)

                    def rview(b, c):
                        return R[:].rearrange("p k t -> p (k t)")[:, bass.ds((b * NC + c) * T, T)]

                    pe.wait_ge(m_te[0], TT // 2)
                    pe.wait_ge(m_te[1], TT // 2)
                    pe.wait_ge(m_sh, 64)
                    shared(0, 0)
                    pe.wait_ge(m_M, 1)
                    pe.wait_ge(m_c, 9)
                    M = small["M"][:].rearrange("p t e -> p (t e)")
                    pe.matmul(ps_pre[:, 0:TT * E], before[:], M, start=True, stop=True)
                    pe.matmul(ps_pre[:, TT * E:2 * TT * E], ones[:], M, start=True, stop=True).then_inc(m_pre, 1)
                    with pe.Fori(1, NB) as b:
                        shared(b, b * (NSJ // 2))

                @block.scalar
                def _(act):
                    for b in range(NB):
                        xb = R[:].rearrange("p k t -> p (k t)")[:, b * NC * T:(b + 1) * NC * T]
                        act.activation(xb, X[:, b * NC * T:(b + 1) * NC * T], ACT.Sigmoid).then_inc(m_sig, 1)
                    for t in range(TT):
                        p = t % 2
                        act.wait_ge(m_t[p], t // 2 + 1)
                        act.activation(rtok[:, t, :], ps_t[p][:], ACT.Copy).then_inc(m_te[p], 1)
                    act.wait_ge(m_lg, 1)
                    act.activation(small["sl"][:], ps_l[:].rearrange("p (t e) -> p t e", t=TT)[:, :, 0:E], ACT.Silu
                                   ).then_inc(m_act, 1)
                    act.wait_ge(m_d, 1)
                    act.activation(small["ex"][:], small["s"][:], ACT.Exp).then_inc(m_act, 1)

                    def shared(b, copies):
                        for j, (_, n) in enumerate(SJ):
                            p, m = j % 2, b * (NSJ // 2) + j // 2
                            act.wait_ge(s_gu[p], m + 1)
                            act.activation(ssl[p][0:n, :], ps_g[p][0:n, :], ACT.Silu).then_inc(s_sl[p], 1)
                            if copies:
                                act.activation(suu[p][0:n, :], ps_u[p][0:n, :], ACT.Copy).then_inc(s_sl[p], 1)
                    with act.Fori(0, NB // 2) as b:
                        shared(b, True)
                    with act.Fori(NB // 2, NB) as b:
                        shared(b, False)

                @block.vector
                def _(dve):
                    own = Steps(dve, g["wk_own"])
                    own.n = (FIRST + NB * BESIDE) * g["WKV_OWN"]
                    for b in range(NB):
                        xb = R[:].rearrange("p k t -> p (k t)")[:, b * NC * T:(b + 1) * NC * T]
                        dve.wait_ge(m_g, 16 * b + 16)
                        dve.wait_ge(m_sig, b + 1)
                        dve.tensor_tensor(xb, xb, gt[:], ALU.mult).then_inc(m_r, 1)
                    S = {k: v[:] for k, v in small.items()}
                    flat = {k: v[:].rearrange("p t e -> p (t e)") for k, v in small.items()}

                    def over_e(a):
                        return a[:].rearrange("p (t o) -> p t o", o=1).to_broadcast([P, TT, E])

                    def over_t(a):
                        return a[:].rearrange("p (o e) -> p o e", o=1).to_broadcast([P, TT, E])

                    def add_shared(b):
                        for c in range(NC):
                            p = c % 2
                            dve.wait_ge(s_y[p], b * 2 + c // 2 + 1)
                            xk = X[:, bass.ds((b * NC + c) * T, T)]
                            dve.tensor_tensor(xk, xk, ps_y[p][:], ALU.add).then_inc(s_yf[p], 1)
                    dve.wait_ge(m_act, 1)
                    own(dve.tensor_tensor(S["s"], ps_l[:].rearrange("p (t e) -> p t e", t=TT)[:, :, E:2 * E], S["sl"],
                                          ALU.mult)); own.sync()
                    own(dve.scalar_tensor_tensor(flat["t0"], flat["s"], -1.0, flat["s"], ALU.mult, ALU.max)); own.sync()
                    own(dve.tensor_reduce(rt1["m"][:], S["t0"], AX.X, ALU.max)); own.sync()
                    dve.tensor_tensor(S["s"], S["t0"], over_e(rt1["m"]), ALU.subtract).then_inc(m_d, 1)
                    dve.wait_ge(m_act, 2)
                    own(dve.tensor_reduce(rt1["sum"][:], S["ex"], AX.X, ALU.add)); own.sync()
                    own(dve.reciprocal(rt1["ri"][:], rt1["sum"][:])); own.sync()
                    own(dve.tensor_tensor(S["pr"], S["ex"], over_e(rt1["ri"]), ALU.mult)); own.sync()
                    dve.wait_ge(m_in, 48)
                    own(dve.tensor_tensor(S["bi"], S["pr"], over_t(ebias), ALU.add))
                    own(dve.tensor_tensor(S["t0"], S["pr"], over_t(escale), ALU.mult)); own.sync()
                    own(dve.tensor_scalar(flat["Wt"], flat["t0"], 1.0, None, ALU.add))
                    this = S["bi"].rearrange("p t (e o) -> p t e o", o=1).to_broadcast([P, TT, E, E])
                    other = S["bi"].rearrange("p t (o e) -> p t o e", o=1).to_broadcast([P, TT, E, E])
                    low = lower[:].rearrange("p (o e) f -> p o e f", o=1).to_broadcast([P, TT, E, E])
                    own(dve.tensor_tensor(big[0][:], other, this, ALU.is_equal)); own.sync()
                    dve.wait_ge(m_c, 9)
                    own(dve.tensor_tensor(big[0][:], big[0][:], low, ALU.mult))
                    own(dve.tensor_tensor(big[1][:], other, this, ALU.is_gt)); own.sync()
                    own(dve.tensor_tensor(big[0][:], big[0][:], big[1][:], ALU.add)); own.sync()
                    own(dve.tensor_reduce(flat["rank"], big[0][:].rearrange("p t e f -> p (t e) f"), AX.X, ALU.add))
                    own.sync()
                    dve.tensor_scalar(flat["M"], flat["rank"], TOPK - 0.5, None, ALU.is_lt).then_inc(m_M, 1)
                    add_shared(0)
                    dve.wait_ge(m_pre, 1)
                    tot_et = small["tot"][:].rearrange("p a b -> p (a b)").rearrange("p (e t) -> p e t", e=E)
                    own(dve.tensor_copy(tot_et, ps_pre[:, TT * E:2 * TT * E].rearrange("p (t e) -> p e t", t=TT)))
                    own.sync()
                    own(dve.tensor_tensor_scan(flat["inc"], fresh[:].rearrange("p e t -> p (e t)"), flat["tot"], 0.0,
                                               ALU.mult, ALU.add)); own.sync()
                    inc_et = flat["inc"].rearrange("p (e t) -> p e t", e=E)
                    own(dve.tensor_scalar(rowi[:], inc_et[:, :, TT - 1], float(P - 1), None, ALU.add)); own.sync()
                    own(dve.tensor_scalar(rowi[:], rowi[:], 7, None, ALU.arith_shift_right)); own.sync()
                    own(dve.tensor_scalar(row["nb"][:], rowi[:], 1.0, None, ALU.max)); own.sync()
                    own(dve.tensor_tensor_scan(row["end"][:], ones[:, 0:E], row["nb"][:], 0.0, ALU.mult, ALU.add))
                    own(dve.tensor_tensor(flat["t0"], flat["inc"], flat["tot"], ALU.subtract)); own.sync()
                    own(dve.tensor_tensor(row["c"][:], row["end"][:], row["nb"][:], ALU.subtract)); own.sync()
                    own(dve.tensor_scalar(row["base"][:], row["c"][:], float(P), None, ALU.mult)); own.sync()
                    own(dve.tensor_tensor(S["t1"], flat["t0"].rearrange("p (e t) -> p t e", e=E), over_t(row["base"]),
                                          ALU.add)); own.sync()
                    own(dve.tensor_tensor(flat["pos"], flat["t1"], ps_pre[:, 0:TT * E], ALU.add)); own.sync()
                    for k in range(TOPK):
                        own(dve.scalar_tensor_tensor(flat["t0"], flat["rank"], float(k), flat["pos"], ALU.is_equal,
                                                     ALU.mult))
                        own(dve.scalar_tensor_tensor(flat["t1"], flat["rank"], float(k), flat["Wt"], ALU.is_equal,
                                                     ALU.mult)); own.sync()
                        own(dve.tensor_reduce(rt1["m"][:], S["t0"], AX.X, ALU.add))
                        own(dve.tensor_reduce(wkk[:, :, k], S["t1"], AX.X, ALU.add)); own.sync()
                        own(dve.tensor_copy(posk[:, :, k], rt1["m"][:])); own.sync()
                    own(dve.tensor_copy(endm[:, WBUF:], row["end"][:]))
                    own(dve.tensor_tensor(ebc[:], row["end"][:].rearrange("p (o e) -> p o e", o=1).to_broadcast([P, NBLK, E]),
                                          blk[:].rearrange("p (n o) -> p n o", o=1).to_broadcast([P, NBLK, E]),
                                          ALU.is_le)); own.sync()
                    own(dve.tensor_reduce(ej[:], ebc[:], AX.X, ALU.add)); own.sync()
                    own(dve.tensor_scalar(eji[:], ej[:], float(E - 1), None, ALU.min)); own.sync()
                    assert WBUF == 3 and all(e // 3 == e * 11 >> 5 for e in range(E))
                    own(dve.tensor_scalar(third[:], eji[:], 11.0, None, ALU.mult)); own.sync()
                    own(dve.tensor_scalar(third[:], third[:], 5, None, ALU.arith_shift_right)); own.sync()
                    own(dve.scalar_tensor_tensor(slot[:], third[:], -3.0, eji[:], ALU.mult, ALU.add))
                    dve.tensor_scalar(wload[:], eji[:], 64.0, 64.0, ALU.mult, ALU.add).then_inc(m_pos, 1)

                    add_shared(1)
                    with dve.Fori(NB // 2, NB) as b:
                        for j, (_, n) in enumerate(SJ):
                            p, m = j % 2, b * (NSJ // 2) + j // 2
                            dve.wait_ge(s_sl[p], m + NSJ // 2 * (NB // 2) + 1)
                            dve.wait_ge(s_gu[p], m + 1)
                            dve.tensor_tensor(hsh[0:n, j, :], ssl[p][0:n, :], ps_u[p][0:n, :], ALU.mult
                                              ).then_inc(s_h[p], 1)
                        add_shared(b)
                    g["own_after_router"] = own.n

        IJ = [(0, P), (P, P), (2 * P, I - 2 * P)]
        GW, DW = NC * I, len(IJ) * C
        b_x, b_tx, b_xt, b_gate, b_gu, b_sl, b_h, b_st = (
            pair(n) for n in ("b_x", "b_tx", "b_xt", "b_gate", "b_gu", "b_sl", "b_h", "b_st"))
        b_ht, b_hte, b_y, b_ye, b_w = (sem(n) for n in ("b_ht", "b_hte", "b_y", "b_ye", "b_w"))
        UN = 4
        with ExitStack() as st:
            g["wkv_buffers"](st, "b")
            wg = sb("wg", [P, WBUF * GW], stack=st)
            wu = sb("wu", [P, WBUF * GW], stack=st)
            wd = sb("wd", [P, WBUF * DW], stack=st)
            xg = [sb(f"xg{s}", [P, C], stack=st) for s in range(2)]
            xgT = [sb(f"xgT{s}", [P, NC, P], stack=st) for s in range(2)]
            sl = [sb(f"bsl{s}", [P, I], stack=st) for s in range(2)]
            h = [sb(f"bh{s}", [P, I], stack=st) for s in range(2)]
            hT = [sb(f"hT{s}", [P, len(IJ), P], stack=st) for s in range(2)]
            ys = [sb(f"ys{s}", [P, C], stack=st) for s in range(2)]
            ps_x, ps_g, ps_u, ps_h, ps_y = psum[0:2], psum[2:4], psum[4:6], psum[6], psum[7]
            WITH = LATER // 2

            def wkv_at(i, s):
                return (FIRST + NB * BESIDE) // 2 + i, FIRST + NB * BESIDE + i * 2 + s
            with nc.Block() as block:
                @block.sync
                def _(sp):
                    def load(n, m, p):
                        sp.wait_ge(b_tx[p], m)
                        sp.dma_start(xg[p][:], Xe[bass.ds(n * P, P)]).then_inc(b_x[p], 16)

                    def store(n, p):
                        sp.wait_ge(b_ye, n + 1)
                        sp.dma_start(Ye[bass.ds(n * P, P)], ys[p][:]).then_inc(b_st[p], 16)
                    load(0, 0, 0)
                    load(1, 0, 1)

                    def body(i, base):
                        for q in range(UN):
                            load(i * UN + q + 2, i * (UN // 2) + q // 2 + 1, q % 2)
                            store(i * UN + q, q % 2)
                            if q >= 2:
                                m, lk = wkv_at(i, q - 2)
                                g["wkv_store"](sp, m, q - 2, lk)
                                if base:
                                    g["wkv_load"](sp, m + 1, q - 2, i * 2 + q + FIRST + NB * BESIDE - base)
                    for j in range(2):
                        g["wkv_load"](sp, wkv_at(0, j)[0], j, wkv_at(0, j)[1] % NK)
                    turn = (3 * NK - FIRST - NB * BESIDE) // 2 - 1
                    for start, stop, base in ((0, turn, 2 * NK), (turn, WITH - 1, 3 * NK)):
                        with sp.Fori(start, stop) as i:
                            body(i, base)
                    body(WITH - 1, None)
                    with sp.Fori(WITH, NBLK // UN - 1) as i:
                        for q in range(UN):
                            load(i * UN + q + 2, i * (UN // 2) + q // 2 + 1, q % 2)
                            store(i * UN + q, q % 2)
                    for q in range(UN):
                        n = NBLK - UN + q
                        if q < 2:
                            load(n + 2, n // 2 + 1, q % 2)
                        store(n, q % 2)
                    for p in range(2):
                        sp.wait_ge(b_st[p], 16 * NBLK // 2)
                        sp.wait_ge(g["wk_store"][p], 16 * 2 * NK)

                @block.gpsimd
                def _(pool):
                    def load(e, s):
                        done = pool.value_load(endm[0:1, bass.ds(e, 1)], min_val=0, max_val=NBLK)
                        pool.wait_ge(b_w, e * 64)
                        pool.wait_ge(b_y, done)
                        pool.wait_ge(m_pos, 1)
                        pool.dma_start(wg[:, s * GW:(s + 1) * GW].rearrange("p (a c n) -> p a c n", a=1, c=NC),
                                       io["WgT"][bass.ds(e, 1)].rearrange("a (c p) n -> p a c n", p=P)
                                       ).then_inc(b_w, 16)
                        pool.dma_start(wu[:, s * GW:(s + 1) * GW].rearrange("p (a c n) -> p a c n", a=1, c=NC),
                                       io["WuT"][bass.ds(e, 1)].rearrange("a (c p) n -> p a c n", p=P)
                                       ).then_inc(b_w, 16)
                        pool.dma_start(wd[:, s * DW:s * DW + 2 * C].rearrange("p (a c n) -> p a c n", a=1, c=2),
                                       io["WdT"][bass.ds(e, 1), 0:2 * P].rearrange("a (c p) n -> p a c n", p=P)
                                       ).then_inc(b_w, 16)
                        pool.dma_start(wd[0:I - 2 * P, s * DW + 2 * C:(s + 1) * DW],
                                       io["WdT"][bass.ds(e, 1), 2 * P:I].rearrange("a p n -> p (a n)")
                                       ).then_inc(b_w, 16)
                    with pool.Fori(0, E // WBUF) as i:
                        for s in range(WBUF):
                            load(i * WBUF + s, s)
                    for e in range(E - E % WBUF, E):
                        load(e, e % WBUF)

                @block.tensor
                def _(pe):
                    def turn_x(n, m, p):
                        pe.wait_ge(b_x[p], m * 16 + 16)
                        pe.wait_ge(b_xt[p], m)
                        for c in range(NC):
                            mm = pe.transpose(ps_x[p][:, c * P:c * P + P], xg[p][:, c * P:c * P + P], ident[:])
                        mm.then_inc(b_tx[p], 1)

                    def gate(n, m, p, par):
                        pe.wait_ge(b_xt[p], m + 1)
                        pe.wait_ge(b_h[p], m)
                        for c in range(NC):
                            mm = pe.matmul(ps_g[p][:, 0:I], xgT[p][:, c, :], wg[:, bass.ds(par * GW + c * I, I)],
                                           start=c == 0, stop=c == NC - 1)
                        mm.then_inc(b_gate[p], 1)

                    def up(n, m, p, par):
                        for c in range(NC):
                            mm = pe.matmul(ps_u[p][:, 0:I], xgT[p][:, c, :], wu[:, bass.ds(par * GW + c * I, I)],
                                           start=c == 0, stop=c == NC - 1)
                        mm.then_inc(b_gu[p], 1)

                    def turn_h(n, m, p):
                        pe.wait_ge(b_h[p], m + 1)
                        pe.wait_ge(b_hte, n)
                        for j, (at, w) in enumerate(IJ):
                            mm = pe.transpose(ps_h[0:w, j * P:j * P + P], h[p][:, at:at + w], ident[:])
                        mm.then_inc(b_ht, 1)

                    def down(n, m, p, par):
                        pe.wait_ge(b_hte, n + 1)
                        pe.wait_ge(b_ye, n)
                        for j, (at, w) in enumerate(IJ):
                            mm = pe.matmul(ps_y[:], hT[p][0:w, j, :], wd[0:w, bass.ds(par * DW + j * C, C)],
                                           start=j == 0, stop=j == len(IJ) - 1)
                        mm.then_inc(b_y, 1)

                    def finish(n, m, p, stage):
                        if stage == 0:
                            turn_h(n, m, p)
                        else:
                            par = pe.value_load(slot[0:1, bass.ds(n, 1)], min_val=0, max_val=WBUF - 1)
                            down(n, m, p, par)

                    def body(i, first=False, last=False):
                        for q in range(UN):
                            n, m, p = i * UN + q, i * 2 + q // 2, q % 2
                            before = (n - 1, m - 1 + p, 1 - p)
                            need = pe.value_load(wload[0:1, bass.ds(n, 1)], min_val=0, max_val=64 * E)
                            par = pe.value_load(slot[0:1, bass.ds(n, 1)], min_val=0, max_val=WBUF - 1)
                            pe.wait_ge(b_w, need)
                            gate(n, m, p, par)
                            if q or not first:
                                finish(*before, 0)
                            up(n, m, p, par)
                            if q < UN - 1 or not last:
                                turn_x(n + 1, m + p, 1 - p)
                            if q or not first:
                                finish(*before, 1)
                    turn_x(0, 0, 0)
                    body(0, first=True)
                    with pe.Fori(1, NBLK // UN - 1) as i:
                        body(i)
                    body(NBLK // UN - 1, last=True)
                    for stage in range(2):
                        finish(NBLK - 1, NBLK // 2 - 1, 1, stage)

                @block.scalar
                def _(act):
                    def evict_x(n, m, p):
                        act.wait_ge(b_tx[p], m + 1)
                        act.activation(xgT[p][:].rearrange("p c t -> p (c t)"), ps_x[p][:], ACT.Copy
                                       ).then_inc(b_xt[p], 1)

                    def evict_y(n, m, p):
                        act.wait_ge(b_y, n + 1)
                        act.wait_ge(b_st[p], m * 16)
                        act.activation(ys[p][:], ps_y[:], ACT.Copy).then_inc(b_ye, 1)

                    def body(i, tiles, first=False, last=False):
                        for q in range(UN):
                            n, m, p = i * UN + q, i * 2 + q // 2, q % 2
                            act.wait_ge(b_gate[p], m + 1)
                            act.activation(sl[p][:], ps_g[p][:, 0:I], ACT.Silu).then_inc(b_sl[p], 1)
                            if q < UN - 1 or not last:
                                evict_x(n + 1, m + p, 1 - p)
                            if tiles and q % 2 == 0:
                                g["wkv_scalar"](act, wkv_at(i, q // 2)[0], q // 2)
                            if q or not first:
                                evict_y(n - 1, m - 1 + p, 1 - p)
                    evict_x(0, 0, 0)
                    body(0, True, first=True)
                    with act.Fori(1, WITH) as i:
                        body(i, True)
                    with act.Fori(WITH, NBLK // UN - 1) as i:
                        body(i, False)
                    body(NBLK // UN - 1, False, last=True)
                    evict_y(NBLK - 1, NBLK // 2 - 1, 1)

                @block.vector
                def _(dve):
                    own = Steps(dve, g["wk_own"])
                    own.n = g["own_after_router"]

                    def evict_h(n, m, p):
                        dve.wait_ge(b_ht, n + 1)
                        own(dve.tensor_copy(hT[p][:, 0:2, :].rearrange("p c t -> p (c t)"), ps_h[:, 0:2 * P]))
                        w = IJ[2][1]
                        own.sync()
                        dve.tensor_copy(hT[p][0:w, 2, :], ps_h[0:w, 2 * P:3 * P]).then_inc(b_hte, 1)

                    def body(i, tiles, first=False):
                        for q in range(UN):
                            n, m, p = i * UN + q, i * 2 + q // 2, q % 2
                            if tiles and not p:
                                tile = g["wkv_vector"](dve, wkv_at(i, q // 2)[0], q // 2, wkv_at(i, q // 2)[1],
                                                       own, euv_here=True)
                            if q or not first:
                                evict_h(n - 1, m - 1 + p, 1 - p)
                            if tiles:
                                for _ in range(3 if p else 2):
                                    next(tile)
                            dve.wait_ge(b_sl[p], m + 1)
                            dve.wait_ge(b_gu[p], m + 1)
                            dve.tensor_tensor(h[p][:], sl[p][:], ps_u[p][:, 0:I], ALU.mult).then_inc(b_h[p], 1)
                            if tiles:
                                for _ in range(4 if p else 5):
                                    next(tile)
                    body(0, True, first=True)
                    for start, stop, tiles in ((1, WITH, True), (WITH, NBLK // UN - 1, False)):
                        with dve.Fori(start, stop) as i:
                            own.enter(i - start, UN + (2 * (g["WKV_OWN"] + 1) if tiles else 0))
                            body(i, tiles)
                            own.leave(stop - start)
                    body(NBLK // UN - 1, False)
                    evict_h(NBLK - 1, NBLK // 2 - 1, 1)
                    g["own_after_blocks"] = own.n

        d_y = pair("d_y")
        d_dg, d_done, d_b, d_f = (pair(n) for n in ("d_dg", "d_done", "d_b", "d_f"))
        with ExitStack() as st:
            yk = [[sb(f"yk{s}{k}", [P, C], stack=st) for k in range(TOPK)] for s in range(2)]
            dg = [[sb(f"dg{s}{k}", [P, P], stack=st) for k in range(TOPK)] for s in range(2)]
            with nc.Block() as block:
                @block.gpsimd
                def _(pool):
                    for t in range(TT):
                        p = t % 2
                        if t >= 2:
                            pool.wait_ge(d_done[p], t // 2)
                        for k in range(TOPK):
                            pool.indirect_dma_start(
                                out=yk[p][k][:], out_offset=None, in_=Ye,
                                in_offset=bass.IndirectOffsetOnAxis(ap=posk[:, t, k:k + 1], axis=0),
                                bounds_check=NBLK * P - 1, oob_is_err=False).then_inc(d_y[p], 16)

                @block.tensor
                def _(pe):
                    for t in range(TT):
                        p, b, tt = t % 2, t // NT, t % NT
                        pe.wait_ge(d_y[p], 16 * TOPK * (t // 2 + 1))
                        pe.wait_ge(d_dg[p], TOPK * (t // 2 + 1))
                        if tt == 0 and b >= 2:
                            pe.wait_ge(d_f[b % 2], b // 2)
                        for c in range(NC):
                            for k in range(TOPK):
                                mm = pe.matmul(psum[b % 2 * NC + c][:, tt * P:tt * P + P], yk[p][k][:, c * P:c * P + P],
                                               dg[p][k][:], start=k == 0, stop=k == TOPK - 1)
                        mm.then_inc(d_done[p], 1)

                def add(dve, b):
                    for p in range(2):
                        dve.wait_ge(d_done[p], (b + 1) * 2)
                    for c in range(NC):
                        k = b * NC + c
                        ins = dve.tensor_tensor(X[:, k * T:(k + 1) * T], X[:, k * T:(k + 1) * T],
                                                psum[b % 2 * NC + c][:], ALU.add)
                    ins.then_inc(d_f[b % 2], 1)

                @block.vector
                def _(dve):
                    for t in range(TT):
                        p, b = t % 2, t // NT
                        if t >= 2:
                            dve.wait_ge(d_done[p], t // 2)
                        for k in range(TOPK):
                            dve.tensor_scalar(dg[p][k][:], ident[:], wkk[:, t, k:k + 1], None, ALU.mult
                                              ).then_inc(d_dg[p], 1)
                        if t % NT == 1 and b:
                            add(dve, b - 1)
                    add(dve, NB - 1)

def state_space(nc, io, g):
    sb, sem, pair, X, ident, psum, G_dram = (g[k] for k in ("sb", "sem", "pair", "X", "ident", "psum", "G_dram"))
    BC_dram = nc.dram_tensor("BC_scratch", [2 * NS, T], F32, kind="Internal").ap()
    RING = 8
    TAPS = 4
    v_in, v_c, v_g, v_sig, v_r, v_u, v_x, v_dt, v_bc, v_bcs, v_dl, v_abs, v_ln, v_du = (
        sem(n) for n in ("v_in", "v_c", "v_g", "v_sig", "v_r", "v_u", "v_x", "v_dt", "v_bc", "v_bcs", "v_dl", "v_abs",
                         "v_ln", "v_du"))
    v_ring = [sem(f"v_ring{j}") for j in range(RING)]
    v_da, v_h, v_hc, v_y, v_out, v_a = (sem(n) for n in ("v_da", "v_h", "v_hc", "v_y", "v_out", "v_a"))
    v_own = sem("v_own")
    v_rel = sem("v_rel")
    with ExitStack() as st:
        gt = sb("v_gt", [P, NC, T], stack=st)
        sig = sb("v_sigx", [P, NC, T], stack=st)
        r = sb("v_r", [P, NC, TAPS - 1 + T], stack=st)
        u = sb("v_u", [P, NC, T], stack=st)
        du = sb("v_dut", [P, NC, T], stack=st)
        delta = sb("v_delta", [P, NC, T], stack=st)
        soft = sb("v_soft", [P, NC, T], stack=st)
        relu = sb("v_relu", [P, NC, T], stack=st)
        dtT = sb("v_dtT", [P, T], stack=st)
        bcT = sb("v_bcT", [2 * NS, T], stack=st)
        ring = [sb(f"v_bc{j}", [P, 2, T], stack=st) for j in range(RING)]
        dA, dBu, h, hC = ([sb(f"v_{n}{s}", [P, NC, T], stack=st) for s in range(2)] for n in ("dA", "dBu", "h", "hC"))
        xw = sb("v_xw", [P, NC, DTR + 2 * NS], stack=st)
        dw = sb("v_dw", [P, C], stack=st)
        taps = sb("v_taps", [P, NC, TAPS], stack=st)
        cvec = sb("v_cvec", [P, 3, NC], stack=st)
        alog = sb("v_alog", [P, NC, NS], stack=st)
        aexp = sb("v_aexp", [P, NC, NS], stack=st)
        A = sb("v_A", [P, NC, NS], stack=st)
        ps_y, ps_dt, ps_bc, ps_dl = psum[0:4], psum[4], psum[5], psum[6:8]
        with nc.Block() as block:
            @block.sync
            def _(sp):
                sp.dma_start(xw[:], io["xprojT"].rearrange("(c p) n -> p c n", p=P)).then_inc(v_in, 16)
                sp.dma_start(dw[:], io["dtprojT"]).then_inc(v_in, 16)
                sp.dma_start(taps[:], io["taps"]).then_inc(v_in, 16)
                sp.dma_start(cvec[:], io["cvec"]).then_inc(v_in, 16)
                sp.dma_start(alog[:], io["alog"]).then_inc(v_in, 16)
                with sp.Fori(0, NB) as b:
                    sp.wait_ge(v_r, b)
                    sp.dma_start(gt[:], G_dram[bass.ds(b * NC + 2 * NK, NC)].rearrange("c p t -> p c t")
                                 ).then_inc(v_g, 16)
                    sp.wait_ge(v_bc, b + 1)
                    sp.dma_start(BC_dram, bcT[:]).then_inc(v_bcs, 16)
                    sp.wait_ge(v_bcs, b * 16 + 16)
                    for n in range(NS):
                        sp.wait_ge(v_hc, b * NS if n < RING else b * NS + (n - RING + 1))
                        sp.dma_start(ring[n % RING][:],
                                     BC_dram.rearrange("(a n) t -> n a t", a=2)[n:n + 1].to_broadcast([P, 2, T])
                                     ).then_inc(v_ring[n % RING], 16)

            @block.gpsimd
            def _(pool):
                pool.memset(r[:, :, 0:TAPS - 1], 0.0).then_inc(v_c, 1)
                with pool.Fori(0, NB) as b:
                    for n in range(NS):
                        p = n % 2
                        pool.wait_ge(v_ring[n % RING], (b * (NS // RING) + n // RING) * 16 + 16)
                        pool.wait_ge(v_y, b * NS if n < 2 else b * NS + n - 1)
                        pool.wait_ge(v_h, b * NS + n + 1)
                        pool.tensor_tensor(hC[p][:], h[p][:], ring[n % RING][:, 1:2, :].to_broadcast([P, NC, T]),
                                           ALU.mult).then_inc(v_hc, 1)

            @block.tensor
            def _(pe):
                pe.wait_ge(v_in, 80)
                with pe.Fori(0, NB) as b:
                    pe.wait_ge(v_u, b + 1)
                    pe.wait_ge(v_x, b * 2)
                    for c in range(NC):
                        mm = pe.matmul(ps_bc[0:2 * NS, :], xw[:, c, DTR:], u[:, c, :], start=c == 0, stop=c == NC - 1)
                    for c in range(NC):
                        mm = pe.matmul(ps_dt[:], xw[:, c, 0:DTR], u[:, c, :], start=c == 0, stop=c == NC - 1)
                    mm.then_inc(v_dt, 1)
                    pe.wait_ge(v_x, b * 2 + 2)
                    for c in range(NC):
                        pe.wait_ge(v_abs, b * NC + max(c - 1, 0))
                        pe.wait_ge(v_rel, b * NC + max(c - 1, 0))
                        pe.matmul(ps_dl[c % 2][:], dw[:, c * P:c * P + P], dtT[:], start=True, stop=True
                                  ).then_inc(v_dl, 1)
                    pe.wait_ge(v_out, b * NC)
                    for n in range(NS):
                        pe.wait_ge(v_hc, b * NS + n + 1)
                        for c in range(NC):
                            mm = pe.matmul(ps_y[c][:], ident[:], hC[n % 2][:, c, :], start=n == 0, stop=n == NS - 1,
                                           skip_group_check=True)
                        mm.then_inc(v_y, 1)

            @block.scalar
            def _(act):
                act.wait_ge(v_in, 80)
                act.activation(aexp[:], alog[:], ACT.Exp).then_inc(v_a, 1)
                act.wait_ge(v_a, 1)
                act.activation(A[:], aexp[:], ACT.Copy, scale=-1.0).then_inc(v_a, 1)
                act.wait_ge(v_a, 2)
                with act.Fori(0, NB) as b:
                    act.activation(sig[:].rearrange("p c t -> p (c t)"), X[:, bass.ds(b * NC * T, NC * T)], ACT.Sigmoid
                                   ).then_inc(v_sig, 1)
                    act.wait_ge(v_dt, b + 1)
                    act.activation(bcT[:], ps_bc[0:2 * NS, :], ACT.Copy).then_inc(v_bc, 1)
                    act.activation(dtT[:], ps_dt[:], ACT.Copy).then_inc(v_x, 2)
                    for c in range(NC):
                        act.wait_ge(v_dl, b * NC + c + 1)
                        act.activation(soft[:, c, :], ps_dl[c % 2][:], ACT.Abs, bias=cvec[:, 1, c:c + 1]
                                       ).then_inc(v_abs, 1)
                    act.wait_ge(v_abs, b * NC + NC)
                    flat = soft[:].rearrange("p c t -> p (c t)")
                    act.activation(flat, flat, ACT.Exp, scale=-1.0).then_inc(v_ln, 1)
                    act.wait_ge(v_ln, b * 2 + 1)
                    act.activation(flat, flat, ACT.Ln, bias=1.0).then_inc(v_ln, 1)
                    act.wait_ge(v_du, b + 1)
                    for n in range(NS):
                        act.wait_ge(v_h, b * NS if n < 2 else b * NS + n - 1)
                        for c in range(NC):
                            ins = act.activation(dA[n % 2][:, c, :], delta[:, c, :], ACT.Exp, scale=A[:, c, n:n + 1])
                        ins.then_inc(v_da, 1)

            @block.vector
            def _(dve):
                own = Steps(dve, v_own)
                dve.wait_ge(v_in, 80)
                dve.wait_ge(v_c, 1)
                with dve.Fori(0, NB) as b:
                    own.enter(b, NC * TAPS + NS * NC + NC)
                    dve.wait_ge(v_g, b * 16 + 16)
                    dve.wait_ge(v_sig, b + 1)
                    dve.tensor_tensor(r[:, :, TAPS - 1:], sig[:], gt[:], ALU.mult).then_inc(v_r, 1)
                    dve.wait_ge(v_r, b + 1)
                    for j in range(TAPS):
                        for c in range(NC):
                            tap, src = taps[:, c, j:j + 1], r[:, c, j:j + T]
                            if j == 0:
                                own(dve.tensor_scalar(u[:, c, :], src, tap, cvec[:, 0, c:c + 1], ALU.mult, ALU.add))
                            else:
                                ins = dve.scalar_tensor_tensor(u[:, c, :], src, tap, u[:, c, :], ALU.mult, ALU.add)
                                if j < TAPS - 1 or c < NC - 1:
                                    own(ins)
                                else:
                                    ins.then_inc(v_u, 1)
                        if j < TAPS - 1:
                            own.sync()
                    for c in range(NC):
                        dve.wait_ge(v_abs, b * NC + c + 1)
                        dve.tensor_scalar(relu[:, c, :], ps_dl[c % 2][:], cvec[:, 1, c:c + 1], 0.0, ALU.add, ALU.max
                                          ).then_inc(v_rel, 1)
                    dve.wait_ge(v_rel, b * NC + NC)
                    dve.wait_ge(v_ln, b * 2 + 2)
                    dve.tensor_tensor(delta[:], relu[:], soft[:], ALU.add).then_inc(v_du, 1)
                    dve.wait_ge(v_du, b + 1)
                    dve.wait_ge(v_u, b + 1)
                    own(dve.tensor_tensor(du[:], delta[:], u[:], ALU.mult))
                    for n in range(NS):
                        p = n % 2
                        own.sync()
                        dve.wait_ge(v_ring[n % RING], (b * (NS // RING) + n // RING) * 16 + 16)
                        own(dve.tensor_tensor(dBu[p][:], du[:], ring[n % RING][:, 0:1, :].to_broadcast([P, NC, T]),
                                              ALU.mult))
                        own.sync()
                        dve.wait_ge(v_da, b * NS + n + 1)
                        dve.wait_ge(v_hc, b * NS if n < 2 else b * NS + n - 1)
                        for c in range(NC):
                            ins = dve.tensor_tensor_scan(h[p][:, c, :], dA[p][:, c, :], dBu[p][:, c, :], 0.0,
                                                         ALU.mult, ALU.add)
                            if c < NC - 1:
                                own(ins)
                        ins.then_inc(v_h, 1)
                    dve.wait_ge(v_y, b * NS + NS)
                    for c in range(NC):
                        own(dve.scalar_tensor_tensor(u[:, c, :], u[:, c, :], cvec[:, 2, c:c + 1], ps_y[c][:],
                                                     ALU.mult, ALU.add))
                    own.sync()
                    for c in range(NC):
                        xk = X[:, bass.ds((b * NC + c) * T, T)]
                        dve.tensor_tensor(xk, xk, u[:, c, :], ALU.add).then_inc(v_out, 1)
                    own.leave(NB)


def linear_attention(nc, io, g):
    sb, sem, pair, X, ident, psum, G_dram = (g[k] for k in ("sb", "sem", "pair", "X", "ident", "psum", "G_dram"))
    L = NB
    DK = C // 2
    HK, HV = DK // HEADS, C // HEADS
    f_in, f_g, f_sig, f_r, f_cv, f_xs, f_own, f_o, f_std, f_sc, f_d, f_st, f_var, f_out = (
        sem(n) for n in ("f_in", "f_g", "f_sig", "f_r", "f_cv", "f_xs", "f_own", "f_o", "f_std", "f_sc", "f_d",
                         "f_st", "f_var", "f_out"))
    f_p, f_pf = ([sem(f"{n}{j}") for j in range(4)] for n in ("f_p", "f_pf"))
    f_t, f_te, f_w = (pair(n) for n in ("f_t", "f_te", "f_w"))
    with ExitStack() as st:
        wqk, wv, wg, wo = (sb(f"f_w{n}", [P, NC, C], stack=st) for n in ("qk", "v", "g", "o"))
        gt = sb("f_gt", [P, NK, P], stack=st)
        r = sb("f_rt", [P, NK, P], stack=st)
        cv = sb("f_conv", [P, NK, P], stack=st)
        xs = sb("f_xst", [P, NK, P], stack=st)
        qk = [sb(f"f_qk{j}", [P, L, 2 * DK], stack=st) for j in range(2)]
        v = [sb(f"f_v{j}", [P, L, C], stack=st) for j in range(2)]
        gate = [sb(f"f_gate{j}", [P, L, C], stack=st) for j in range(2)]
        ra = sb("f_ra", [P, L, 2 * HEADS, HK // 2], stack=st)
        rb = sb("f_rb", [P, L, 2 * HEADS, HK // 2], stack=st)
        rot = sb("f_rot", [P, L, 2 * HEADS, HK], stack=st)
        vw = sb("f_vw", [P, L, C], stack=st)
        o = sb("f_ot", [P, L, C], stack=st)
        oT = sb("f_oT", [P, NC, L * P], stack=st)
        xo = sb("f_xo", [P, NK, P], stack=st)
        cs = sb("f_cs", [P, 2, L, HK // 2], stack=st)
        taps = sb("f_taps", [P, NC, 2], stack=st)
        rr = sb("f_rr", [P, 2, C], stack=st)
        rd = sb("f_rd", [P, C], stack=st)
        eps = sb("f_eps", [P, 1], stack=st)
        tiny = {n: sb(f"f_{n}", [P, L * HEADS], stack=st) for n in
                ("dd", "ad", "sel", "sc_", "cnt", "rc", "fl", "mu", "var_", "std_", "rs")}
        same = sb("f_same", [P, L, L, HEADS], stack=st)
        dots = sb("f_dots", [P, L, L, HEADS], stack=st)
        ps_p, ps_t, ps_w = psum[0:4], psum[4:6], psum[6:8]
        JT = T // P
        with nc.Block() as block:
            @block.sync
            def _(sp):
                for w, n in ((wqk, "Wqk"), (wv, "fWv"), (wg, "fWg"), (wo, "fWout")):
                    sp.dma_start(w[:], io[n].rearrange("(c p) n -> p c n", p=P)).then_inc(f_in, 16)
                sp.dma_start(taps[:], io["ftaps"]).then_inc(f_in, 16)
                sp.dma_start(cs[:].rearrange("p a l d -> p (a l d)"), io["cs"].to_broadcast([P, 2 * L * HK // 2])
                             ).then_inc(f_in, 16)
                sp.dma_start(rr[:].rearrange("p a c -> p (a c)"), io["fr"].to_broadcast([P, 2 * C])).then_inc(f_in, 16)
                def load(t):
                    if t:
                        sp.wait_ge(f_r, t)
                    sp.dma_start(gt[:], G_dram[3 * NK:4 * NK].rearrange("k p t -> p k t")[:, :, t * P:t * P + P]
                                 ).then_inc(f_g, 16)
                load(0)
                load(1)
                for t in range(JT):
                    if t + 2 < JT:
                        load(t + 2)
                    sp.wait_ge(f_out, t * NC + NC)
                    sp.dma_start(io["out"].rearrange("k p t -> p k t")[:, :, t * P:t * P + P], xo[:]
                                 ).then_inc(f_st, 16)
                sp.wait_ge(f_st, 16 * JT)

            @block.tensor
            def _(pe):
                def project(t):
                    pe.wait_ge(f_xs, t + 1)
                    for l in range(L):
                        for j, w in enumerate((wqk, wv, wg)):
                            use = l * 3 + j
                            if t or use >= 4:
                                pe.wait_ge(f_pf[use % 4], t * 3 + use // 4)
                            for c in range(NC):
                                mm = pe.matmul(ps_p[use % 4][:], xs[:, l * NC + c, :], w[:, c, :],
                                               start=c == 0, stop=c == NC - 1)
                            mm.then_inc(f_p[use % 4], 1)

                def output(t):
                    pe.wait_ge(f_o, t + 1)
                    for l in range(L):
                        if t or l >= 2:
                            pe.wait_ge(f_te[l % 2], t * 2 + l // 2)
                        for c in range(NC):
                            mm = pe.transpose(ps_t[l % 2][:, c * P:c * P + P], o[:, l, c * P:c * P + P], ident[:])
                        mm.then_inc(f_t[l % 2], 1)
                    for p in range(2):
                        pe.wait_ge(f_te[p], t * 2 + 2)
                    for m in range(NC):
                        if t or m >= 2:
                            pe.wait_ge(f_out, t * NC + m - 1)
                        for c in range(NC):
                            mm = pe.matmul(ps_w[m % 2][:], wo[:, c, m * P:m * P + P], oT[:, c, :],
                                           start=c == 0, stop=c == NC - 1)
                        mm.then_inc(f_w[m % 2], 1)

                pe.wait_ge(f_in, 112)
                project(0)
                for t in range(JT):
                    if t + 1 < JT:
                        project(t + 1)
                    output(t)

            @block.scalar
            def _(act):
                def sigmoid(t):
                    if t:
                        act.wait_ge(f_cv, t * 2 * NC)
                    act.activation(r[:], X[:].rearrange("p (k t) -> p k t", k=NK)[:, :, t * P:t * P + P], ACT.Sigmoid
                                   ).then_inc(f_sig, 1)

                def silu(t):
                    act.wait_ge(f_cv, (t + 1) * 2 * NC)
                    act.activation(xs[:], cv[:], ACT.Silu).then_inc(f_xs, 1)

                def evict(t, use):
                    l, j = use // 3, use % 3
                    act.wait_ge(f_p[use % 4], t * 3 + use // 4 + 1)
                    if use == 0 and t >= 2:
                        act.wait_ge(f_o, t - 1)
                    ps = ps_p[use % 4]
                    if j == 0:
                        act.activation(qk[t % 2][:, l, 0:DK], ps[:, 0:DK], ACT.Silu)
                        ins = act.activation(qk[t % 2][:, l, DK:], ps[:, DK:], ACT.Copy)
                    elif j == 1:
                        ins = act.activation(v[t % 2][:, l, :], ps[:], ACT.Copy)
                    else:
                        ins = act.activation(gate[t % 2][:, l, :], ps[:], ACT.Silu)
                    ins.then_inc(f_pf[use % 4], 1)

                sigmoid(0)
                silu(0)
                sigmoid(1)
                for use in range(3 * L):
                    evict(0, use)
                silu(1)
                for t in range(JT):
                    for use in range(3 * L):
                        if t + 1 < JT:
                            evict(t + 1, use)
                        if use == 3 and t + 2 < JT:
                            sigmoid(t + 2)
                        if use == 5:
                            act.wait_ge(f_d, t * 2 + 1)
                            act.activation(tiny["sc_"][:], tiny["ad"][:], ACT.Sigmoid).then_inc(f_sc, 1)
                        if use == 8:
                            act.wait_ge(f_d, t * 2 + 2)
                            act.activation(vw[:], o[:], ACT.Square).then_inc(f_sc, 1)
                            act.wait_ge(f_var, t + 1)
                            act.activation(tiny["std_"][:], tiny["var_"][:], ACT.Sqrt, bias=eps[:], scale=1.0 / HV
                                           ).then_inc(f_std, 1)
                    if t:
                        for p in range(2):
                            act.wait_ge(f_w[p], t * 2)
                    for l in range(L):
                        act.wait_ge(f_t[l % 2], t * 2 + l // 2 + 1)
                        act.activation(oT[:, :, l * P:l * P + P], ps_t[l % 2][:].rearrange("p (c t) -> p c t", c=NC),
                                       ACT.Copy).then_inc(f_te[l % 2], 1)
                    if t + 2 < JT:
                        silu(t + 2)

            @block.vector
            def _(dve):
                own = Steps(dve, f_own)
                dve.wait_ge(f_in, 112)
                own(dve.memset(eps[:], EPS))
                own(dve.tensor_tensor(rd[:], rr[:, 1, :], rr[:, 0, :], ALU.subtract))
                own.sync()
                K = {k: x[:] for k, x in tiny.items()}

                def do(ins):
                    own(ins)
                    own.sync()

                def convolve(t):
                    dve.wait_ge(f_g, t * 16 + 16)
                    dve.wait_ge(f_sig, t + 1)
                    dve.tensor_tensor(r[:], r[:], gt[:], ALU.mult).then_inc(f_r, 1)
                    if t:
                        dve.wait_ge(f_xs, t)
                    dve.wait_ge(f_r, t + 1)
                    for c in range(NC):
                        dve.tensor_scalar(cv[:, c::NC, :], r[:, c::NC, :], taps[:, c, 1:2], None, ALU.mult
                                          ).then_inc(f_cv, 1)
                    dve.wait_ge(f_cv, t * 2 * NC + NC)
                    for c in range(NC):
                        dve.scalar_tensor_tensor(cv[:, NC + c::NC, :], r[:, c:NK - NC:NC, :], taps[:, c, 0:1],
                                                 cv[:, NC + c::NC, :], ALU.mult, ALU.add).then_inc(f_cv, 1)

                def add(t, m):
                    dve.wait_ge(f_w[m % 2], t * 2 + m // 2 + 1)
                    if m == 0 and t:
                        dve.wait_ge(f_st, t * 16)
                    dve.tensor_tensor(xo[:, m::NC, :],
                                      X[:].rearrange("p (k t) -> p k t", k=NK)[:, m::NC, t * P:t * P + P],
                                      ps_w[m % 2][:].rearrange("p (l t) -> p l t", l=L), ALU.add).then_inc(f_out, 1)

                def attend(t):
                    V, QK = v[t % 2], qk[t % 2]
                    for j in range(4):
                        dve.wait_ge(f_pf[j], t * 3 + 3)
                    do(dve.tensor_tensor(vw[:], V[:], rd[:].rearrange("p (o c) -> p o c", o=1).to_broadcast([P, L, C]),
                                         ALU.mult))
                    do(dve.tensor_reduce(K["dd"], vw[:].rearrange("p l (h d) -> p (l h) d", d=HV), AX.X, ALU.add))
                    own(dve.tensor_scalar(K["sel"], K["dd"], 0.0, None, ALU.is_gt))
                    dve.scalar_tensor_tensor(K["ad"], K["dd"], -1.0, K["dd"], ALU.mult, ALU.max).then_inc(f_d, 1)
                    if t:
                        add(t - 1, 1)
                    q4 = QK[:].rearrange("p l (h d) -> p l h d", d=HK)
                    x1, x2 = q4[:, :, :, 0:HK // 2], q4[:, :, :, HK // 2:]
                    cos, sin = (cs[:, a].rearrange("p l (o d) -> p l o d", o=1).to_broadcast([P, L, 2 * HEADS, HK // 2])
                                for a in range(2))
                    own(dve.tensor_tensor(ra[:], x1, cos, ALU.mult))
                    do(dve.tensor_tensor(rb[:], x2, sin, ALU.mult))
                    do(dve.tensor_tensor(rot[:, :, :, 0:HK // 2], ra[:], rb[:], ALU.subtract))
                    if t:
                        add(t - 1, 2)
                    own(dve.tensor_tensor(ra[:], x2, cos, ALU.mult))
                    do(dve.tensor_tensor(rb[:], x1, sin, ALU.mult))
                    do(dve.tensor_tensor(rot[:, :, :, HK // 2:], ra[:], rb[:], ALU.add))
                    if t:
                        add(t - 1, 3)
                    sel = K["sel"].rearrange("p (l h) -> p l h", l=L)
                    for l in range(L):
                        n = l + 1
                        ql = rot[:, l:l + 1, 0:HEADS, :].rearrange("p o h d -> p o (h d)").to_broadcast([P, n, DK])
                        km = rot[:, 0:n, HEADS:, :].rearrange("p m h d -> p m (h d)")
                        own(dve.tensor_tensor(same[:, l, 0:n, :], sel[:, 0:n, :],
                                              sel[:, l:l + 1, :].to_broadcast([P, n, HEADS]), ALU.is_equal))
                        do(dve.tensor_tensor(vw[:, 0:n, 0:DK], km, ql, ALU.mult))
                        own(dve.tensor_reduce(K["cnt"].rearrange("p (l h) -> p l h", l=L)[:, l, :],
                                              same[:, l, 0:n, :].rearrange("p m h -> p h m"), AX.X, ALU.add))
                        do(dve.tensor_reduce(dots[:, l, 0:n, :], vw[:, 0:n, 0:DK].rearrange("p m (h d) -> p m h d", d=HK),
                                             AX.X, ALU.add))
                        own(dve.tensor_tensor(dots[:, l, 0:n, :], dots[:, l, 0:n, :], same[:, l, 0:n, :], ALU.mult))
                    do(dve.reciprocal(K["rc"], K["cnt"]))
                    dve.wait_ge(f_sc, t * 2 + 1)
                    do(dve.scalar_tensor_tensor(K["fl"], K["sc_"], float(HK) ** -0.5, K["rc"], ALU.mult, ALU.mult))
                    fl = K["fl"].rearrange("p (l h) -> p l h", l=L)
                    if t:
                        for p in range(2):
                            dve.wait_ge(f_t[p], t * 2)
                    for l in range(L):
                        n = l + 1
                        do(dve.tensor_tensor(dots[:, l, 0:n, :], dots[:, l, 0:n, :],
                                             fl[:, l:l + 1, :].to_broadcast([P, n, HEADS]), ALU.mult))
                        do(dve.tensor_tensor(vw[:, 0:n, :].rearrange("p m (h d) -> p m h d", d=HV),
                                             V[:, 0:n, :].rearrange("p m (h d) -> p m h d", d=HV),
                                             dots[:, l, 0:n, :].rearrange("p m (h o) -> p m h o", o=1)
                                             .to_broadcast([P, n, HEADS, HV]), ALU.mult))
                        do(dve.tensor_reduce(o[:, l, :], vw[:, 0:n, :].rearrange("p m c -> p c m"), AX.X, ALU.add))
                    o3 = o[:].rearrange("p l (h d) -> p (l h) d", d=HV)

                    def wide(a):
                        return a.rearrange("p (n o) -> p n o", o=1).to_broadcast([P, L * HEADS, HV])
                    do(dve.tensor_reduce(K["mu"], o3, AX.X, ALU.add))
                    do(dve.tensor_scalar(K["mu"], K["mu"], 1.0 / HV, None, ALU.mult))
                    dve.tensor_tensor(o3, o3, wide(K["mu"]), ALU.subtract).then_inc(f_d, 1)
                    dve.wait_ge(f_sc, t * 2 + 2)
                    dve.tensor_reduce(K["var_"], vw[:].rearrange("p l (h d) -> p (l h) d", d=HV), AX.X, ALU.add
                                      ).then_inc(f_var, 1)
                    dve.wait_ge(f_std, t + 1)
                    do(dve.reciprocal(K["rs"], K["std_"]))
                    do(dve.tensor_tensor(o3, o3, wide(K["rs"]), ALU.mult))
                    dve.tensor_tensor(o[:], o[:], gate[t % 2][:], ALU.mult).then_inc(f_o, 1)

                convolve(0)
                convolve(1)
                for t in range(JT):
                    attend(t)
                    if t + 2 < JT:
                        convolve(t + 2)
                    add(t, 0)
                for m in range(1, NC):
                    add(JT - 1, m)


def rotary():
    import numpy as np

    hk = C // 2 // HEADS
    inv = (1.0 / 10000.0 ** (np.arange(0, hk, 2, dtype=np.float32) / hk)).astype(np.float32)
    a = np.arange(NB, dtype=np.float32)[:, None] * inv[None, :]
    return np.stack([np.cos(a), np.sin(a)]).astype(np.float32).reshape(1, -1)


def prepare(inputs):
    import numpy as np

    n = {k: np.asarray(v) for k, v in inputs.items()}

    def tiles(a):
        return np.ascontiguousarray(a.reshape(NB, T, NC, P).transpose(0, 2, 3, 1).reshape(NK, P, T))

    def columns(a):
        return np.ascontiguousarray(a.reshape(-1, P).T)

    names = ["L0_cond", "L0_cond2", "L1_cond", "L1_cond2"]
    return {
        "x": tiles(n["x"]),
        "f": tiles(n["fside_BxSxS_0"]),
        "condT": np.ascontiguousarray(n["cond_512"].T),
        "w": columns(np.stack([n[k + "_w"] for k in names])),
        "u": columns(np.stack([n[k + "_u"] for k in names])),
        "Wq": n["L0_attn_Wq"], "Wk": n["L0_attn_Wk"], "Wv": n["L0_attn_Wv"], "Wo": n["L0_attn_Wo"],
        "bo": columns(n["L0_attn_bo"]),
        "rw": np.ascontiguousarray(np.concatenate([n["L0_ffn_rg_w"].T, n["L0_ffn_ru_w"].T], 1)),
        "ebias": n["L0_ffn_extra_bias"].reshape(1, E), "escale": n["L0_ffn_extra_scale"].reshape(1, E),
        "SgT": np.ascontiguousarray(n["L0_ffn_Sg"].T), "SuT": np.ascontiguousarray(n["L0_ffn_Su"].T),
        "SdT": np.ascontiguousarray(n["L0_ffn_Sd"].T),
        "xprojT": np.ascontiguousarray(n["L1_attn_xproj_w"].T), "dtprojT": np.ascontiguousarray(n["L1_attn_dtproj_w"].T),
        "taps": np.ascontiguousarray(n["L1_attn_conv_w"].reshape(NC, P, 4).transpose(1, 0, 2)),
        "cvec": columns(np.stack([n["L1_attn_conv_b"], n["L1_attn_dtproj_b"], n["L1_attn_D_skip"]])).reshape(P, 3, NC),
        "alog": np.ascontiguousarray(n["L1_attn_A_log"].reshape(NC, P, NS).transpose(1, 0, 2)),
        "Wqk": np.ascontiguousarray(np.concatenate([n["L1_ffn_Wq"], n["L1_ffn_Wk"]], 1)),
        "fWv": n["L1_ffn_Wv"], "fWg": n["L1_ffn_Wg"], "fWout": n["L1_ffn_Wout"],
        "ftaps": np.ascontiguousarray(n["L1_ffn_conv_w"].reshape(NC, P, 2).transpose(1, 0, 2)),
        "fr": np.ascontiguousarray(n["L1_ffn_router_w"].reshape(C, 2).T).reshape(1, 2 * C),
        "cs": rotary(),
        "WgT": np.ascontiguousarray(n["L0_ffn_Wg"].transpose(0, 2, 1)),
        "WuT": np.ascontiguousarray(n["L0_ffn_Wu"].transpose(0, 2, 1)),
        "WdT": np.ascontiguousarray(n["L0_ffn_Wd"].transpose(0, 2, 1)),
    }


def kernel(**inputs):
    import numpy as np
    import concourse.bacc as bacc
    from concourse.bass_utils import run_bass_kernel_spmd as run

    nc = bacc.Bacc("TRN2", target_bir_lowering=False, num_devices=1)
    arrays = prepare(inputs)
    io = {k: nc.dram_tensor("in_" + k, a.shape, mybir.dt.from_np(a.dtype), kind="ExternalInput").ap()
          for k, a in arrays.items()}
    io["out"] = nc.dram_tensor("out", (NK, P, T), F32, kind="ExternalOutput").ap()
    build(nc, io)
    got = run(nc, [{"in_" + k: a for k, a in arrays.items()}], core_ids=[0]).results[0]["out"]
    return np.ascontiguousarray(got.reshape(NB, NC, P, T).transpose(0, 3, 1, 2).reshape(NB, T, C))
```

```python
from contextlib import ExitStack

import concourse.bass as bass
from concourse import mybir

F32 = mybir.dt.float32
I32 = mybir.dt.int32
U32 = mybir.dt.uint32
BF16 = mybir.dt.bfloat16
ALU = mybir.AluOpType
ACT = mybir.ActivationFunctionType
AX = mybir.AxisListType

ZERO = 1
P = 128
NB = 4
T = 512
C = 512
NC = C // P
NT = T // P
NK = NB * NC
NLAYER = 4
HEADS = 16
DH = C // HEADS
HG = P // DH
MASKED = -1.0e30
NS = 16
DTR = 128
EPS = 1e-5
E = 16
TOPK = 4
I = 352
ISH = 704
NTOK = NB * T
TT = NTOK // P
NBLK = NTOK * TOPK // P + E
WBUF = 3
ZB = 5
FIRST = NC
BESIDE = 8
LATER = NLAYER * NK - FIRST - NB * BESIDE


class Steps:

    def __init__(self, eng, sem):
        self.eng, self.sem, self.base, self.n = eng, sem, 0, 0

    def __call__(self, ins):
        ins.then_inc(self.sem, 1)
        self.n += 1
        return ins

    def sync(self):
        self.eng.wait_ge(self.sem, ZERO + self.base + self.n)

    def enter(self, i, per_iteration):
        self.outer = (self.base, self.n, per_iteration)
        self.base, self.n = self.base + self.n + i * per_iteration, 0

    def leave(self, iterations):
        base, n, per = self.outer
        assert self.n == per, (self.n, per)
        self.base, self.n = base, n + per * iterations


def build(nc, io):
    ctx = ExitStack()
    with ctx:
        fresh = []

        def sem(name, stack=None):
            fresh.append((stack or ctx).enter_context(nc.semaphore(name)))
            return fresh[-1]

        def plain_sem(name):
            return ctx.enter_context(nc.semaphore(name))

        def start():
            with nc.Block() as block:
                @block.sync
                def _(sp):
                    for s in fresh:
                        sp.sem_inc(s, ZERO)
            fresh.clear()

        def sb(name, shape, dt=F32, stack=None):
            return (stack or ctx).enter_context(nc.sbuf_tensor(name, shape, dt))

        def pair(name):
            return [sem(f"{name}0"), sem(f"{name}1")]

        def recycle(stack, held):
            with nc.Block() as block:
                @block.sync
                def _(sp):
                    for s in held:
                        sp.sem_clear(s)
            stack.close()

        X = sb("X", [P, NK * T])
        ident = sb("ident", [P, P])
        par = sb("par", [P, NLAYER * NK, 3])
        posk = sb("posk", [P, TT, TOPK], U32)
        wkk = sb("wkk", [P, TT, TOPK])
        psum = [ctx.enter_context(nc.psum_tensor(f"bank{i}", [P, T], F32)) for i in range(8)]
        Xe = nc.dram_tensor("Xe_scratch", [NBLK * P, C], F32, kind="Internal").ap()
        Ye = nc.dram_tensor("Ye_scratch", [NBLK * P, C], F32, kind="Internal").ap()
        G_dram = nc.dram_tensor("G_scratch", [NLAYER * NK, P, T], F32, kind="Internal").ap()

        wk_load = pair("wk_load")
        wk_min = pair("wk_min")
        wk_exp = pair("wk_exp")
        wk_euv = pair("wk_euv")
        wk_out = pair("wk_out")
        wk_store = pair("wk_store")
        wk_own = sem("wk_own")
        W = [{}, {}]

        def wkv_buffers(stack, phase):
            for s in range(2):
                for n in ["f", "fm", "um", "ek", "eu", "ekv", "nf", "nb", "df", "db", "p", "g"]:
                    W[s][n] = sb(f"wk{phase}_{n}{s}", [P, T], stack=stack)
                W[s]["par"] = sb(f"wk{phase}_par{s}", [P, 3], stack=stack)

        def wkv_load(sp, m, s, k):
            sp.wait_ge(wk_out[s], ZERO + m)
            sp.dma_start(W[s]["f"][:], io["f"][bass.ds(k, 1)].rearrange("a p t -> p (a t)")
                         ).then_inc(wk_load[s], 16)

        def wkv_store(sp, m, s, lk):
            sp.wait_ge(wk_out[s], ZERO + m + 1)
            sp.dma_start(G_dram[bass.ds(lk, 1)].rearrange("a p t -> p (a t)"), W[s]["g"][:]
                         ).then_inc(wk_store[s], 16)

        def wkv_scalar(act, m, s):
            w = W[s]
            act.wait_ge(wk_min[s], ZERO + 2 * m + 2)
            act.activation(w["ek"][:], w["fm"][:], ACT.Exp).then_inc(wk_exp[s], 1)
            act.activation(w["eu"][:], w["um"][:], ACT.Exp).then_inc(wk_exp[s], 1)

        def wkv_gpsimd(pool, m, s):
            w = W[s]
            pool.wait_ge(wk_exp[s], ZERO + 2 * m + 2)
            pool.tensor_tensor(w["p"][:], w["eu"][:], w["f"][:], ALU.mult).then_inc(wk_euv[s], 1)

        def wkv_vector(dve, m, s, lk, own, euv_here=False):
            w = W[s]
            own.sync()
            own(dve.tensor_copy(w["par"][:], par[:].rearrange("p a b -> p (a b)")[:, bass.ds(lk * 3, 3)]))
            decay, u, scale = (w["par"][:, j:j + 1] for j in range(3))
            yield
            dve.wait_ge(wk_load[s], ZERO + 16 * m + 16)
            dve.tensor_scalar(w["fm"][:], w["f"][:], 30.0, None, ALU.min).then_inc(wk_min[s], 1)
            own.sync()
            dve.tensor_scalar(w["um"][:], w["f"][:], u, 30.0, ALU.add, ALU.min).then_inc(wk_min[s], 1)
            yield
            dve.wait_ge(wk_exp[s], ZERO + 2 * m + 1)
            own(dve.tensor_tensor(w["ekv"][:], w["ek"][:], w["f"][:], ALU.mult))
            d = decay.to_broadcast([P, T])
            yield
            own(dve.tensor_tensor_scan(w["df"][:], d, w["ek"][:], 0.0, ALU.mult, ALU.add))
            yield
            own(dve.tensor_tensor_scan(w["db"][:, ::-1], d, w["ek"][:, ::-1], 0.0, ALU.mult, ALU.add))
            yield
            own.sync()
            own(dve.tensor_tensor_scan(w["nf"][:], d, w["ekv"][:], 0.0, ALU.mult, ALU.add))
            yield
            own(dve.tensor_tensor_scan(w["nb"][:, ::-1], d, w["ekv"][:, ::-1], 0.0, ALU.mult, ALU.add))
            yield
            own.sync()
            own(dve.scalar_tensor_tensor(w["df"][:, 0:T - 1], w["db"][:, 1:T], decay, w["df"][:, 0:T - 1],
                                         ALU.mult, ALU.add))
            yield
            own(dve.scalar_tensor_tensor(w["nf"][:, 0:T - 1], w["nb"][:, 1:T], decay, w["nf"][:, 0:T - 1],
                                         ALU.mult, ALU.add))
            dve.wait_ge(wk_exp[s], ZERO + 2 * m + 2)
            yield
            if euv_here:
                own(dve.tensor_tensor(w["p"][:], w["eu"][:], w["f"][:], ALU.mult))
            own.sync()
            own(dve.tensor_tensor(w["df"][:], w["df"][:], w["eu"][:], ALU.add))
            yield
            own.sync()
            own(dve.tensor_scalar(w["df"][:], w["df"][:], 1e-8, None, ALU.max))
            yield
            if not euv_here:
                dve.wait_ge(wk_euv[s], ZERO + m + 1)
            own(dve.tensor_tensor(w["nf"][:], w["nf"][:], w["p"][:], ALU.add))
            yield
            own.sync()
            for half in (slice(0, T // 2), slice(T // 2, T)):
                own(dve.reciprocal(w["db"][:, half], w["df"][:, half]))
                yield
            own.sync()
            dve.wait_ge(wk_store[s], ZERO + 16 * m)
            dve.scalar_tensor_tensor(w["g"][:], w["nf"][:], scale, w["db"][:], ALU.mult, ALU.mult
                                     ).then_inc(wk_out[s], 1)
            yield

        WKV_OWN = 13

        c_in = sem("c_in")
        c_x = sem("c_x")
        c_pool = sem("c_pool")
        c_act = sem("c_act")
        c_dve = sem("c_dve")
        c_pe = sem("c_pe")
        start()
        with ExitStack() as st:
            wkv_buffers(st, "c")
            wst = sb("wst", [P, NLAYER * NC], stack=st)
            ust = sb("ust", [P, NLAYER * NC], stack=st)
            condT = sb("condT", [P, NB], stack=st)
            ones = sb("ones", [P, P], stack=st)
            ew = sb("ew", [P, NLAYER * NC], stack=st)
            dcy = sb("dcy", [P, NLAYER * NC], stack=st)
            tf = sb("tf", [P, NB], stack=st)
            tfh = sb("tfh", [P, NB], stack=st)
            tfs = sb("tfs", [P, NB], stack=st)
            par5 = par[:].rearrange("p (l b c) f -> p l b c f", l=NLAYER, b=NB)
            with nc.Block() as block:
                @block.sync
                def _(sp):
                    sp.dma_start(wst[:], io["w"]).then_inc(c_in, 16)
                    sp.dma_start(ust[:], io["u"]).then_inc(c_in, 16)
                    sp.dma_start(condT[:], io["condT"]).then_inc(c_in, 16)
                    for s in range(2):
                        wkv_load(sp, 0, s, s)
                    for b in range(NB):
                        sp.dma_start(X[:, b * NC * T:(b + 1) * NC * T].rearrange("p (k t) -> p k t", k=NC),
                                     io["x"][b * NC:b * NC + NC].rearrange("k p t -> p k t")).then_inc(c_x, 16)
                        if b == 0:
                            for s in range(2):
                                wkv_store(sp, 0, s, s)
                                wkv_load(sp, 1, s, 2 + s)
                    for s in range(2):
                        wkv_store(sp, 1, s, 2 + s)
                    sp.wait_ge(c_x, ZERO + 16 * NB)
                    for s in range(2):
                        sp.wait_ge(wk_store[s], ZERO + 16 * 2)

                @block.gpsimd
                def _(pool):
                    pool.memset(ones[:], 1.0).then_inc(c_pool, 1)
                    pool.memset(ident[:], 0.0).then_inc(c_pool, 1)
                    pool.wait_ge(c_pool, ZERO + 2)
                    pool.affine_select(out=ident[:], in_=ident[:], compare_op=ALU.not_equal, fill=1.0, base=0,
                                       pattern=[[-1, P]], channel_multiplier=1).then_inc(c_pool, 1)
                    with pool.Fori(0, FIRST // 2) as i:
                        for s in range(2):
                            wkv_gpsimd(pool, i, s)

                @block.tensor
                def _(pe):
                    pe.wait_ge(c_pool, ZERO + 1)
                    pe.wait_ge(c_in, ZERO + 48)
                    pe.matmul(psum[0][:, 0:NB], ones[:], condT[:], start=True, stop=True).then_inc(c_pe, 1)

                @block.scalar
                def _(act):
                    act.wait_ge(c_pe, ZERO + 1)
                    act.activation(tf[:], psum[0][:, 0:NB], ACT.Sigmoid).then_inc(c_act, 1)
                    act.activation(ew[:], wst[:], ACT.Exp).then_inc(c_act, 1)
                    act.wait_ge(c_act, ZERO + 2)
                    act.activation(dcy[:], ew[:], ACT.Exp, scale=-1.0).then_inc(c_act, 1)
                    with act.Fori(0, FIRST // 2) as i:
                        for s in range(2):
                            wkv_scalar(act, i, s)

                @block.vector
                def _(dve):
                    own = Steps(dve, c_dve)
                    dve.wait_ge(c_act, ZERO + 3)
                    dve.wait_ge(c_in, ZERO + 48)
                    own(dve.tensor_scalar(tfh[:], tf[:], 0.5, 0.5, ALU.mult, ALU.add))
                    own(dve.tensor_scalar(tfs[:], tf[:], 0.2, 0.8, ALU.mult, ALU.add))
                    own.sync()
                    view = [x[:].rearrange("p (l c) -> p l c", l=NLAYER) for x in (dcy, ust)]
                    for b in range(NB):
                        own(dve.tensor_scalar(par5[:, :, b, :, 0], view[0], tfh[:, b:b + 1], None, ALU.mult))
                        own(dve.tensor_copy(par5[:, :, b, :, 1], view[1]))
                        own(dve.tensor_scalar(par5[:, :, b, :, 2], view[0], 0.0, tfs[:, b:b + 1], ALU.mult, ALU.add))
                    own.sync()
                    wk = Steps(dve, wk_own)
                    with dve.Fori(0, FIRST // 2) as i:
                        wk.enter(i, 2 * WKV_OWN)
                        for s in range(2):
                            for _ in wkv_vector(dve, i, s, i * 2 + s, wk):
                                pass
                        wk.leave(FIRST // 2)

        stage, held = ExitStack(), []

        def stage_sem(name):
            held.append(sem(name, stage))
            return held[-1]
        attention(nc, io, {**locals(), "sem": stage_sem, "pair": lambda n: [stage_sem(n + "0"), stage_sem(n + "1")]})
        recycle(stage, held)
        experts(nc, io, locals())
        state_space(nc, io, locals())
        linear_attention(nc, io, locals())


def attention(nc, io, g):
    sb, sem, pair, X, ident, psum, G_dram = (g[k] for k in ("sb", "sem", "pair", "X", "ident", "psum", "G_dram"))
    wk_own = g["wk_own"]
    SB = 3
    ps_s, ps_t, ps_p, ps_c = psum[0:SB], psum[3], psum[4:6], psum[6:8]
    STEPS = HEADS * NT
    uses = [len(range(k, STEPS, SB)) for k in range(SB)]
    NZ = NBLK // ZB // NB
    AHEAD = 2
    PACE = STEPS // (BESIDE - AHEAD)
    PIECES = 15
    with ExitStack() as st:
        g["wkv_buffers"](st, "a")
        zeros = sb("zeros", [P, C], stack=st)
        wq, wk, wv, wo = (sb(f"at_w{n}", [P, NC, C], stack=st) for n in "qkvo")
        bo = sb("bo", [P, NC], stack=st)
        mask = sb("mask", [P, P], stack=st)
        mask16 = sb("mask16", [P, P], BF16, stack=st)
        ident16 = sb("ident16", [P, P], BF16, stack=st)
        gt = sb("gt", [P, NC * T], stack=st)
        r = sb("at_r", [P, NC, T], stack=st)
        qT = [sb(f"qT{s}", [P, HG, T], stack=st) for s in range(2)]
        kT = [sb(f"kT{s}", [P, T], stack=st) for s in range(2)]
        v = sb("v", [P, NT, C], stack=st)
        prob = [sb(f"prob{k}", [P, T], stack=st) for k in range(SB)]
        probT = [sb(f"probT{s}", [P, NT, P], stack=st) for s in range(2)]
        cn = sb("cn", [P, NT, HG, DH], stack=st)
        cT = sb("cT", [P, NC, T], stack=st)
        nmax = [sb(f"nmax{k}", [P, 1], stack=st) for k in range(SB)]
        rsum = [sb(f"rsum{s}", [P, NT, HG], stack=st) for s in range(2)]
        rinv = sb("rinv", [P, NT, HG], stack=st)
        a_z = sem("a_z")
        a_w = [sem(f"a_w{n}") for n in "vqko"]
        a_bo = sem("a_bo")
        a_mask = sem("a_mask")
        a_m16 = sem("a_m16")
        a_g = sem("a_g")
        a_sig = sem("a_sig")
        a_r = sem("a_r")
        a_pr = pair("a_pr")
        a_pf = pair("a_pf")
        a_s, a_nm, a_exp = (
            [sem(f"{n}{k}") for k in range(SB)] for n in ("a_s", "a_nm", "a_exp"))
        a_t = sem("a_t")
        a_te = sem("a_te")
        a_pv = sem("a_pv")
        a_ri = sem("a_ri")
        a_cn = sem("a_cn")
        use_v, use_q, use_k, use_t, use_o = (
            [0, 1, 2, 3], [4, 6, 9, 12], [5, 7, 10, 13], [8, 11, 14, 15], [16, 17, 18, 19])
        USES = 20 // 2
        g["start"]()
        with nc.Block() as block:
            @block.sync
            def _(sp):
                def load_g(k):
                    sp.dma_start(gt[:].rearrange("p (c t) -> p c t", c=NC),
                                 G_dram[k:k + NC].rearrange("c p t -> p c t")).then_inc(a_g, 16)
                load_g(0)
                for j in range(2):
                    g["wkv_load"](sp, FIRST // 2, j, (FIRST + j) % NK)
                for i, (w, n) in enumerate(((wv, "Wv"), (wq, "Wq"), (wk, "Wk"), (wo, "Wo"))):
                    sp.dma_start(w[:], io[n].rearrange("(c p) n -> p c n", p=P)).then_inc(a_w[i], 16)
                sp.dma_start(bo[:], io["bo"]).then_inc(a_bo, 16)
                sp.wait_ge(a_mask, ZERO + 5)
                for b in range(NB):
                    first, m = FIRST + b * BESIDE, (FIRST + b * BESIDE) // 2
                    for n in range(b * NZ, b * NZ + NZ):
                        sp.dma_start(g["Xe"][n * ZB * P:(n + 1) * ZB * P].rearrange("(a p) d -> p a d", p=P),
                                     zeros[:].rearrange("p (a d) -> p a d", a=1).to_broadcast([P, ZB, C])
                                     ).then_inc(a_z, 16)
                    for j in range(BESIDE):
                        g["wkv_store"](sp, m + j // 2, j % 2, first + j)
                        if j + 2 < BESIDE or b + 1 < NB:
                            g["wkv_load"](sp, m + j // 2 + 1, j % 2, (first + j + 2) % NK)
                        if j == NC and b + 1 < NB:
                            for p in range(2):
                                sp.wait_ge(g["wk_store"][p], ZERO + 16 * (m + 2))
                            sp.wait_ge(a_r, ZERO + b + 1)
                            load_g((b + 1) * NC)
                sp.wait_ge(a_z, ZERO + 16 * (NBLK // ZB))
                for s in range(2):
                    sp.wait_ge(g["wk_store"][s], ZERO + 16 * (FIRST + NB * BESIDE) // 2)

            @block.gpsimd
            def _(pool):
                pool.memset(mask[:], 0.0).then_inc(a_mask, 1)
                pool.memset(zeros[:], 0.0).then_inc(a_mask, 1)
                for j in range(2):
                    pool.memset(qT[j][:], 0.0).then_inc(a_mask, 1)
                pool.wait_ge(a_mask, ZERO + 4)
                pool.affine_select(out=mask[:], in_=mask[:], compare_op=ALU.is_ge, fill=MASKED, base=0,
                                   pattern=[[-1, P]], channel_multiplier=1).then_inc(a_mask, 1)
                with pool.Fori(0, NB) as b:
                    for j in range(BESIDE):
                        g["wkv_gpsimd"](pool, FIRST // 2 + b * (BESIDE // 2) + j // 2, j % 2)

            @block.tensor
            def _(pe):
                def project(b, use, lhs, rhs):
                    p = use % 2
                    pe.wait_ge(a_pf[p], ZERO + b * USES + use // 2)
                    for c in range(NC):
                        mm = pe.matmul(ps_p[p][:], lhs(c), rhs(c), start=c == 0, stop=c == NC - 1)
                    mm.then_inc(a_pr[p], 1)

                def project_qk(b, hg, part):
                    cols = slice(hg * P, hg * P + P)
                    use, w = ((use_q[hg], wq), (use_k[hg], wk))[part]
                    project(b, use, lambda c: w[:, c, cols], lambda c: r[:, c, :])

                def scores(b, s):
                    hg, hh, qt, k = s // 16, s // 4 % 4, s % 4, s % SB
                    if s % 16 == 0:
                        for use in (use_q[hg], use_k[hg]):
                            pe.wait_ge(a_pf[use % 2], ZERO + b * USES + use // 2 + 1)
                    pe.wait_ge(a_exp[k], ZERO + b * uses[k] + s // SB)
                    n = (qt + 1) * P
                    pe.matmul(ps_s[k][:, 0:n], qT[hg % 2][:, hh, qt * P:n], kT[hg % 2][:, 0:n],
                              start=True, stop=True)
                    pe.matmul(ps_s[k][:, qt * P:n], ident16[:], mask16[:], start=False, stop=True,
                              skip_group_check=True).then_inc(a_s[k], 1)

                def transposes(b, s):
                    qt, k = s % 4, s % SB
                    pe.wait_ge(a_exp[k], ZERO + b * uses[k] + s // SB + 1)
                    pe.wait_ge(a_te, ZERO + b * STEPS + s)
                    for kb in range(qt + 1):
                        mm = pe.transpose(ps_t[:, kb * P:kb * P + P], prob[k][:, kb * P:kb * P + P], ident[:])
                    mm.then_inc(a_t, 1)

                def context(b, s):
                    hg, hh, qt, p = s // 16, s // 4 % 4, s % 4, s % 2
                    pe.wait_ge(a_te, ZERO + b * STEPS + s + 1)
                    if s % 16 == 0:
                        if hg >= 2:
                            pe.wait_ge(a_cn, ZERO + b * NC + hg - 1)
                        else:
                            pe.wait_ge(a_cn, ZERO + b * NC)
                    at = qt * P + hh * DH
                    for kb in range(qt + 1):
                        mm = pe.matmul(ps_c[hg % 2][:, at:at + DH], probT[p][:, kb, :],
                                       v[:, kb, (hg * HG + hh) * DH:(hg * HG + hh + 1) * DH],
                                       start=kb == 0, stop=kb == qt, skip_group_check=True)
                    mm.then_inc(a_pv, 1)

                def turn(b, hg):
                    use = use_t[hg]
                    pe.wait_ge(a_cn, ZERO + b * NC + hg + 1)
                    pe.wait_ge(a_pf[use % 2], ZERO + b * USES + use // 2)
                    for qt in range(NT):
                        mm = pe.transpose(ps_p[use % 2][:, qt * P:qt * P + P],
                                          cn[:, qt].rearrange("p h d -> p (h d)"), ident[:])
                    mm.then_inc(a_pr[use % 2], 1)

                def row(b):
                    pe.wait_ge(a_r, ZERO + b + 1)
                    pe.wait_ge(a_w[0], ZERO + 16)
                    for tt in range(NT):
                        project(b, use_v[tt], lambda c: r[:, c, tt * P:tt * P + P], lambda c: wv[:, c, :])
                    for part in range(2):
                        pe.wait_ge(a_w[1 + part], ZERO + 16)
                        project_qk(b, 0, part)
                    for s in range(STEPS + 4):
                        if s < STEPS:
                            scores(b, s)
                        if 2 <= s < STEPS + 2:
                            transposes(b, s - 2)
                        if s >= 4:
                            context(b, s - 4)
                        if s % 16 == 7 and s > 16:
                            turn(b, s // 16 - 1)
                        if s % 16 in (8, 10) and s // 16 + 1 < NC:
                            project_qk(b, s // 16 + 1, s % 16 // 10)
                    turn(b, NC - 1)
                    use = use_t[NC - 1]
                    pe.wait_ge(a_pf[use % 2], ZERO + b * USES + use // 2 + 1)
                    pe.wait_ge(a_w[3], ZERO + 16)
                    for m in range(NC):
                        project(b, use_o[m], lambda c: wo[:, c, m * P:m * P + P], lambda c: cT[:, c, :])

                pe.wait_ge(a_m16, ZERO + 2)
                with pe.Fori(0, NB) as b:
                    row(b)

            @block.scalar
            def _(act):
                def evict(b, use, out, scale=1.0):
                    act.wait_ge(a_pr[use % 2], ZERO + b * USES + use // 2 + 1)
                    act.activation(out, ps_p[use % 2][:], ACT.Copy, scale=scale).then_inc(a_pf[use % 2], 1)

                def evict_q(b, hg):
                    use = use_q[hg]
                    act.wait_ge(a_pr[use % 2], ZERO + b * USES + use // 2 + 1)
                    for hh in range(HG):
                        rows = slice(hh * DH, hh * DH + DH)
                        ins = act.activation(qT[hg % 2][rows, hh, :], ps_p[use % 2][rows, :], ACT.Copy,
                                             scale=float(DH) ** -0.5)
                    ins.then_inc(a_pf[use % 2], 1)

                def evict_k(b, hg):
                    evict(b, use_k[hg], kT[hg % 2][:])

                def wkv(b, j):
                    g["wkv_scalar"](act, FIRST // 2 + b * (BESIDE // 2) + j // 2, j % 2)

                def sigmoid(b):
                    act.activation(r[:].rearrange("p c t -> p (c t)"), X[:, bass.ds(b * NC * T, NC * T)], ACT.Sigmoid
                                   ).then_inc(a_sig, 1)

                def row(b, last=False):
                    for j in range(AHEAD):
                        wkv(b, j)
                    for tt in range(NT):
                        evict(b, use_v[tt], v[:, tt, :])
                    evict_q(b, 0)
                    evict_k(b, 0)
                    for s in range(STEPS + 3):
                        if 2 <= s < STEPS + 2:
                            n = (s - 2) % NT + 1
                            act.wait_ge(a_t, ZERO + b * STEPS + s - 1)
                            act.wait_ge(a_pv, ZERO + b * STEPS + max(s - 3, 0))
                            act.activation(probT[s % 2][:, 0:n, :].rearrange("p k q -> p (k q)"),
                                           ps_t[:, 0:n * P], ACT.Copy).then_inc(a_te, 1)
                        if s < STEPS:
                            qt, k, n = s % NT, s % SB, (s % NT + 1) * P
                            act.wait_ge(a_nm[k], ZERO + b * uses[k] + s // SB + 1)
                            act.wait_ge(a_t, ZERO + b * STEPS + max(s - SB + 1, 0))
                            act.activation(prob[k][:, 0:n], ps_s[k][:, 0:n], ACT.Exp, bias=nmax[k][:],
                                           accum_out=rsum[s // 16 % 2][:, qt, s // NT % HG:s // NT % HG + 1]
                                           ).then_inc(a_exp[k], 1)
                        if s % PACE == 1 and s // PACE < BESIDE - AHEAD:
                            wkv(b, s // PACE + AHEAD)
                        if s % 16 == 8 and s > 16:
                            evict(b, use_t[s // 16 - 1], cT[:, s // 16 - 1, :])
                        if s % 16 == 10 and s // 16 + 1 < NC:
                            evict_q(b, s // 16 + 1)
                        if s % 16 == 12 and s // 16 + 1 < NC:
                            evict_k(b, s // 16 + 1)
                        if s == 46 and not last:
                            sigmoid(b + 1)
                    evict(b, use_t[NC - 1], cT[:, NC - 1, :])

                sigmoid(0)
                act.wait_ge(a_mask, ZERO + 5)
                with act.Fori(0, NB - 1) as b:
                    row(b)
                row(NB - 1, last=True)

            @block.vector
            def _(dve):
                own = Steps(dve, wk_own)
                own.n = FIRST * g["WKV_OWN"]

                def gated(b):
                    dve.wait_ge(a_g, ZERO + b * 16 + 16)
                    dve.wait_ge(a_sig, ZERO + b + 1)
                    dve.tensor_tensor(r[:].rearrange("p c t -> p (c t)"), r[:].rearrange("p c t -> p (c t)"), gt[:],
                                      ALU.mult).then_inc(a_r, 1)

                def tile(b, j):
                    return g["wkv_vector"](dve, FIRST // 2 + b * (BESIDE // 2) + j // 2, j % 2,
                                           FIRST + b * BESIDE + j, own)

                def due(steps):
                    return (PIECES - 2) * steps // (PACE - 2)

                def normalise(b, hg):
                    dve.wait_ge(a_pv, ZERO + b * STEPS + (hg + 1) * NT * HG)
                    dve.reciprocal(rinv[:], rsum[hg % 2][:]).then_inc(a_ri, 1)
                    before = use_t[hg - 1]
                    if hg:
                        dve.wait_ge(a_pr[before % 2], ZERO + b * USES + before // 2 + 1)
                    dve.wait_ge(a_ri, ZERO + b * NC + hg + 1)
                    dve.tensor_tensor(cn[:], ps_c[hg % 2][:].rearrange("p (q h d) -> p q h d", q=NT, h=HG),
                                      rinv[:].rearrange("p q (h o) -> p q h o", o=1).to_broadcast([P, NT, HG, DH]),
                                      ALU.mult).then_inc(a_cn, 1)

                def row(b, last=False):
                    ahead = [tile(b, j) for j in range(AHEAD)]
                    for pieces in ahead:
                        next(pieces)
                        next(pieces)
                    for pieces in ahead:
                        for _ in pieces:
                            pass
                    beside = None
                    for s in range(STEPS):
                        k, n = s % SB, (s % NT + 1) * P
                        dve.wait_ge(a_s[k], ZERO + b * uses[k] + s // SB + 1)
                        dve.tensor_reduce(nmax[k][:], ps_s[k][:, 0:n], AX.X, ALU.max, negate=True
                                          ).then_inc(a_nm[k], 1)
                        if s % 16 == 5 and s > 16:
                            normalise(b, s // 16 - 1)
                        if s // PACE < BESIDE - AHEAD:
                            at = s % PACE
                            if at == 0:
                                beside = tile(b, s // PACE + AHEAD)
                                now = 2
                            elif at == 1:
                                now = 0
                            else:
                                now = due(at - 1) - due(at - 2)
                            for _ in range(now):
                                next(beside)
                        if s == 50 and not last:
                            gated(b + 1)
                    normalise(b, NC - 1)
                    for m in range(NC):
                        use = use_o[m]
                        dve.wait_ge(a_pr[use % 2], ZERO + b * USES + use // 2 + 1)
                        xk = X[:, bass.ds((b * NC + m) * T, T)]
                        dve.scalar_tensor_tensor(xk, ps_p[use % 2][:], bo[:, m:m + 1], xk, ALU.add, ALU.add
                                                 ).then_inc(a_pf[use % 2], 1)

                gated(0)
                dve.wait_ge(a_mask, ZERO + 5)
                dve.tensor_copy(mask16[:], mask[:]).then_inc(a_m16, 1)
                dve.tensor_copy(ident16[:], ident[:]).then_inc(a_m16, 1)
                dve.wait_ge(a_bo, ZERO + 16)
                with dve.Fori(0, NB - 1) as b:
                    own.enter(b, BESIDE * g["WKV_OWN"])
                    row(b)
                    own.leave(NB - 1)
                row(NB - 1, last=True)


def experts(nc, io, g):
    sb, sem, pair, X, ident, psum, G_dram = (g[k] for k in ("sb", "sem", "pair", "X", "ident", "psum", "G_dram"))
    Xe, Ye, posk, wkk = (g[k] for k in ("Xe", "Ye", "posk", "wkk"))
    SJ = [(0, 128), (128, 128), (256, 128), (384, 128), (512, 96), (608, 96)]
    NSJ = len(SJ)
    with ExitStack() as keep:
        endm = sb("endm", [P, E + WBUF], I32, stack=keep)
        slot = sb("slot", [P, NBLK], I32, stack=keep)
        wload = sb("wload", [P, NBLK], I32, stack=keep)
        m_in = sem("m_in")
        m_sh = sem("m_sh")
        m_g = [sem(f"m_g{b}") for b in range(NB)]
        m_sig = sem("m_sig")
        m_r = sem("m_r")
        m_t = pair("m_t")
        m_te = pair("m_te")
        m_lg = sem("m_lg")
        m_c = sem("m_c")
        m_act = sem("m_act")
        m_d = sem("m_d")
        m_M = sem("m_M")
        m_pre = sem("m_pre")
        m_pos = sem("m_pos")
        m_sc = g["plain_sem"]("m_sc")
        s_gu, s_sl, s_h, s_y, s_yf = (pair(n) for n in ("s_gu", "s_sl", "s_h", "s_y", "s_yf"))
        b_x, b_tx, b_xt, b_gate, b_gu, b_sl, b_h, b_st = (
            pair(n) for n in ("b_x", "b_tx", "b_xt", "b_gate", "b_gu", "b_sl", "b_h", "b_st"))
        b_ht, b_hte, b_y, b_ye = (sem(n) for n in ("b_ht", "b_hte", "b_y", "b_ye"))
        b_w = g["plain_sem"]("b_w")
        g["start"]()
        with ExitStack() as st:
            R = sb("m_R", [P, NK, T], stack=st)
            rtok = sb("rtok", [P, TT, C], stack=st)
            sig = [sb(f"m_sig{j}", [P, NC * T], stack=st) for j in range(2)]
            rw = sb("rw", [P, NC, 2 * E], stack=st)
            ebias = sb("ebias", [P, E], stack=st)
            escale = sb("escale", [P, E], stack=st)
            sg = sb("sg", [P, NC, ISH], stack=st)
            su = sb("su", [P, NC, ISH], stack=st)
            sd = sb("sd", [P, NSJ, C], stack=st)
            ssl = [sb(f"ssl{s}", [P, T], stack=st) for s in range(2)]
            suu = [sb(f"suu{s}", [P, T], stack=st) for s in range(2)]
            hsh = sb("hsh", [P, NSJ, T], stack=st)
            before = sb("before", [P, P], stack=st)
            ones = sb("m_ones", [P, P], stack=st)
            lower = sb("lower", [P, E, E], stack=st)
            fresh = sb("fresh", [P, E, TT], stack=st)
            blk = sb("blk", [P, NBLK], stack=st)
            big = [sb(f"big{j}", [P, TT, E, E], BF16, stack=st) for j in range(2)]
            small = {n: sb(f"rt_{n}", [P, TT, E], stack=st) for n in
                     ("sl", "s", "ex", "pr", "bi", "rank", "M", "Wt", "tot", "inc", "pos", "t0", "t1")}
            row = {n: sb(f"rr_{n}", [P, E], stack=st) for n in ("nb", "end", "base", "c")}
            rowi = sb("rowi", [P, E], I32, stack=st)
            rt1 = {n: sb(f"r1_{n}", [P, TT], stack=st) for n in ("m", "sum", "ri")}
            ended = sb("ended", [P, NBLK, E], BF16, stack=st)
            ej = sb("ej", [P, NBLK], stack=st)
            eji = sb("eji", [P, NBLK], I32, stack=st)
            third = sb("third", [P, NBLK], I32, stack=st)
            ps_t, ps_l, ps_pre = psum[0:2], psum[2], psum[3]
            ps_g, ps_u, ps_y = psum[4:6], psum[6:8], psum[0:2]
            with nc.Block() as block:
                @block.sync
                def _(sp):
                    def load_g(b):
                        sp.dma_start(R[:, b * NC:b * NC + NC, :],
                                     G_dram[NK + b * NC:NK + b * NC + NC].rearrange("c p t -> p c t")
                                     ).then_inc(m_g[b], 16)
                    load_g(0)
                    sp.dma_start(sg[:], io["SgT"].rearrange("(c p) n -> p c n", p=P)).then_inc(m_sh, 16)
                    sp.dma_start(su[:], io["SuT"].rearrange("(c p) n -> p c n", p=P)).then_inc(m_sh, 16)
                    sp.dma_start(sd[:, 0:4, :], io["SdT"][0:4 * P].rearrange("(c p) n -> p c n", p=P)
                                 ).then_inc(m_sh, 16)
                    sp.dma_start(sd[0:96, 4:6, :], io["SdT"][4 * P:ISH].rearrange("(c p) n -> p c n", p=96)
                                 ).then_inc(m_sh, 16)
                    sp.dma_start(rw[:], io["rw"].rearrange("(c p) e -> p c e", p=P)).then_inc(m_in, 16)
                    sp.dma_start(ebias[:], io["ebias"].to_broadcast([P, E])).then_inc(m_in, 16)
                    sp.dma_start(escale[:], io["escale"].to_broadcast([P, E])).then_inc(m_in, 16)
                    for b in range(1, NB):
                        load_g(b)

                @block.gpsimd
                def _(pool):
                    pool.memset(before[:], 1.0).then_inc(m_c, 1)
                    pool.memset(ones[:], 1.0).then_inc(m_c, 1)
                    pool.memset(lower[:], 1.0).then_inc(m_c, 1)
                    pool.memset(fresh[:], 1.0).then_inc(m_c, 1)
                    pool.memset(endm[:], 0).then_inc(m_c, 1)
                    pool.iota(blk[:], pattern=[[1, NBLK]], base=0, channel_multiplier=0,
                              allow_small_or_imprecise_dtypes=True).then_inc(m_c, 1)
                    pool.wait_ge(m_c, ZERO + 6)
                    pool.affine_select(out=before[:], in_=before[:], compare_op=ALU.is_gt, fill=0.0, base=0,
                                       pattern=[[1, P]], channel_multiplier=-1).then_inc(m_c, 1)
                    pool.affine_select(out=lower[:], in_=lower[:], compare_op=ALU.is_gt, fill=0.0, base=0,
                                       pattern=[[1, E], [-1, E]], channel_multiplier=0).then_inc(m_c, 1)
                    pool.affine_select(out=fresh[:], in_=fresh[:], compare_op=ALU.is_gt, fill=0.0, base=0,
                                       pattern=[[0, E], [1, TT]], channel_multiplier=0).then_inc(m_c, 1)

                    def shared(base):
                        for j in range(NSJ):
                            m, (_, n) = base + j // 2, SJ[j]
                            pool.wait_ge(s_sl[j % 2], ZERO + 2 * m + 2)
                            if j == 0:
                                pool.wait_ge(m_c, ZERO + 9)
                            pool.tensor_tensor(hsh[0:n, j, :], ssl[j % 2][0:n, :], suu[j % 2][0:n, :], ALU.mult
                                               ).then_inc(s_h[j % 2], 1)
                    with pool.Fori(0, NB // 2) as b:
                        shared(b * (NSJ // 2))
                    pool.wait_ge(m_pos, ZERO + 1)
                    for p in range(2):
                        pool.wait_ge(m_te[p], ZERO + TT // 2)
                    for t in range(TT):
                        for k in range(TOPK):
                            pool.indirect_dma_start(
                                out=Xe, out_offset=bass.IndirectOffsetOnAxis(ap=posk[:, t, k:k + 1], axis=0),
                                in_=rtok[:, t, :], in_offset=None, bounds_check=NBLK * P - 1, oob_is_err=False
                            ).then_inc(m_sc, 16)
                    pool.wait_ge(m_sc, 16 * TT * TOPK)

                @block.tensor
                def _(pe):
                    def shared(b, base):
                        for j, (at, n) in enumerate(SJ):
                            p, m = j % 2, base + j // 2
                            pe.wait_ge(s_h[p], ZERO + m)
                            for ps, w in ((ps_g[p], sg), (ps_u[p], su)):
                                for c in range(NC):
                                    mm = pe.matmul(ps[0:n, :], w[:, c, at:at + n], rview(b, c),
                                                   start=c == 0, stop=c == NC - 1)
                            mm.then_inc(s_gu[p], 1)
                        for p in range(2):
                            pe.wait_ge(s_h[p], ZERO + base + NSJ // 2)
                        for c in range(NC):
                            p = c % 2
                            pe.wait_ge(s_yf[p], ZERO + b * 2 + c // 2)
                            for j, (at, n) in enumerate(SJ):
                                mm = pe.matmul(ps_y[p][:], sd[0:n, j, c * P:c * P + P], hsh[0:n, j, :],
                                               start=j == 0, stop=j == NSJ - 1)
                            mm.then_inc(s_y[p], 1)

                    def rview(b, c):
                        return R[:].rearrange("p k t -> p (k t)")[:, bass.ds((b * NC + c) * T, T)]

                    pe.wait_ge(m_r, ZERO + 1)
                    pe.wait_ge(m_sh, ZERO + 64)
                    shared(0, 0)
                    pe.wait_ge(m_in, ZERO + 48)
                    for t in range(TT):
                        b, tt, p = t // NT, t % NT, t % 2
                        cols = slice(tt * P, tt * P + P)
                        pe.wait_ge(m_r, ZERO + b + 1)
                        if t >= 2:
                            pe.wait_ge(m_te[p], ZERO + t // 2)
                        else:
                            pe.wait_ge(s_yf[p], ZERO + NC // 2)
                        for c in range(NC):
                            mm = pe.transpose(ps_t[p][:, c * P:c * P + P], R[:, b * NC + c, cols], ident[:])
                        mm.then_inc(m_t[p], 1)
                        for c in range(NC):
                            mm = pe.matmul(ps_l[:, t * 2 * E:(t + 1) * 2 * E], R[:, b * NC + c, cols], rw[:, c, :],
                                           start=c == 0, stop=c == NC - 1)
                    mm.then_inc(m_lg, 1)
                    pe.wait_ge(m_te[0], ZERO + TT // 2)
                    pe.wait_ge(m_te[1], ZERO + TT // 2)
                    shared(1, NSJ // 2)
                    pe.wait_ge(m_M, ZERO + 1)
                    pe.wait_ge(m_c, ZERO + 9)
                    M = small["M"][:].rearrange("p t e -> p (t e)")
                    pe.matmul(ps_pre[:, 0:TT * E], before[:], M, start=True, stop=True)
                    pe.matmul(ps_pre[:, TT * E:2 * TT * E], ones[:], M, start=True, stop=True).then_inc(m_pre, 1)
                    with pe.Fori(2, NB) as b:
                        shared(b, b * (NSJ // 2))

                @block.scalar
                def _(act):
                    for b in range(NB):
                        if b >= 2:
                            act.wait_ge(m_r, ZERO + b - 1)
                        act.activation(sig[b % 2][:], X[:, b * NC * T:(b + 1) * NC * T], ACT.Sigmoid
                                       ).then_inc(m_sig, 1)

                    def shared(b, copies):
                        for j, (_, n) in enumerate(SJ):
                            p, m = j % 2, b * (NSJ // 2) + j // 2
                            act.wait_ge(s_gu[p], ZERO + m + 1)
                            act.activation(ssl[p][0:n, :], ps_g[p][0:n, :], ACT.Silu).then_inc(s_sl[p], 1)
                            if copies:
                                act.activation(suu[p][0:n, :], ps_u[p][0:n, :], ACT.Copy).then_inc(s_sl[p], 1)
                    shared(0, True)
                    for t in range(TT):
                        p = t % 2
                        act.wait_ge(m_t[p], ZERO + t // 2 + 1)
                        act.activation(rtok[:, t, :], ps_t[p][:], ACT.Copy).then_inc(m_te[p], 1)
                    act.wait_ge(m_lg, ZERO + 1)
                    act.activation(small["sl"][:], ps_l[:].rearrange("p (t e) -> p t e", t=TT)[:, :, 0:E], ACT.Silu
                                   ).then_inc(m_act, 1)
                    act.wait_ge(m_d, ZERO + 1)
                    act.activation(small["ex"][:], small["s"][:], ACT.Exp).then_inc(m_act, 1)
                    shared(1, True)
                    with act.Fori(NB // 2, NB) as b:
                        shared(b, False)

                @block.vector
                def _(dve):
                    own = Steps(dve, g["wk_own"])
                    own.n = (FIRST + NB * BESIDE) * g["WKV_OWN"]

                    def do(ins):
                        own(ins)
                        own.sync()

                    for b in range(NB):
                        xb = R[:].rearrange("p k t -> p (k t)")[:, b * NC * T:(b + 1) * NC * T]
                        dve.wait_ge(m_g[b], ZERO + 16)
                        dve.wait_ge(m_sig, ZERO + b + 1)
                        dve.tensor_tensor(xb, xb, sig[b % 2][:], ALU.mult).then_inc(m_r, 1)
                    S = {k: v[:] for k, v in small.items()}
                    flat = {k: v[:].rearrange("p t e -> p (t e)") for k, v in small.items()}

                    def over_e(a):
                        return a[:].rearrange("p (t o) -> p t o", o=1).to_broadcast([P, TT, E])

                    def over_t(a):
                        return a[:].rearrange("p (o e) -> p o e", o=1).to_broadcast([P, TT, E])

                    def add_shared(b):
                        for c in range(NC):
                            p = c % 2
                            dve.wait_ge(s_y[p], ZERO + b * 2 + c // 2 + 1)
                            xk = X[:, bass.ds((b * NC + c) * T, T)]
                            dve.tensor_tensor(xk, xk, ps_y[p][:], ALU.add).then_inc(s_yf[p], 1)
                    add_shared(0)
                    dve.wait_ge(m_act, ZERO + 1)
                    do(dve.tensor_tensor(S["s"], ps_l[:].rearrange("p (t e) -> p t e", t=TT)[:, :, E:2 * E], S["sl"],
                                         ALU.mult))
                    do(dve.scalar_tensor_tensor(flat["t0"], flat["s"], -1.0, flat["s"], ALU.mult, ALU.max))
                    do(dve.tensor_reduce(rt1["m"][:], S["t0"], AX.X, ALU.max))
                    dve.tensor_tensor(S["s"], S["t0"], over_e(rt1["m"]), ALU.subtract).then_inc(m_d, 1)
                    dve.wait_ge(m_act, ZERO + 2)
                    do(dve.tensor_reduce(rt1["sum"][:], S["ex"], AX.X, ALU.add))
                    do(dve.reciprocal(rt1["ri"][:], rt1["sum"][:]))
                    do(dve.tensor_tensor(S["pr"], S["ex"], over_e(rt1["ri"]), ALU.mult))
                    dve.wait_ge(m_in, ZERO + 48)
                    own(dve.tensor_tensor(S["bi"], S["pr"], over_t(ebias), ALU.add))
                    do(dve.tensor_tensor(S["t0"], S["pr"], over_t(escale), ALU.mult))
                    own(dve.tensor_scalar(flat["Wt"], flat["t0"], 1.0, None, ALU.add))
                    this = S["bi"].rearrange("p t (e o) -> p t e o", o=1).to_broadcast([P, TT, E, E])
                    other = S["bi"].rearrange("p t (o e) -> p t o e", o=1).to_broadcast([P, TT, E, E])
                    low = lower[:].rearrange("p (o e) f -> p o e f", o=1).to_broadcast([P, TT, E, E])
                    do(dve.tensor_tensor(big[0][:], other, this, ALU.is_equal))
                    dve.wait_ge(m_c, ZERO + 9)
                    own(dve.tensor_tensor(big[0][:], big[0][:], low, ALU.mult))
                    do(dve.tensor_tensor(big[1][:], other, this, ALU.is_gt))
                    do(dve.tensor_tensor(big[0][:], big[0][:], big[1][:], ALU.add))
                    own(dve.tensor_reduce(flat["rank"], big[0][:].rearrange("p t e f -> p (t e) f"), AX.X, ALU.add))
                    own.sync()
                    dve.tensor_scalar(flat["M"], flat["rank"], TOPK - 0.5, None, ALU.is_lt).then_inc(m_M, 1)
                    add_shared(1)
                    dve.wait_ge(m_pre, ZERO + 1)
                    tot_et = small["tot"][:].rearrange("p a b -> p (a b)").rearrange("p (e t) -> p e t", e=E)
                    own(dve.tensor_copy(tot_et, ps_pre[:, TT * E:2 * TT * E].rearrange("p (t e) -> p e t", t=TT)))
                    own.sync()
                    do(dve.tensor_tensor_scan(flat["inc"], fresh[:].rearrange("p e t -> p (e t)"), flat["tot"], 0.0,
                                              ALU.mult, ALU.add))
                    inc_et = flat["inc"].rearrange("p (e t) -> p e t", e=E)
                    do(dve.tensor_scalar(rowi[:], inc_et[:, :, TT - 1], float(P - 1), None, ALU.add))
                    do(dve.tensor_scalar(rowi[:], rowi[:], 7, None, ALU.arith_shift_right))
                    do(dve.tensor_scalar(row["nb"][:], rowi[:], 1.0, None, ALU.max))
                    own(dve.tensor_tensor_scan(row["end"][:], ones[:, 0:E], row["nb"][:], 0.0, ALU.mult, ALU.add))
                    do(dve.tensor_tensor(flat["t0"], flat["inc"], flat["tot"], ALU.subtract))
                    do(dve.tensor_tensor(row["c"][:], row["end"][:], row["nb"][:], ALU.subtract))
                    do(dve.tensor_scalar(row["base"][:], row["c"][:], float(P), None, ALU.mult))
                    do(dve.tensor_tensor(S["t1"], flat["t0"].rearrange("p (e t) -> p t e", e=E), over_t(row["base"]),
                                         ALU.add))
                    do(dve.tensor_tensor(flat["pos"], flat["t1"], ps_pre[:, 0:TT * E], ALU.add))
                    for k in range(TOPK):
                        own(dve.scalar_tensor_tensor(flat["t0"], flat["rank"], float(k), flat["pos"], ALU.is_equal,
                                                     ALU.mult))
                        do(dve.scalar_tensor_tensor(flat["t1"], flat["rank"], float(k), flat["Wt"], ALU.is_equal,
                                                    ALU.mult))
                        own(dve.tensor_reduce(rt1["m"][:], S["t0"], AX.X, ALU.add))
                        do(dve.tensor_reduce(wkk[:, :, k], S["t1"], AX.X, ALU.add))
                        do(dve.tensor_copy(posk[:, :, k], rt1["m"][:]))
                    own(dve.tensor_copy(endm[:, WBUF:], row["end"][:]))
                    do(dve.tensor_tensor(ended[:],
                                         row["end"][:].rearrange("p (o e) -> p o e", o=1).to_broadcast([P, NBLK, E]),
                                         blk[:].rearrange("p (n o) -> p n o", o=1).to_broadcast([P, NBLK, E]),
                                         ALU.is_le))
                    do(dve.tensor_reduce(ej[:], ended[:], AX.X, ALU.add))
                    do(dve.tensor_scalar(eji[:], ej[:], float(E - 1), None, ALU.min))
                    assert WBUF == 3 and all(e // 3 == e * 11 >> 5 for e in range(E))
                    do(dve.tensor_scalar(third[:], eji[:], 11.0, None, ALU.mult))
                    do(dve.tensor_scalar(third[:], third[:], 5, None, ALU.arith_shift_right))
                    own(dve.scalar_tensor_tensor(slot[:], third[:], -3.0, eji[:], ALU.mult, ALU.add))
                    dve.tensor_scalar(wload[:], eji[:], 64.0, 64.0, ALU.mult, ALU.add).then_inc(m_pos, 1)

                    with dve.Fori(NB // 2, NB) as b:
                        for j, (_, n) in enumerate(SJ):
                            p, m = j % 2, b * (NSJ // 2) + j // 2
                            dve.wait_ge(s_sl[p], ZERO + m + NSJ // 2 * (NB // 2) + 1)
                            dve.wait_ge(s_gu[p], ZERO + m + 1)
                            dve.tensor_tensor(hsh[0:n, j, :], ssl[p][0:n, :], ps_u[p][0:n, :], ALU.mult
                                              ).then_inc(s_h[p], 1)
                        add_shared(b)
                    g["own_after_router"] = own.n

        IJ = [(0, P), (P, P), (2 * P, I - 2 * P)]
        GW, DW = NC * I, len(IJ) * C
        UN = 4
        with ExitStack() as st:
            g["wkv_buffers"](st, "b")
            wg = sb("wg", [P, WBUF * GW], stack=st)
            wu = sb("wu", [P, WBUF * GW], stack=st)
            wd = sb("wd", [P, WBUF * DW], stack=st)
            xg = [sb(f"xg{s}", [P, C], stack=st) for s in range(2)]
            xgT = [sb(f"xgT{s}", [P, NC, P], stack=st) for s in range(2)]
            sl = [sb(f"bsl{s}", [P, I], stack=st) for s in range(2)]
            h = [sb(f"bh{s}", [P, I], stack=st) for s in range(2)]
            hT = [sb(f"hT{s}", [P, len(IJ), P], stack=st) for s in range(2)]
            ys = [sb(f"ys{s}", [P, C], stack=st) for s in range(2)]
            ps_x, ps_g, ps_u, ps_h, ps_y = psum[0:2], psum[2:4], psum[4:6], psum[6], psum[7]
            WITH = LATER // 2

            def wkv_at(i, s):
                return (FIRST + NB * BESIDE) // 2 + i, FIRST + NB * BESIDE + i * 2 + s
            with nc.Block() as block:
                @block.sync
                def _(sp):
                    def load(n, m, p):
                        sp.wait_ge(b_tx[p], ZERO + m)
                        sp.dma_start(xg[p][:], Xe[bass.ds(n * P, P)]).then_inc(b_x[p], 16)

                    def store(n, p):
                        sp.wait_ge(b_ye, ZERO + n + 1)
                        sp.dma_start(Ye[bass.ds(n * P, P)], ys[p][:]).then_inc(b_st[p], 16)
                    load(0, 0, 0)
                    load(1, 0, 1)

                    def body(i, base):
                        for q in range(UN):
                            load(i * UN + q + 2, i * (UN // 2) + q // 2 + 1, q % 2)
                            store(i * UN + q, q % 2)
                            if q >= 2:
                                m, lk = wkv_at(i, q - 2)
                                g["wkv_store"](sp, m, q - 2, lk)
                                if base:
                                    g["wkv_load"](sp, m + 1, q - 2, i * 2 + q + FIRST + NB * BESIDE - base)
                    for j in range(2):
                        g["wkv_load"](sp, wkv_at(0, j)[0], j, wkv_at(0, j)[1] % NK)
                    turn = (3 * NK - FIRST - NB * BESIDE) // 2 - 1
                    for start, stop, base in ((0, turn, 2 * NK), (turn, WITH - 1, 3 * NK)):
                        with sp.Fori(start, stop) as i:
                            body(i, base)
                    body(WITH - 1, None)
                    with sp.Fori(WITH, NBLK // UN - 1) as i:
                        for q in range(UN):
                            load(i * UN + q + 2, i * (UN // 2) + q // 2 + 1, q % 2)
                            store(i * UN + q, q % 2)
                    for q in range(UN):
                        n = NBLK - UN + q
                        if q < 2:
                            load(n + 2, n // 2 + 1, q % 2)
                        store(n, q % 2)
                    for p in range(2):
                        sp.wait_ge(b_st[p], ZERO + 16 * NBLK // 2)
                        sp.wait_ge(g["wk_store"][p], ZERO + 16 * 2 * NK)

                @block.gpsimd
                def _(pool):
                    def load(e, s, first=False):
                        if not first:
                            done = pool.value_load(endm[0:1, bass.ds(e, 1)], min_val=0, max_val=NBLK)
                            pool.wait_ge(b_y, ZERO + done)
                            pool.wait_ge(b_w, e * 64)
                        pool.dma_start(wg[:, s * GW:(s + 1) * GW].rearrange("p (a c n) -> p a c n", a=1, c=NC),
                                       io["WgT"][bass.ds(e, 1)].rearrange("a (c p) n -> p a c n", p=P)
                                       ).then_inc(b_w, 16)
                        pool.dma_start(wu[:, s * GW:(s + 1) * GW].rearrange("p (a c n) -> p a c n", a=1, c=NC),
                                       io["WuT"][bass.ds(e, 1)].rearrange("a (c p) n -> p a c n", p=P)
                                       ).then_inc(b_w, 16)
                        pool.dma_start(wd[:, s * DW:s * DW + 2 * C].rearrange("p (a c n) -> p a c n", a=1, c=2),
                                       io["WdT"][bass.ds(e, 1), 0:2 * P].rearrange("a (c p) n -> p a c n", p=P)
                                       ).then_inc(b_w, 16)
                        pool.dma_start(wd[0:I - 2 * P, s * DW + 2 * C:(s + 1) * DW],
                                       io["WdT"][bass.ds(e, 1), 2 * P:I].rearrange("a p n -> p (a n)")
                                       ).then_inc(b_w, 16)
                    load(0, 0, first=True)
                    assert E % WBUF == 1
                    with pool.Fori(0, E // WBUF) as i:
                        for s in range(1, WBUF + 1):
                            load(i * WBUF + s, s % WBUF)

                @block.tensor
                def _(pe):
                    def turn_x(n, m, p):
                        pe.wait_ge(b_x[p], ZERO + m * 16 + 16)
                        pe.wait_ge(b_xt[p], ZERO + m)
                        for c in range(NC):
                            mm = pe.transpose(ps_x[p][:, c * P:c * P + P], xg[p][:, c * P:c * P + P], ident[:])
                        mm.then_inc(b_tx[p], 1)

                    def gate(n, m, p, par):
                        pe.wait_ge(b_xt[p], ZERO + m + 1)
                        pe.wait_ge(b_h[p], ZERO + m)
                        for c in range(NC):
                            mm = pe.matmul(ps_g[p][:, 0:I], xgT[p][:, c, :], wg[:, bass.ds(par * GW + c * I, I)],
                                           start=c == 0, stop=c == NC - 1)
                        mm.then_inc(b_gate[p], 1)

                    def up(n, m, p, par):
                        for c in range(NC):
                            mm = pe.matmul(ps_u[p][:, 0:I], xgT[p][:, c, :], wu[:, bass.ds(par * GW + c * I, I)],
                                           start=c == 0, stop=c == NC - 1)
                        mm.then_inc(b_gu[p], 1)

                    def turn_h(n, m, p):
                        pe.wait_ge(b_h[p], ZERO + m + 1)
                        pe.wait_ge(b_hte, ZERO + n)
                        for j, (at, w) in enumerate(IJ):
                            mm = pe.transpose(ps_h[0:w, j * P:j * P + P], h[p][:, at:at + w], ident[:])
                        mm.then_inc(b_ht, 1)

                    def down(n, m, p, par):
                        pe.wait_ge(b_hte, ZERO + n + 1)
                        pe.wait_ge(b_ye, ZERO + n)
                        for j, (at, w) in enumerate(IJ):
                            mm = pe.matmul(ps_y[:], hT[p][0:w, j, :], wd[0:w, bass.ds(par * DW + j * C, C)],
                                           start=j == 0, stop=j == len(IJ) - 1)
                        mm.then_inc(b_y, 1)

                    def slot_of(n):
                        return pe.value_load(slot[0:1, bass.ds(n, 1)], min_val=0, max_val=WBUF - 1)

                    def body(i, first=False, last=False):
                        par = None if first else slot_of(i * UN - 1)
                        for q in range(UN):
                            n, m, p = i * UN + q, i * 2 + q // 2, q % 2
                            before = (n - 1, m - 1 + p, 1 - p, par)
                            need = pe.value_load(wload[0:1, bass.ds(n, 1)], min_val=0, max_val=64 * E)
                            par = slot_of(n)
                            pe.wait_ge(b_w, need)
                            gate(n, m, p, par)
                            if q or not first:
                                turn_h(*before[:3])
                            up(n, m, p, par)
                            if q < UN - 1 or not last:
                                turn_x(n + 1, m + p, 1 - p)
                            if q or not first:
                                down(*before)
                    turn_x(0, 0, 0)
                    body(0, first=True)
                    with pe.Fori(1, NBLK // UN - 1) as i:
                        body(i)
                    body(NBLK // UN - 1, last=True)
                    turn_h(NBLK - 1, NBLK // 2 - 1, 1)
                    down(NBLK - 1, NBLK // 2 - 1, 1, slot_of(NBLK - 1))

                @block.scalar
                def _(act):
                    def evict_x(n, m, p):
                        act.wait_ge(b_tx[p], ZERO + m + 1)
                        act.activation(xgT[p][:].rearrange("p c t -> p (c t)"), ps_x[p][:], ACT.Copy
                                       ).then_inc(b_xt[p], 1)

                    def evict_y(n, m, p):
                        act.wait_ge(b_y, ZERO + n + 1)
                        act.wait_ge(b_st[p], ZERO + m * 16)
                        act.activation(ys[p][:], ps_y[:], ACT.Copy).then_inc(b_ye, 1)

                    def body(i, tiles, first=False, last=False):
                        for q in range(UN):
                            n, m, p = i * UN + q, i * 2 + q // 2, q % 2
                            act.wait_ge(b_gate[p], ZERO + m + 1)
                            act.activation(sl[p][:], ps_g[p][:, 0:I], ACT.Silu).then_inc(b_sl[p], 1)
                            if q < UN - 1 or not last:
                                evict_x(n + 1, m + p, 1 - p)
                            if tiles and q % 2 == 0:
                                g["wkv_scalar"](act, wkv_at(i, q // 2)[0], q // 2)
                            if q or not first:
                                evict_y(n - 1, m - 1 + p, 1 - p)
                    evict_x(0, 0, 0)
                    body(0, True, first=True)
                    with act.Fori(1, WITH) as i:
                        body(i, True)
                    with act.Fori(WITH, NBLK // UN - 1) as i:
                        body(i, False)
                    body(NBLK // UN - 1, False, last=True)
                    evict_y(NBLK - 1, NBLK // 2 - 1, 1)

                @block.vector
                def _(dve):
                    own = Steps(dve, g["wk_own"])
                    own.n = g["own_after_router"]

                    def evict_h(n, m, p):
                        dve.wait_ge(b_ht, ZERO + n + 1)
                        own(dve.tensor_copy(hT[p][:, 0:2, :].rearrange("p c t -> p (c t)"), ps_h[:, 0:2 * P]))
                        w = IJ[2][1]
                        own.sync()
                        dve.tensor_copy(hT[p][0:w, 2, :], ps_h[0:w, 2 * P:3 * P]).then_inc(b_hte, 1)

                    def body(i, tiles, first=False):
                        for q in range(UN):
                            n, m, p = i * UN + q, i * 2 + q // 2, q % 2
                            if tiles and not p:
                                tile = g["wkv_vector"](dve, wkv_at(i, q // 2)[0], q // 2, wkv_at(i, q // 2)[1],
                                                       own, euv_here=True)
                            if q or not first:
                                evict_h(n - 1, m - 1 + p, 1 - p)
                            if tiles:
                                for _ in range(3 if p else 2):
                                    next(tile)
                            dve.wait_ge(b_sl[p], ZERO + m + 1)
                            dve.wait_ge(b_gu[p], ZERO + m + 1)
                            dve.tensor_tensor(h[p][:], sl[p][:], ps_u[p][:, 0:I], ALU.mult).then_inc(b_h[p], 1)
                            if tiles:
                                for _ in range(5):
                                    next(tile)
                    body(0, True, first=True)
                    for start, stop, tiles in ((1, WITH, True), (WITH, NBLK // UN - 1, False)):
                        with dve.Fori(start, stop) as i:
                            own.enter(i - start, UN + (2 * (g["WKV_OWN"] + 1) if tiles else 0))
                            body(i, tiles)
                            own.leave(stop - start)
                    body(NBLK // UN - 1, False)
                    evict_h(NBLK - 1, NBLK // 2 - 1, 1)


def state_space(nc, io, g):
    sb, sem, pair, X, ident, psum, G_dram = (g[k] for k in ("sb", "sem", "pair", "X", "ident", "psum", "G_dram"))
    BC_dram = nc.dram_tensor("BC_scratch", [2 * NS, T], F32, kind="Internal").ap()
    RING = 4
    TAPS = 4
    ON_PE = 2
    v_in, v_c, v_g, v_sig, v_r, v_u, v_x, v_dt, v_bc0, v_bcs0, v_bc, v_dl, v_abs, v_ln, v_du = (
        sem(n) for n in ("v_in", "v_c", "v_g", "v_sig", "v_r", "v_u", "v_x", "v_dt", "v_bc0", "v_bcs0", "v_bc",
                         "v_dl", "v_abs", "v_ln", "v_du"))
    v_ring = [sem(f"v_ring{j}") for j in range(RING)]
    v_da, v_h, v_hc, v_y, v_out, v_a = (sem(n) for n in ("v_da", "v_h", "v_hc", "v_y", "v_out", "v_a"))
    v_own = sem("v_own")
    v_cv, v_uu, v_dg = (sem(n) for n in ("v_cv", "v_uu", "v_dg"))
    v_bcs = g["plain_sem"]("v_bcs")
    d_dg, d_done = ([sem(f"{n}{j}") for j in range(NT)] for n in ("d_dg", "d_done"))
    d_y = [g["plain_sem"](f"d_y{j}") for j in range(NT)]
    d_x = sem("d_x")
    posk, wkk, Ye = g["posk"], g["wkk"], g["Ye"]
    g["start"]()
    with ExitStack() as st:
        gt = sb("v_gt", [P, NC, T], stack=st)
        sig = sb("v_sigx", [P, NC, T], stack=st)
        r = sb("v_r", [P, NC, TAPS - 1 + T], stack=st)
        u = sb("v_u", [P, NC, T], stack=st)
        du = sb("v_dut", [P, NC, T], stack=st)
        delta = sb("v_delta", [P, NC, T], stack=st)
        soft = sb("v_soft", [P, NC, T], stack=st)
        relu = sb("v_relu", [P, NC, T], stack=st)
        dtT = sb("v_dtT", [P, T], stack=st)
        bcT = sb("v_bcT", [2 * NS, T], stack=st)
        ring = [sb(f"v_bc{j}", [P, 2, T], stack=st) for j in range(RING)]
        dA, dBu, h, hC = ([sb(f"v_{n}{s}", [P, NC, T], stack=st) for s in range(2)] for n in ("dA", "dBu", "h", "hC"))
        xw = sb("v_xw", [P, NC, DTR + 2 * NS], stack=st)
        dw = sb("v_dw", [P, C], stack=st)
        taps = sb("v_taps", [P, NC, TAPS], stack=st)
        cvec = sb("v_cvec", [P, 3, NC], stack=st)
        diag = sb("v_diag", [P, ON_PE, TAPS, P], stack=st)
        ddiag = sb("v_ddiag", [P, NC, P], stack=st)
        alog = sb("v_alog", [P, NC, NS], stack=st)
        aexp = sb("v_aexp", [P, NC, NS], stack=st)
        A = sb("v_A", [P, NC, NS], stack=st)
        ps_y, ps_dt, ps_bc, ps_dl = psum[0:4], psum[4], psum[5], psum[6:8]
        yk = [[a[:, k, :] for k in range(TOPK)] for a in (*h, *dBu)]
        dg = [[dA[j % 2][:, j // 2, k * P:(k + 1) * P] for k in range(TOPK)] for j in range(NT)]
        with nc.Block() as block:
            @block.sync
            def _(sp):
                sp.dma_start(xw[:], io["xprojT"].rearrange("(c p) n -> p c n", p=P)).then_inc(v_in, 16)
                sp.dma_start(dw[:], io["dtprojT"]).then_inc(v_in, 16)
                sp.dma_start(taps[:], io["taps"]).then_inc(v_in, 16)
                sp.dma_start(cvec[:], io["cvec"]).then_inc(v_in, 16)
                sp.dma_start(alog[:], io["alog"]).then_inc(v_in, 16)

                def load_g(b, first=False):
                    if not first:
                        sp.wait_ge(v_r, ZERO + b)
                    sp.dma_start(gt[:], G_dram[bass.ds(b * NC + 2 * NK, NC)].rearrange("c p t -> p c t")
                                 ).then_inc(v_g, 16)

                def store_bc(b):
                    sp.wait_ge(v_bc, ZERO + b * (NS // RING) * 16)
                    for slot in v_ring:
                        sp.wait_ge(slot, ZERO + b * (NS // RING) * 16)
                    sp.dma_start(BC_dram, bcT[:]).then_inc(v_bcs, 16)

                def row(after, first=False, last=False):
                    if not last:
                        load_g(after)
                    b = after - 1
                    for n in range(NS):
                        if n >= RING or not first:
                            sp.wait_ge(v_hc, ZERO + b * NS + (n + 1 - RING))
                        if n == 0 and not first:
                            sp.wait_ge(v_bcs, b * 16)
                        sp.dma_start(ring[n % RING][:],
                                     BC_dram.rearrange("(a n) t -> n a t", a=2)[n:n + 1].to_broadcast([P, 2, T])
                                     ).then_inc(v_ring[n % RING], 16)
                    if not last:
                        store_bc(after)

                load_g(0, first=True)
                sp.wait_ge(v_bc0, ZERO + 1)
                sp.dma_start(BC_dram, bcT[:]).then_inc(v_bcs0, 16)
                sp.wait_ge(v_bcs0, ZERO + 16)
                row(1, first=True)
                with sp.Fori(2, NB) as after:
                    row(after)
                row(NB, last=True)

            @block.gpsimd
            def _(pool):
                pool.memset(r[:, :, 0:TAPS - 1], 0.0).then_inc(v_c, 1)
                for t in range(TT):
                    p = t % NT
                    if t >= NT:
                        pool.wait_ge(d_done[p], ZERO + t // NT)
                    for k in range(TOPK):
                        pool.indirect_dma_start(
                            out=yk[p][k], out_offset=None, in_=Ye,
                            in_offset=bass.IndirectOffsetOnAxis(ap=posk[:, t, k:k + 1], axis=0),
                            bounds_check=NBLK * P - 1, oob_is_err=False).then_inc(d_y[p], 16)

                def row(b, first=False):
                    for n in range(NS):
                        p = n % 2
                        pool.wait_ge(v_ring[n % RING], ZERO + (b * (NS // RING) + n // RING) * 16 + 16)
                        if n >= 2 or not first:
                            pool.wait_ge(v_y, ZERO + b * NS + n - 1)
                        pool.wait_ge(v_h, ZERO + b * NS + n + 1)
                        pool.tensor_tensor(hC[p][:], h[p][:], ring[n % RING][:, 1:2, :].to_broadcast([P, NC, T]),
                                           ALU.mult).then_inc(v_hc, 1)
                row(0, first=True)
                with pool.Fori(1, NB) as b:
                    row(b)

            @block.tensor
            def _(pe):
                def combine(t):
                    b, tt = t // NT, t % NT
                    pe.wait_ge(d_y[tt], 16 * TOPK * (b + 1))
                    pe.wait_ge(d_dg[tt], ZERO + TOPK * (b + 1))
                    if tt == 0 and b:
                        pe.wait_ge(d_x, ZERO + b * NC)
                    for c in range(NC):
                        for k in range(TOPK):
                            mm = pe.matmul(ps_y[c][:, tt * P:tt * P + P], yk[tt][k][:, c * P:c * P + P], dg[tt][k],
                                           start=k == 0, stop=k == TOPK - 1)
                    mm.then_inc(d_done[tt], 1)

                def convolve(b, c, first=False):
                    pe.wait_ge(v_r, ZERO + b + 1)
                    if not first:
                        pe.wait_ge(v_abs, ZERO + b * NC)
                    for j in range(TAPS):
                        mm = pe.matmul(ps_dl[c % 2][:], diag[:, c, j, :], r[:, c, j:j + T],
                                       start=j == 0, stop=j == TAPS - 1)
                    mm.then_inc(v_cv, 1)

                def project_bc(b, first=False):
                    pe.wait_ge(v_u, ZERO + b * NC + NC)
                    if not first:
                        pe.wait_ge(v_x, ZERO + b * 2)
                    for c in range(NC):
                        pe.matmul(ps_bc[0:2 * NS, :], xw[:, c, DTR:], u[:, c, :], start=c == 0, stop=c == NC - 1)

                def project_dt(b):
                    for c in range(NC):
                        mm = pe.matmul(ps_dt[:], xw[:, c, 0:DTR], u[:, c, :], start=c == 0, stop=c == NC - 1)
                    mm.then_inc(v_dt, 1)

                def delta_of(b, c):
                    pe.wait_ge(v_x, ZERO + b * 2 + 2)
                    if c >= 2:
                        pe.wait_ge(v_abs, ZERO + b * NC + (c - 1))
                    pe.matmul(ps_dl[c % 2][:], dw[:, c * P:c * P + P], dtT[:], start=True, stop=True
                              ).then_inc(v_dl, 1)

                def row(b, first=False, last=False):
                    if first:
                        pe.wait_ge(d_x, ZERO + NB * NC)
                    else:
                        pe.wait_ge(v_out, ZERO + b * NC)
                    for c in range(NC):
                        pe.matmul(ps_y[c][:], ddiag[:, c, :], u[:, c, :], start=True, stop=False,
                                  skip_group_check=True)
                    for n in range(NS):
                        pe.wait_ge(v_hc, ZERO + b * NS + n + 1)
                        for c in range(NC):
                            mm = pe.matmul(ps_y[c][:], ident[:], hC[n % 2][:, c, :], start=False, stop=n == NS - 1,
                                           skip_group_check=True)
                        mm.then_inc(v_y, 1)
                        if not last:
                            if n in (1, 3):
                                convolve(b + 1, n // 2)
                            elif n == 5:
                                project_bc(b + 1)
                            elif n == 6:
                                project_dt(b + 1)
                            elif n in (8, 9):
                                for c in range(2):
                                    delta_of(b + 1, (n - 8) * 2 + c)

                pe.wait_ge(v_in, ZERO + 80)
                pe.wait_ge(v_dg, ZERO + ON_PE * TAPS + NC)
                for t in range(TT):
                    combine(t)
                    if t in (6, 7):
                        convolve(0, t - 6, first=True)
                    elif t == 8:
                        project_bc(0, first=True)
                    elif t == 9:
                        project_dt(0)
                    elif t in (10, 11):
                        for c in range(2):
                            delta_of(0, (t - 10) * 2 + c)
                row(0, first=True)
                with pe.Fori(1, NB - 1) as b:
                    row(b)
                row(NB - 1, last=True)

            @block.scalar
            def _(act):
                soft_flat = soft[:].rearrange("p c t -> p (c t)")

                def sigmoid(b):
                    act.activation(sig[:].rearrange("p c t -> p (c t)"), X[:, bass.ds(b * NC * T, NC * T)], ACT.Sigmoid
                                   ).then_inc(v_sig, 1)

                def convolved(b, c, first=False):
                    act.wait_ge(v_cv, ZERO + b * ON_PE + c + 1)
                    if c == 0 and not first:
                        act.wait_ge(v_uu, ZERO + b)
                    act.activation(u[:, c, :], ps_dl[c % 2][:], ACT.Identity, bias=cvec[:, 0, c:c + 1]
                                   ).then_inc(v_u, 1)

                def evict(b, first=False):
                    act.wait_ge(v_dt, ZERO + b + 1)
                    ins = act.activation(bcT[:], ps_bc[0:2 * NS, :], ACT.Copy)
                    if first:
                        ins.then_inc(v_bc0, 1)
                    else:
                        ins.then_inc(v_bc, NS // RING * 16)
                    act.activation(dtT[:], ps_dt[:], ACT.Copy).then_inc(v_x, 2)

                def absolute(b, c):
                    act.wait_ge(v_dl, ZERO + b * NC + c + 1)
                    act.activation(relu[:, c, :], ps_dl[c % 2][:], ACT.Relu, bias=cvec[:, 1, c:c + 1])
                    act.activation(soft[:, c, :], ps_dl[c % 2][:], ACT.Abs, bias=cvec[:, 1, c:c + 1]
                                   ).then_inc(v_abs, 1)

                def softplus(b):
                    act.wait_ge(v_abs, ZERO + b * NC + NC)
                    act.activation(soft_flat, soft_flat, ACT.Exp, scale=-1.0).then_inc(v_ln, 1)
                    act.wait_ge(v_ln, ZERO + b * 2 + 1)
                    act.activation(soft_flat, soft_flat, ACT.Ln, bias=1.0).then_inc(v_ln, 1)

                def row(b, first=False, last=False):
                    act.wait_ge(v_du, ZERO + b + 1)
                    for n in range(NS):
                        if n >= 2 or not first:
                            act.wait_ge(v_h, ZERO + b * NS + n - 1)
                        for c in range(NC):
                            ins = act.activation(dA[n % 2][:, c, :], delta[:, c, :], ACT.Exp, scale=A[:, c, n:n + 1])
                        ins.then_inc(v_da, 1)
                        if not last:
                            if n == 0:
                                sigmoid(b + 1)
                            elif n in (5, 6):
                                convolved(b + 1, n - 5)
                            elif n == 9:
                                evict(b + 1)
                            elif n in (11, 12):
                                for c in range(2):
                                    absolute(b + 1, (n - 11) * 2 + c)
                            elif n == 13:
                                softplus(b + 1)

                act.wait_ge(d_x, ZERO + NC)
                sigmoid(0)
                act.wait_ge(v_in, ZERO + 80)
                act.activation(aexp[:], alog[:], ACT.Exp).then_inc(v_a, 1)
                act.wait_ge(v_a, ZERO + 1)
                act.activation(A[:], aexp[:], ACT.Copy, scale=-1.0).then_inc(v_a, 1)
                act.wait_ge(v_a, ZERO + 2)
                for c in range(ON_PE):
                    convolved(0, c, first=True)
                evict(0, first=True)
                for c in range(NC):
                    absolute(0, c)
                softplus(0)
                row(0, first=True)
                with act.Fori(1, NB - 1) as b:
                    row(b)
                row(NB - 1, last=True)

            @block.vector
            def _(dve):
                own = Steps(dve, v_own)

                def gated(b):
                    dve.wait_ge(v_g, ZERO + b * 16 + 16)
                    dve.wait_ge(v_sig, ZERO + b + 1)
                    dve.tensor_tensor(r[:, :, TAPS - 1:], sig[:], gt[:], ALU.mult).then_inc(v_r, 1)

                def tap(b, j, first=False):
                    if j == 0:
                        dve.wait_ge(v_r, ZERO + b + 1)
                        if not first:
                            dve.wait_ge(v_y, ZERO + (b - 1) * NS + 1)
                    own.sync()
                    for c in range(ON_PE, NC):
                        w, src = taps[:, c, j:j + 1], r[:, c, j:j + T]
                        if j == 0:
                            ins = dve.tensor_scalar(u[:, c, :], src, w, cvec[:, 0, c:c + 1], ALU.mult, ALU.add)
                        else:
                            ins = dve.scalar_tensor_tensor(u[:, c, :], src, w, u[:, c, :], ALU.mult, ALU.add)
                        if j < TAPS - 1:
                            own(ins)
                        else:
                            ins.then_inc(v_u, 1)

                def row_of(b, c):
                    return X[:, bass.ds((b * NC + c) * T, T)]

                def take(b):
                    dve.wait_ge(v_y, ZERO + b * NS + NS)
                    for c in range(NC):
                        dve.tensor_tensor(row_of(b, c), row_of(b, c), ps_y[c][:], ALU.add).then_inc(v_out, 1)

                def row(b, first=False, last=False):
                    if not first:
                        dve.wait_ge(v_da, ZERO + b * NS)
                    dve.wait_ge(v_u, ZERO + b * NC + NC)
                    dve.wait_ge(v_ln, ZERO + b * 2 + 2)
                    dve.tensor_tensor(delta[:], relu[:], soft[:], ALU.add).then_inc(v_du, 1)
                    dve.wait_ge(v_du, ZERO + b + 1)
                    own.sync()
                    dve.tensor_tensor(du[:], delta[:], u[:], ALU.mult).then_inc(v_uu, 1)
                    dve.wait_ge(v_uu, ZERO + b + 1)
                    for n in range(NS):
                        p = n % 2
                        own.sync()
                        dve.wait_ge(v_ring[n % RING], ZERO + (b * (NS // RING) + n // RING) * 16 + 16)
                        own(dve.tensor_tensor(dBu[p][:], du[:], ring[n % RING][:, 0:1, :].to_broadcast([P, NC, T]),
                                              ALU.mult))
                        own.sync()
                        dve.wait_ge(v_da, ZERO + b * NS + n + 1)
                        if n >= 2 or not first:
                            dve.wait_ge(v_hc, ZERO + b * NS + n - 1)
                        for c in range(NC):
                            ins = dve.tensor_tensor_scan(h[p][:, c, :], dA[p][:, c, :], dBu[p][:, c, :], 0.0,
                                                         ALU.mult, ALU.add)
                            if c < NC - 1:
                                own(ins)
                        ins.then_inc(v_h, 1)
                        if n == 1 and not first:
                            take(b - 1)
                        if not last:
                            if n == 1:
                                gated(b + 1)
                            elif 2 <= n < 2 + TAPS:
                                tap(b + 1, n - 2)

                dve.wait_ge(v_in, ZERO + 80)
                dve.wait_ge(v_c, ZERO + 1)
                for c in range(ON_PE):
                    for j in range(TAPS):
                        dve.tensor_scalar(diag[:, c, j, :], ident[:], taps[:, c, j:j + 1], None, ALU.mult
                                          ).then_inc(v_dg, 1)
                for c in range(NC):
                    dve.tensor_scalar(ddiag[:, c, :], ident[:], cvec[:, 2, c:c + 1], None, ALU.mult).then_inc(v_dg, 1)

                def add(b):
                    for done in d_done:
                        dve.wait_ge(done, ZERO + b + 1)
                    for c in range(NC):
                        dve.tensor_tensor(row_of(b, c), row_of(b, c), ps_y[c][:], ALU.add).then_inc(d_x, 1)

                for t in range(TT):
                    p, b = t % NT, t // NT
                    if b:
                        dve.wait_ge(d_done[p], ZERO + b)
                    for k in range(TOPK):
                        dve.tensor_scalar(dg[p][k], ident[:], wkk[:, t, k:k + 1], None, ALU.mult).then_inc(d_dg[p], 1)
                    if t % NT == NT - 1 and b:
                        add(b - 1)
                    if t == 2 * NT - 1:
                        gated(0)
                        for j in range(TAPS):
                            tap(0, j, first=True)
                add(NB - 1)
                row(0, first=True)
                with dve.Fori(1, NB - 1) as b:
                    own.enter(b - 1, NS * NC + (TAPS - 1) * (NC - ON_PE))
                    row(b)
                    own.leave(NB - 2)
                row(NB - 1, last=True)
                own.sync()
                take(NB - 1)


def linear_attention(nc, io, g):
    sb, sem, pair, X, ident, psum, G_dram = (g[k] for k in ("sb", "sem", "pair", "X", "ident", "psum", "G_dram"))
    L = NB
    DK = C // 2
    HK, HV = DK // HEADS, C // HEADS
    f_in, f_g, f_sig, f_r, f_cv, f_xs, f_own, f_o, f_std, f_sc, f_d, f_st, f_var, f_out = (
        sem(n) for n in ("f_in", "f_g", "f_sig", "f_r", "f_cv", "f_xs", "f_own", "f_o", "f_std", "f_sc", "f_d",
                         "f_st", "f_var", "f_out"))
    f_p, f_pf = ([sem(f"{n}{j}") for j in range(4)] for n in ("f_p", "f_pf"))
    f_wt = [sem(f"f_wt{j}") for j in range(4)]
    f_t, f_te, f_w = (pair(n) for n in ("f_t", "f_te", "f_w"))
    g["start"]()
    with ExitStack() as st:
        wqk, wv, wg, wo = (sb(f"f_w{n}", [P, NC, C], stack=st) for n in ("qk", "v", "g", "o"))
        gt = sb("f_gt", [P, NK, P], stack=st)
        r = sb("f_rt", [P, NK, P], stack=st)
        cv = sb("f_conv", [P, NK, P], stack=st)
        xs = sb("f_xst", [P, NK, P], stack=st)
        qk = [sb(f"f_qk{j}", [P, L, 2 * DK], stack=st) for j in range(2)]
        v = [sb(f"f_v{j}", [P, L, C], stack=st) for j in range(2)]
        gate = [sb(f"f_gate{j}", [P, L, C], stack=st) for j in range(2)]
        ra = sb("f_ra", [P, L, 2 * HEADS, HK // 2], stack=st)
        rb = sb("f_rb", [P, L, 2 * HEADS, HK // 2], stack=st)
        rot = sb("f_rot", [P, L, 2 * HEADS, HK], stack=st)
        vw = sb("f_vw", [P, L, C], stack=st)
        o = sb("f_ot", [P, L, C], stack=st)
        oT = sb("f_oT", [P, NC, L * P], stack=st)
        xo = sb("f_xo", [P, NK, P], stack=st)
        cs = sb("f_cs", [P, 2, L, HK // 2], stack=st)
        taps = sb("f_taps", [P, NC, 2], stack=st)
        rr = sb("f_rr", [P, 2, C], stack=st)
        rd = sb("f_rd", [P, C], stack=st)
        eps = sb("f_eps", [P, 1], stack=st)
        tiny = {n: sb(f"f_{n}", [P, L * HEADS], stack=st) for n in
                ("dd", "ad", "sel", "sc_", "cnt", "rc", "fl", "mu", "var_", "std_", "rs")}
        same = sb("f_same", [P, L, L, HEADS], stack=st)
        dots = sb("f_dots", [P, L, L, HEADS], stack=st)
        ps_p, ps_t, ps_w = psum[0:4], psum[4:6], psum[6:8]
        JT = T // P
        with nc.Block() as block:
            @block.sync
            def _(sp):
                sp.dma_start(taps[:], io["ftaps"]).then_inc(f_in, 16)
                sp.dma_start(cs[:].rearrange("p a l d -> p (a l d)"), io["cs"].to_broadcast([P, 2 * L * HK // 2])
                             ).then_inc(f_in, 16)
                sp.dma_start(rr[:].rearrange("p a c -> p (a c)"), io["fr"].to_broadcast([P, 2 * C])
                             ).then_inc(f_in, 16)

                def load(t):
                    if t:
                        sp.wait_ge(f_r, ZERO + t)
                    sp.dma_start(gt[:], G_dram[3 * NK:4 * NK].rearrange("k p t -> p k t")[:, :, t * P:t * P + P]
                                 ).then_inc(f_g, 16)
                load(0)
                for i, (w, n) in enumerate(((wqk, "Wqk"), (wv, "fWv"), (wg, "fWg"), (wo, "fWout"))):
                    sp.dma_start(w[:], io[n].rearrange("(c p) n -> p c n", p=P)).then_inc(f_wt[i], 16)
                load(1)
                for t in range(JT):
                    if t + 2 < JT:
                        load(t + 2)
                    sp.wait_ge(f_out, ZERO + t * NC + NC)
                    sp.dma_start(io["out"].rearrange("k p t -> p k t")[:, :, t * P:t * P + P], xo[:]
                                 ).then_inc(f_st, 16)
                sp.wait_ge(f_st, ZERO + 16 * JT)

            @block.tensor
            def _(pe):
                def project(t):
                    pe.wait_ge(f_xs, ZERO + t + 1)
                    for l in range(L):
                        for j, w in enumerate((wqk, wv, wg)):
                            use = l * 3 + j
                            if not (t or l):
                                pe.wait_ge(f_wt[j], ZERO + 16)
                            if t or use >= 4:
                                pe.wait_ge(f_pf[use % 4], ZERO + t * 3 + use // 4)
                            for c in range(NC):
                                mm = pe.matmul(ps_p[use % 4][:], xs[:, l * NC + c, :], w[:, c, :],
                                               start=c == 0, stop=c == NC - 1)
                            mm.then_inc(f_p[use % 4], 1)

                def output(t):
                    pe.wait_ge(f_o, ZERO + t + 1)
                    for l in range(L):
                        if t or l >= 2:
                            pe.wait_ge(f_te[l % 2], ZERO + t * 2 + l // 2)
                        for c in range(NC):
                            mm = pe.transpose(ps_t[l % 2][:, c * P:c * P + P], o[:, l, c * P:c * P + P], ident[:])
                        mm.then_inc(f_t[l % 2], 1)
                    for p in range(2):
                        pe.wait_ge(f_te[p], ZERO + t * 2 + 2)
                    for m in range(NC):
                        if t or m >= 2:
                            pe.wait_ge(f_out, ZERO + t * NC + m - 1)
                        for c in range(NC):
                            mm = pe.matmul(ps_w[m % 2][:], wo[:, c, m * P:m * P + P], oT[:, c, :],
                                           start=c == 0, stop=c == NC - 1)
                        mm.then_inc(f_w[m % 2], 1)

                project(0)
                pe.wait_ge(f_wt[3], ZERO + 16)
                for t in range(JT):
                    if t + 1 < JT:
                        project(t + 1)
                    output(t)

            @block.scalar
            def _(act):
                def sigmoid(t):
                    if t:
                        act.wait_ge(f_cv, ZERO + t * 2 * NC)
                    act.activation(r[:], X[:].rearrange("p (k t) -> p k t", k=NK)[:, :, t * P:t * P + P], ACT.Sigmoid
                                   ).then_inc(f_sig, 1)

                def silu(t):
                    act.wait_ge(f_cv, ZERO + (t + 1) * 2 * NC)
                    act.activation(xs[:], cv[:], ACT.Silu).then_inc(f_xs, 1)

                def evict(t, use):
                    l, j = use // 3, use % 3
                    act.wait_ge(f_p[use % 4], ZERO + t * 3 + use // 4 + 1)
                    if use == 0 and t >= 2:
                        act.wait_ge(f_o, ZERO + t - 1)
                    ps = ps_p[use % 4]
                    if j == 0:
                        act.activation(qk[t % 2][:, l, 0:DK], ps[:, 0:DK], ACT.Silu)
                        ins = act.activation(qk[t % 2][:, l, DK:], ps[:, DK:], ACT.Copy)
                    elif j == 1:
                        ins = act.activation(v[t % 2][:, l, :], ps[:], ACT.Copy)
                    else:
                        ins = act.activation(gate[t % 2][:, l, :], ps[:], ACT.Silu)
                    ins.then_inc(f_pf[use % 4], 1)

                sigmoid(0)
                silu(0)
                sigmoid(1)
                for use in range(3 * L):
                    evict(0, use)
                silu(1)
                for t in range(JT):
                    for use in range(3 * L):
                        if t + 1 < JT:
                            evict(t + 1, use)
                        if use == 3 and t + 2 < JT:
                            sigmoid(t + 2)
                        if use == 5:
                            act.wait_ge(f_d, ZERO + t * 2 + 1)
                            act.activation(tiny["sc_"][:], tiny["ad"][:], ACT.Sigmoid).then_inc(f_sc, 1)
                        if use == 8:
                            act.wait_ge(f_d, ZERO + t * 2 + 2)
                            act.activation(vw[:], o[:], ACT.Square).then_inc(f_sc, 1)
                            act.wait_ge(f_var, ZERO + t + 1)
                            act.activation(tiny["std_"][:], tiny["var_"][:], ACT.Sqrt, bias=eps[:], scale=1.0 / HV
                                           ).then_inc(f_std, 1)
                    if t:
                        for p in range(2):
                            act.wait_ge(f_w[p], ZERO + t * 2)
                    for l in range(L):
                        act.wait_ge(f_t[l % 2], ZERO + t * 2 + l // 2 + 1)
                        act.activation(oT[:, :, l * P:l * P + P], ps_t[l % 2][:].rearrange("p (c t) -> p c t", c=NC),
                                       ACT.Copy).then_inc(f_te[l % 2], 1)
                    if t + 2 < JT:
                        silu(t + 2)

            @block.vector
            def _(dve):
                own = Steps(dve, f_own)
                dve.wait_ge(f_in, ZERO + 48)
                own(dve.memset(eps[:], EPS))
                own(dve.tensor_tensor(rd[:], rr[:, 1, :], rr[:, 0, :], ALU.subtract))
                own.sync()
                K = {k: x[:] for k, x in tiny.items()}

                def do(ins):
                    own(ins)
                    own.sync()

                def convolve(t):
                    dve.wait_ge(f_g, ZERO + t * 16 + 16)
                    dve.wait_ge(f_sig, ZERO + t + 1)
                    dve.tensor_tensor(r[:], r[:], gt[:], ALU.mult).then_inc(f_r, 1)
                    if t:
                        dve.wait_ge(f_xs, ZERO + t)
                    dve.wait_ge(f_r, ZERO + t + 1)
                    for c in range(NC):
                        dve.tensor_scalar(cv[:, c::NC, :], r[:, c::NC, :], taps[:, c, 1:2], None, ALU.mult
                                          ).then_inc(f_cv, 1)
                    dve.wait_ge(f_cv, ZERO + t * 2 * NC + NC)
                    for c in range(NC):
                        dve.scalar_tensor_tensor(cv[:, NC + c::NC, :], r[:, c:NK - NC:NC, :], taps[:, c, 0:1],
                                                 cv[:, NC + c::NC, :], ALU.mult, ALU.add).then_inc(f_cv, 1)

                def add(t, m):
                    dve.wait_ge(f_w[m % 2], ZERO + t * 2 + m // 2 + 1)
                    if m == 0 and t:
                        dve.wait_ge(f_st, ZERO + t * 16)
                    dve.tensor_tensor(xo[:, m::NC, :],
                                      X[:].rearrange("p (k t) -> p k t", k=NK)[:, m::NC, t * P:t * P + P],
                                      ps_w[m % 2][:].rearrange("p (l t) -> p l t", l=L), ALU.add).then_inc(f_out, 1)

                def attend(t):
                    V, QK = v[t % 2], qk[t % 2]
                    for j in range(4):
                        dve.wait_ge(f_pf[j], ZERO + t * 3 + 3)
                    do(dve.tensor_tensor(vw[:], V[:],
                                         rd[:].rearrange("p (o c) -> p o c", o=1).to_broadcast([P, L, C]), ALU.mult))
                    do(dve.tensor_reduce(K["dd"], vw[:].rearrange("p l (h d) -> p (l h) d", d=HV), AX.X, ALU.add))
                    own(dve.tensor_scalar(K["sel"], K["dd"], 0.0, None, ALU.is_gt))
                    dve.scalar_tensor_tensor(K["ad"], K["dd"], -1.0, K["dd"], ALU.mult, ALU.max).then_inc(f_d, 1)
                    if t:
                        add(t - 1, 1)
                    q4 = QK[:].rearrange("p l (h d) -> p l h d", d=HK)
                    x1, x2 = q4[:, :, :, 0:HK // 2], q4[:, :, :, HK // 2:]
                    cos, sin = (cs[:, a].rearrange("p l (o d) -> p l o d", o=1)
                                .to_broadcast([P, L, 2 * HEADS, HK // 2]) for a in range(2))
                    own(dve.tensor_tensor(ra[:], x1, cos, ALU.mult))
                    do(dve.tensor_tensor(rb[:], x2, sin, ALU.mult))
                    do(dve.tensor_tensor(rot[:, :, :, 0:HK // 2], ra[:], rb[:], ALU.subtract))
                    if t:
                        add(t - 1, 2)
                    own(dve.tensor_tensor(ra[:], x2, cos, ALU.mult))
                    do(dve.tensor_tensor(rb[:], x1, sin, ALU.mult))
                    do(dve.tensor_tensor(rot[:, :, :, HK // 2:], ra[:], rb[:], ALU.add))
                    if t:
                        add(t - 1, 3)
                    sel = K["sel"].rearrange("p (l h) -> p l h", l=L)
                    for l in range(L):
                        n = l + 1
                        ql = rot[:, l:l + 1, 0:HEADS, :].rearrange("p o h d -> p o (h d)").to_broadcast([P, n, DK])
                        km = rot[:, 0:n, HEADS:, :].rearrange("p m h d -> p m (h d)")
                        own(dve.tensor_tensor(same[:, l, 0:n, :], sel[:, 0:n, :],
                                              sel[:, l:l + 1, :].to_broadcast([P, n, HEADS]), ALU.is_equal))
                        do(dve.tensor_tensor(vw[:, 0:n, 0:DK], km, ql, ALU.mult))
                        own(dve.tensor_reduce(K["cnt"].rearrange("p (l h) -> p l h", l=L)[:, l, :],
                                              same[:, l, 0:n, :].rearrange("p m h -> p h m"), AX.X, ALU.add))
                        do(dve.tensor_reduce(dots[:, l, 0:n, :],
                                             vw[:, 0:n, 0:DK].rearrange("p m (h d) -> p m h d", d=HK),
                                             AX.X, ALU.add))
                        own(dve.tensor_tensor(dots[:, l, 0:n, :], dots[:, l, 0:n, :], same[:, l, 0:n, :], ALU.mult))
                    do(dve.reciprocal(K["rc"], K["cnt"]))
                    dve.wait_ge(f_sc, ZERO + t * 2 + 1)
                    do(dve.scalar_tensor_tensor(K["fl"], K["sc_"], float(HK) ** -0.5, K["rc"], ALU.mult, ALU.mult))
                    fl = K["fl"].rearrange("p (l h) -> p l h", l=L)
                    if t:
                        for p in range(2):
                            dve.wait_ge(f_t[p], ZERO + t * 2)
                    for l in range(L):
                        n = l + 1
                        do(dve.tensor_tensor(dots[:, l, 0:n, :], dots[:, l, 0:n, :],
                                             fl[:, l:l + 1, :].to_broadcast([P, n, HEADS]), ALU.mult))
                        do(dve.tensor_tensor(vw[:, 0:n, :].rearrange("p m (h d) -> p m h d", d=HV),
                                             V[:, 0:n, :].rearrange("p m (h d) -> p m h d", d=HV),
                                             dots[:, l, 0:n, :].rearrange("p m (h o) -> p m h o", o=1)
                                             .to_broadcast([P, n, HEADS, HV]), ALU.mult))
                        do(dve.tensor_reduce(o[:, l, :], vw[:, 0:n, :].rearrange("p m c -> p c m"), AX.X, ALU.add))
                    o3 = o[:].rearrange("p l (h d) -> p (l h) d", d=HV)

                    def wide(a):
                        return a.rearrange("p (n o) -> p n o", o=1).to_broadcast([P, L * HEADS, HV])
                    do(dve.tensor_reduce(K["mu"], o3, AX.X, ALU.add))
                    do(dve.tensor_scalar(K["mu"], K["mu"], 1.0 / HV, None, ALU.mult))
                    dve.tensor_tensor(o3, o3, wide(K["mu"]), ALU.subtract).then_inc(f_d, 1)
                    dve.wait_ge(f_sc, ZERO + t * 2 + 2)
                    dve.tensor_reduce(K["var_"], vw[:].rearrange("p l (h d) -> p (l h) d", d=HV), AX.X, ALU.add
                                      ).then_inc(f_var, 1)
                    dve.wait_ge(f_std, ZERO + t + 1)
                    do(dve.reciprocal(K["rs"], K["std_"]))
                    do(dve.tensor_tensor(o3, o3, wide(K["rs"]), ALU.mult))
                    dve.tensor_tensor(o[:], o[:], gate[t % 2][:], ALU.mult).then_inc(f_o, 1)

                convolve(0)
                convolve(1)
                for t in range(JT):
                    attend(t)
                    if t + 2 < JT:
                        convolve(t + 2)
                    add(t, 0)
                for m in range(1, NC):
                    add(JT - 1, m)


def rotary():
    import numpy as np

    hk = C // 2 // HEADS
    inv = (1.0 / 10000.0 ** (np.arange(0, hk, 2, dtype=np.float32) / hk)).astype(np.float32)
    a = np.arange(NB, dtype=np.float32)[:, None] * inv[None, :]
    return np.stack([np.cos(a), np.sin(a)]).astype(np.float32).reshape(1, -1)


def prepare(inputs):
    import numpy as np

    n = {k: np.asarray(v) for k, v in inputs.items()}

    def tiles(a):
        return np.ascontiguousarray(a.reshape(NB, T, NC, P).transpose(0, 2, 3, 1).reshape(NK, P, T))

    def columns(a):
        return np.ascontiguousarray(a.reshape(-1, P).T)

    names = ["L0_cond", "L0_cond2", "L1_cond", "L1_cond2"]
    return {
        "x": tiles(n["x"]),
        "f": tiles(n["fside_BxSxS_0"]),
        "condT": np.ascontiguousarray(n["cond_512"].T),
        "w": columns(np.stack([n[k + "_w"] for k in names])),
        "u": columns(np.stack([n[k + "_u"] for k in names])),
        "Wq": n["L0_attn_Wq"], "Wk": n["L0_attn_Wk"], "Wv": n["L0_attn_Wv"], "Wo": n["L0_attn_Wo"],
        "bo": columns(n["L0_attn_bo"]),
        "rw": np.ascontiguousarray(np.concatenate([n["L0_ffn_rg_w"].T, n["L0_ffn_ru_w"].T], 1)),
        "ebias": n["L0_ffn_extra_bias"].reshape(1, E), "escale": n["L0_ffn_extra_scale"].reshape(1, E),
        "SgT": np.ascontiguousarray(n["L0_ffn_Sg"].T), "SuT": np.ascontiguousarray(n["L0_ffn_Su"].T),
        "SdT": np.ascontiguousarray(n["L0_ffn_Sd"].T),
        "xprojT": np.ascontiguousarray(n["L1_attn_xproj_w"].T),
        "dtprojT": np.ascontiguousarray(n["L1_attn_dtproj_w"].T),
        "taps": np.ascontiguousarray(n["L1_attn_conv_w"].reshape(NC, P, 4).transpose(1, 0, 2)),
        "cvec": columns(np.stack([n["L1_attn_conv_b"], n["L1_attn_dtproj_b"], n["L1_attn_D_skip"]])
                        ).reshape(P, 3, NC),
        "alog": np.ascontiguousarray(n["L1_attn_A_log"].reshape(NC, P, NS).transpose(1, 0, 2)),
        "Wqk": np.ascontiguousarray(np.concatenate([n["L1_ffn_Wq"], n["L1_ffn_Wk"]], 1)),
        "fWv": n["L1_ffn_Wv"], "fWg": n["L1_ffn_Wg"], "fWout": n["L1_ffn_Wout"],
        "ftaps": np.ascontiguousarray(n["L1_ffn_conv_w"].reshape(NC, P, 2).transpose(1, 0, 2)),
        "fr": np.ascontiguousarray(n["L1_ffn_router_w"].reshape(C, 2).T).reshape(1, 2 * C),
        "cs": rotary(),
        "WgT": np.ascontiguousarray(n["L0_ffn_Wg"].transpose(0, 2, 1)),
        "WuT": np.ascontiguousarray(n["L0_ffn_Wu"].transpose(0, 2, 1)),
        "WdT": np.ascontiguousarray(n["L0_ffn_Wd"].transpose(0, 2, 1)),
    }


def kernel(**inputs):
    import numpy as np
    import concourse.bacc as bacc
    from concourse.bass_utils import run_bass_kernel_spmd as run

    nc = bacc.Bacc("TRN2", target_bir_lowering=False, num_devices=1)
    arrays = prepare(inputs)
    io = {k: nc.dram_tensor("in_" + k, a.shape, mybir.dt.from_np(a.dtype), kind="ExternalInput").ap()
          for k, a in arrays.items()}
    io["out"] = nc.dram_tensor("out", (NK, P, T), F32, kind="ExternalOutput").ap()
    build(nc, io)
    got = run(nc, [{"in_" + k: a for k, a in arrays.items()}], core_ids=[0]).results[0]["out"]
    return np.ascontiguousarray(got.reshape(NB, NC, P, T).transpose(0, 3, 1, 2).reshape(NB, T, C))
```
